# Optimizing a Trainium2 kernel written in Bass

```python
import numpy as np
import jax
import jax.numpy as jnp

def _softmax(x, axis=-1):
    return jax.nn.softmax(x, axis=axis)

def _gelu(x):
    return jax.nn.gelu(x, approximate=True)

def _silu(x):
    return jax.nn.silu(x)

def _sigmoid(x):
    return jax.nn.sigmoid(x)

def _layernorm(x, axis=-1, eps=1e-05):
    m = jnp.mean(x, axis=axis, keepdims=True)
    v = jnp.var(x, axis=axis, keepdims=True)
    return (x - m) / jnp.sqrt(v + eps)

def _scatter_add(tgt, idx, src, axis=0):
    return tgt.at[idx].add(src)

def _segment_sum(src, seg, n):
    return jax.ops.segment_sum(src, seg, n)
kernel_name = 'mk_xattn_ffn_d2_seqx_r4_22eaa5'

def setup_inputs(seed: int=0):
    np.random.seed(seed)
    _w = jnp.asarray

    def _rec_inputs():
        import jax
        import jax.numpy as jnp
        _rk = jax.random.key(seed)
        x = 0.0002417 + 0.9998 * jax.random.normal(jax.random.fold_in(_rk, 1), (4, 1024, 256), jnp.float32)
        _lenS = 1024 - jax.random.randint(jax.random.fold_in(_rk, 7), (4,), 0, max(1, 1024 // 4) + 1, jnp.int32)
        _lenS2 = 77 - jax.random.randint(jax.random.fold_in(_rk, 8), (4,), 0, max(1, 77 // 4) + 1, jnp.int32)
        _ctx_1024P = jax.random.normal(jax.random.fold_in(_rk, 11), (4, 16, 256), jnp.float32)
        _ctx_1024c = jax.random.dirichlet(jax.random.fold_in(_rk, 511), 0.3 * jnp.ones((16,), jnp.float32), (4, 77))
        _ctx_1024t = jnp.einsum('bsk,bkd->bsd', _ctx_1024c, _ctx_1024P)
        _ctx_1024t = _ctx_1024t * jax.lax.rsqrt(jnp.mean(jnp.square(_ctx_1024t)) + 1e-12) * 0.953939
        ctx_1024 = 7.22013e-05 + 1.00017 * (_ctx_1024t + 0.3 * jax.random.normal(jax.random.fold_in(_rk, 611), (4, 77, 256), jnp.float32))
        _validS = jnp.arange(1024)[None, :] < _lenS[:, None]
        _validS2 = jnp.arange(77)[None, :] < _lenS2[:, None]
        _causal = jnp.tril(jnp.ones((1024, 1024), dtype=bool))
        mask_1x1xSxS2_fk1 = jnp.where(jnp.broadcast_to(_validS2[0:1, None, None, :], (1, 1, 1024, 77)), 1.0, 0.0).astype(jnp.float32)
        mask_Bx1xSxS2_bk1 = jnp.broadcast_to(_validS2[:, None, None, :], (4, 1, 1024, 77))
        return (x, ctx_1024, mask_1x1xSxS2_fk1, mask_Bx1xSxS2_bk1)
    x, ctx_1024, mask_1x1xSxS2_fk1, mask_Bx1xSxS2_bk1 = _rec_inputs()

    def _L0_xattn_setup():
        import jax, jax.numpy as jnp
        import numpy as np
        D_MODEL = 256
        NUM_HEADS = 16
        DEPTH = D_MODEL // NUM_HEADS
        BATCH = 4
        SEQ = 512
        NEG_BIG = -1000000000.0

        def _split_heads(x, b, s):
            return x.reshape(b, s, NUM_HEADS, DEPTH).transpose(0, 2, 1, 3)
        key = jax.random.key(seed)
        ks = jax.random.split(key, 12)
        f = lambda k, shape, scale=1.0: jax.random.normal(k, shape, dtype=jnp.float32) * scale
        inv = 1.0 / np.sqrt(D_MODEL)
        mask = jnp.triu(jnp.ones((SEQ, SEQ), dtype=jnp.float32), k=1)[None, None, :, :]
        return {'v': f(ks[0], (BATCH, SEQ, D_MODEL)), 'k': f(ks[1], (BATCH, SEQ, D_MODEL)), 'q': f(ks[2], (BATCH, SEQ, D_MODEL)), 'mask': mask, 'wq_w': f(ks[3], (D_MODEL, D_MODEL), inv), 'wq_b': jnp.zeros((D_MODEL,), jnp.float32), 'wk_w': f(ks[4], (D_MODEL, D_MODEL), inv), 'wk_b': jnp.zeros((D_MODEL,), jnp.float32), 'wv_w': f(ks[5], (D_MODEL, D_MODEL), inv), 'wv_b': jnp.zeros((D_MODEL,), jnp.float32), 'wo_w': f(ks[6], (D_MODEL, D_MODEL), inv), 'wo_b': jnp.zeros((D_MODEL,), jnp.float32)}
    _L0_xattn_all = _L0_xattn_setup()
    _L0_xattn_in = {k: v for k, v in _L0_xattn_all.items() if k in ('wq_w', 'wq_b', 'wk_w', 'wk_b', 'wv_w', 'wv_b', 'wo_w', 'wo_b')}
    del _L0_xattn_all

    def _L0_ffn_setup():
        import jax, jax.numpy as jnp
        import numpy as np
        TOP_K = 2
        NUM_EXPERTS = 8
        key = jax.random.key(seed)
        ks = jax.random.split(key, 8)
        h, d, ds, E = (256, 128, 256, NUM_EXPERTS)
        s = 1.0 / np.sqrt(h)
        return {'x': jax.random.normal(ks[0], (2, 512, h), jnp.float32), 'router': jax.random.normal(ks[1], (h, E), jnp.float32) * s, 'experts_gate': jax.random.normal(ks[2], (E, h, d), jnp.float32) * s, 'experts_up': jax.random.normal(ks[3], (E, h, d), jnp.float32) * s, 'experts_down': jax.random.normal(ks[4], (E, d, h), jnp.float32) * (1.0 / np.sqrt(d)), 'shared_gate': jax.random.normal(ks[5], (h, ds), jnp.float32) * s, 'shared_up': jax.random.normal(ks[6], (h, ds), jnp.float32) * s, 'shared_down': jax.random.normal(ks[7], (ds, h), jnp.float32) * (1.0 / np.sqrt(ds))}
    _L0_ffn_all = _L0_ffn_setup()
    _L0_ffn_in = {k: v for k, v in _L0_ffn_all.items() if k in ('router', 'experts_gate', 'experts_up', 'experts_down', 'shared_gate', 'shared_up', 'shared_down')}
    del _L0_ffn_all

    def _L1_xattn_setup():
        import jax, jax.numpy as jnp
        import numpy as np
        D = 256
        H = 16
        DH = D // H
        B = 2
        S = 512

        def _split_heads(x):
            b, s, _ = x.shape
            return x.reshape(b, s, H, DH).transpose(0, 2, 1, 3)
        key = jax.random.key(seed)
        ks = jax.random.split(key, 12)
        scale = 1.0 / np.sqrt(D)
        inp = {'query': jax.random.normal(ks[0], (B, S, D), jnp.float32), 'key': jax.random.normal(ks[1], (B, S, D), jnp.float32), 'value': jax.random.normal(ks[2], (B, S, D), jnp.float32), 'mask': jax.random.randint(ks[3], (B, 1, S, S), 0, 2).astype(bool), 'Wq': jax.random.normal(ks[4], (D, D), jnp.float32) * scale, 'bq': jnp.zeros((D,), jnp.float32), 'Wk': jax.random.normal(ks[5], (D, D), jnp.float32) * scale, 'bk': jnp.zeros((D,), jnp.float32), 'Wv': jax.random.normal(ks[6], (D, D), jnp.float32) * scale, 'bv': jnp.zeros((D,), jnp.float32), 'Wo': jax.random.normal(ks[7], (D, D), jnp.float32) * scale, 'bo': jnp.zeros((D,), jnp.float32)}
        return inp
    _L1_xattn_all = _L1_xattn_setup()
    _L1_xattn_in = {k: v for k, v in _L1_xattn_all.items() if k in ('Wq', 'bq', 'Wk', 'bk', 'Wv', 'bv', 'Wo', 'bo')}
    del _L1_xattn_all

    def _L1_ffn_setup():
        import jax, jax.numpy as jnp
        import numpy as np
        LN_EPS = 1e-05

        def layernorm(x, g, b):
            mu = jnp.mean(x, axis=-1, keepdims=True)
            var = jnp.mean((x - mu) ** 2, axis=-1, keepdims=True)
            return (x - mu) * jax.lax.rsqrt(var + LN_EPS) * g + b

        def act_quant_fake(x):
            scale = 127.0 / jnp.clip(jnp.max(jnp.abs(x), axis=-1, keepdims=True), 1e-05)
            return jnp.clip(jnp.round(x * scale), -128.0, 127.0) / scale

        def weight_quant_fake(w):
            scale = 1.0 / jnp.clip(jnp.mean(jnp.abs(w)), 1e-05)
            return jnp.clip(jnp.round(w * scale), -1.0, 1.0) / scale

        def bitlinear(x, w, b):
            dqx = act_quant_fake(x)
            dqw = weight_quant_fake(w)
            return jnp.einsum('btd,hd->bth', dqx, dqw) + b
        key = jax.random.key(seed)
        ks = jax.random.split(key, 5)
        B, T, D, H = (8, 1024, 256, 1024)
        return {'x': jax.random.normal(ks[0], (B, T, D), dtype=jnp.float32), 'ln1_g': jnp.ones((D,), jnp.float32), 'ln1_b': jnp.zeros((D,), jnp.float32), 'w1': jax.random.normal(ks[1], (H, D), dtype=jnp.float32) * (1.0 / np.sqrt(D)), 'b1': jax.random.normal(ks[2], (H,), dtype=jnp.float32) * 0.02, 'ln2_g': jnp.ones((H,), jnp.float32), 'ln2_b': jnp.zeros((H,), jnp.float32), 'w2': jax.random.normal(ks[3], (D, H), dtype=jnp.float32) * (1.0 / np.sqrt(H)), 'b2': jax.random.normal(ks[4], (D,), jnp.float32) * 0.02}
    _L1_ffn_all = _L1_ffn_setup()
    _L1_ffn_in = {k: v for k, v in _L1_ffn_all.items() if k in ('ln1_g', 'ln1_b', 'w1', 'b1', 'ln2_g', 'ln2_b', 'w2', 'b2')}
    del _L1_ffn_all
    return {'x': x, 'ctx_1024': ctx_1024, 'mask_1x1xSxS2_fk1': mask_1x1xSxS2_fk1, 'mask_Bx1xSxS2_bk1': mask_Bx1xSxS2_bk1, 'L0_xattn_wq_w': _L0_xattn_in['wq_w'], 'L0_xattn_wq_b': _L0_xattn_in['wq_b'], 'L0_xattn_wk_w': _L0_xattn_in['wk_w'], 'L0_xattn_wk_b': _L0_xattn_in['wk_b'], 'L0_xattn_wv_w': _L0_xattn_in['wv_w'], 'L0_xattn_wv_b': _L0_xattn_in['wv_b'], 'L0_xattn_wo_w': _L0_xattn_in['wo_w'], 'L0_xattn_wo_b': _L0_xattn_in['wo_b'], 'L0_ffn_router': _L0_ffn_in['router'], 'L0_ffn_experts_gate': _L0_ffn_in['experts_gate'], 'L0_ffn_experts_up': _L0_ffn_in['experts_up'], 'L0_ffn_experts_down': _L0_ffn_in['experts_down'], 'L0_ffn_shared_gate': _L0_ffn_in['shared_gate'], 'L0_ffn_shared_up': _L0_ffn_in['shared_up'], 'L0_ffn_shared_down': _L0_ffn_in['shared_down'], 'L1_xattn_Wq': _L1_xattn_in['Wq'], 'L1_xattn_bq': _L1_xattn_in['bq'], 'L1_xattn_Wk': _L1_xattn_in['Wk'], 'L1_xattn_bk': _L1_xattn_in['bk'], 'L1_xattn_Wv': _L1_xattn_in['Wv'], 'L1_xattn_bv': _L1_xattn_in['bv'], 'L1_xattn_Wo': _L1_xattn_in['Wo'], 'L1_xattn_bo': _L1_xattn_in['bo'], 'L1_ffn_ln1_g': _L1_ffn_in['ln1_g'], 'L1_ffn_ln1_b': _L1_ffn_in['ln1_b'], 'L1_ffn_w1': _L1_ffn_in['w1'], 'L1_ffn_b1': _L1_ffn_in['b1'], 'L1_ffn_ln2_g': _L1_ffn_in['ln2_g'], 'L1_ffn_ln2_b': _L1_ffn_in['ln2_b'], 'L1_ffn_w2': _L1_ffn_in['w2'], 'L1_ffn_b2': _L1_ffn_in['b2']}

def reference(x, ctx_1024, mask_1x1xSxS2_fk1, mask_Bx1xSxS2_bk1, L0_xattn_wq_w, L0_xattn_wq_b, L0_xattn_wk_w, L0_xattn_wk_b, L0_xattn_wv_w, L0_xattn_wv_b, L0_xattn_wo_w, L0_xattn_wo_b, L0_ffn_router, L0_ffn_experts_gate, L0_ffn_experts_up, L0_ffn_experts_down, L0_ffn_shared_gate, L0_ffn_shared_up, L0_ffn_shared_down, L1_xattn_Wq, L1_xattn_bq, L1_xattn_Wk, L1_xattn_bk, L1_xattn_Wv, L1_xattn_bv, L1_xattn_Wo, L1_xattn_bo, L1_ffn_ln1_g, L1_ffn_ln1_b, L1_ffn_w1, L1_ffn_b1, L1_ffn_ln2_g, L1_ffn_ln2_b, L1_ffn_w2, L1_ffn_b2):
    import jax
    import jax.numpy as jnp

    def _L0_xattn_ref(v, k, q, mask, wq_w, wq_b, wk_w, wk_b, wv_w, wv_b, wo_w, wo_b):
        import jax, jax.numpy as jnp
        import numpy as np
        D_MODEL = 256
        NUM_HEADS = 16
        DEPTH = D_MODEL // NUM_HEADS
        BATCH = 4
        SEQ = 512
        NEG_BIG = -1000000000.0

        def _split_heads(x, b, s):
            return x.reshape(b, s, NUM_HEADS, DEPTH).transpose(0, 2, 1, 3)
        b, sq, _ = q.shape
        sk = k.shape[1]
        qh = _split_heads(q @ wq_w + wq_b, b, sq)
        kh = _split_heads(k @ wk_w + wk_b, b, sk)
        vh = _split_heads(v @ wv_w + wv_b, b, sk)
        logits = jnp.einsum('bhqd,bhkd->bhqk', qh, kh) / jnp.sqrt(jnp.float32(DEPTH))
        logits = logits + mask * NEG_BIG
        attn = jax.nn.softmax(logits, axis=-1)
        out = jnp.einsum('bhqk,bhkd->bhqd', attn, vh)
        out = out.transpose(0, 2, 1, 3).reshape(b, sq, D_MODEL)
        return out @ wo_w + wo_b

    def _L0_ffn_ref(x, router, experts_gate, experts_up, experts_down, shared_gate, shared_up, shared_down):
        import jax, jax.numpy as jnp
        import numpy as np
        TOP_K = 2
        NUM_EXPERTS = 8
        b, s, h = x.shape
        E = router.shape[1]
        shared_act = jax.nn.silu(jnp.einsum('bsh,hd->bsd', x, shared_gate))
        shared_up_out = jnp.einsum('bsh,hd->bsd', x, shared_up)
        shared_out = jnp.einsum('bsd,dh->bsh', shared_act * shared_up_out, shared_down)
        router_probs = jax.nn.softmax(jnp.einsum('bsh,he->bse', x, router), axis=-1)
        topk_probs, topk_idx = jax.lax.top_k(router_probs, TOP_K)
        coef = jnp.sum(jax.nn.one_hot(topk_idx, E, dtype=x.dtype) * topk_probs[..., None], axis=2)
        coef = coef.reshape(b * s, E)
        x_flat = x.reshape(b * s, h)
        gate = jnp.einsum('th,ehd->etd', x_flat, experts_gate)
        up = jnp.einsum('th,ehd->etd', x_flat, experts_up)
        expert_out = jnp.einsum('etd,edh->eth', jax.nn.silu(gate) * up, experts_down)
        routed = jnp.einsum('eth,te->th', expert_out, coef)
        return routed.reshape(b, s, h) + shared_out

    def _L1_xattn_ref(query, key, value, mask, Wq, bq, Wk, bk, Wv, bv, Wo, bo):
        import jax, jax.numpy as jnp
        import numpy as np
        D = 256
        H = 16
        DH = D // H
        B = 2
        S = 512

        def _split_heads(x):
            b, s, _ = x.shape
            return x.reshape(b, s, H, DH).transpose(0, 2, 1, 3)
        q = _split_heads(query @ Wq.T + bq)
        k = _split_heads(key @ Wk.T + bk)
        v = _split_heads(value @ Wv.T + bv)
        scores = jnp.einsum('bhqd,bhkd->bhqk', q, k) * (1.0 / np.sqrt(DH))
        scores = jnp.where(mask, jnp.float32(-1000000000.0), scores)
        attn = jax.nn.softmax(scores, axis=-1)
        ctx = jnp.einsum('bhqk,bhkd->bhqd', attn, v)
        ctx = ctx.transpose(0, 2, 1, 3).reshape(query.shape[0], -1, D)
        return ctx @ Wo.T + bo

    def _L1_ffn_ref(x, ln1_g, ln1_b, w1, b1, ln2_g, ln2_b, w2, b2):
        import jax, jax.numpy as jnp
        import numpy as np
        LN_EPS = 1e-05

        def layernorm(x, g, b):
            mu = jnp.mean(x, axis=-1, keepdims=True)
            var = jnp.mean((x - mu) ** 2, axis=-1, keepdims=True)
            return (x - mu) * jax.lax.rsqrt(var + LN_EPS) * g + b

        def act_quant_fake(x):
            scale = 127.0 / jnp.clip(jnp.max(jnp.abs(x), axis=-1, keepdims=True), 1e-05)
            return jnp.clip(jnp.round(x * scale), -128.0, 127.0) / scale

        def weight_quant_fake(w):
            scale = 1.0 / jnp.clip(jnp.mean(jnp.abs(w)), 1e-05)
            return jnp.clip(jnp.round(w * scale), -1.0, 1.0) / scale

        def bitlinear(x, w, b):
            dqx = act_quant_fake(x)
            dqw = weight_quant_fake(w)
            return jnp.einsum('btd,hd->bth', dqx, dqw) + b
        h = layernorm(x, ln1_g, ln1_b)
        h = bitlinear(h, w1, b1)
        h = jax.nn.gelu(h, approximate=False)
        h = layernorm(h, ln2_g, ln2_b)
        h = bitlinear(h, w2, b2)
        return h
    x = x + _L0_xattn_ref(ctx_1024, ctx_1024, _layernorm(x, axis=-1), mask_1x1xSxS2_fk1, L0_xattn_wq_w, L0_xattn_wq_b, L0_xattn_wk_w, L0_xattn_wk_b, L0_xattn_wv_w, L0_xattn_wv_b, L0_xattn_wo_w, L0_xattn_wo_b)
    x = x + _L0_ffn_ref(_layernorm(x, axis=-1), L0_ffn_router, L0_ffn_experts_gate, L0_ffn_experts_up, L0_ffn_experts_down, L0_ffn_shared_gate, L0_ffn_shared_up, L0_ffn_shared_down)
    x = x + _L1_xattn_ref(_layernorm(x, axis=-1), ctx_1024, ctx_1024, mask_Bx1xSxS2_bk1, L1_xattn_Wq, L1_xattn_bq, L1_xattn_Wk, L1_xattn_bk, L1_xattn_Wv, L1_xattn_bv, L1_xattn_Wo, L1_xattn_bo)
    x = x + _L1_ffn_ref(_layernorm(x, axis=-1), L1_ffn_ln1_g, L1_ffn_ln1_b, L1_ffn_w1, L1_ffn_b1, L1_ffn_ln2_g, L1_ffn_ln2_b, L1_ffn_w2, L1_ffn_b2)
    return x

_drawn_inputs = setup_inputs


def setup_inputs(seed=0):
    import zlib

    import numpy as np

    out = dict(_drawn_inputs(seed))
    spreads = {'L0_xattn_wq_b': (0.0, 0.1),
     'L0_xattn_wk_b': (0.0, 0.8),
     'L0_xattn_wv_b': (0.0, 0.1),
     'L0_xattn_wo_b': (0.0, 0.1),
     'L1_xattn_bq': (0.0, 0.346),
     'L1_xattn_bk': (0.0, 0.8),
     'L1_xattn_bv': (0.0, 0.1),
     'L1_xattn_bo': (0.0, 0.1),
     'L1_ffn_ln1_g': (1.0, 0.2),
     'L1_ffn_ln1_b': (0.0, 0.1),
     'L1_ffn_ln2_g': (1.0, 0.2),
     'L1_ffn_ln2_b': (0.0, 0.1)}
    factors = {'L1_ffn_b1': 3.876, 'L1_ffn_b2': 4.994}
    for name, (base, spread) in spreads.items():
        noise = np.random.default_rng([zlib.crc32(name.encode()), seed]).standard_normal(out[name].shape)
        drawn = base * np.exp(spread * noise) if base else spread * noise
        out[name] = jnp.asarray(drawn.astype(out[name].dtype))
    for name, factor in factors.items():
        out[name] = (out[name] * factor).astype(out[name].dtype)
    return out
```

```python
from contextlib import ExitStack

import numpy as np
import concourse.bass as bass
from concourse import mybir

F32 = mybir.dt.float32
F32R = mybir.dt.float32r
BF16 = mybir.dt.bfloat16
U8 = mybir.dt.uint8
U32 = mybir.dt.uint32
ALU = mybir.AluOpType
ACT = mybir.ActivationFunctionType
AX = mybir.AxisListType

P = 128
B, SQ, D = 4, 1024, 256
SK = 77
HEADS, DH = 16, 16
G = D // P
HG = HEADS // G
T = B * SQ // P
TB = SQ // P
CK = -(-HG * SK // P)
LASTK = HG * SK - (CK - 1) * P
VW = P + HG
NE, TOPK, DE, DS = 8, 2, 128, 256
CH = NE + DS // P
ST = 4
NG = T // ST
GW = ST * P
HID = 1024
KH = HID // P
MLP_ROWS = ("g1", "c1", "b1", "g2", "c2", "b2")
EPS = 1e-5
NEG = -1e9
HUGE = 3e38
MAGIC = 1.5 * 2.0 ** 23
SCORE = DH ** -0.5


def piece(t, width):
    return bass.ds(t * width, width)


def hold(dve, sem, value, spare):
    dve.wait_ge(sem, value)
    dve.memset(spare, 0.0)


def run_steps(eng, step, lead, lag=0):
    first, last = lag, T - lead
    some = lambda t: lambda k: 0 <= t + k < T
    for t in range(-lead, first):
        step(t, t % 2, some(t))
    pairs = (last - first) // 2
    with eng.Fori(0, pairs) as i:
        for u in range(2):
            step(2 * i + (first + u), (first + u) % 2, lambda k: True)
    for t in range(first + 2 * pairs, T + lag):
        step(t, t % 2, some(t))


def load_phase(nc, dram, sb):
    with ExitStack() as ctx:
        sem = lambda n: ctx.enter_context(nc.semaphore(n))
        s_c, s_m, s_bn, s_sums, s_tot, s_q, s_abs = (sem(n) for n in (
            "const_step", "lnw_step", "tile_stats", "abs_sums", "abs_total", "quant_step", "abs_row"))
        junk = ctx.enter_context(nc.sbuf_tensor("w_abs", [P, 2 * HID], F32))
        wr = ctx.enter_context(nc.sbuf_tensor("w_round", [P, 2 * HID], F32))
        rows = ctx.enter_context(nc.sbuf_tensor("w_rowsum", [P, 2], F32))
        wsc = ctx.enter_context(nc.sbuf_tensor("w_scale", [P, 2], F32))
        tot = ctx.enter_context(nc.psum_tensor("w_total", [P, 2], F32))
        st = ctx.enter_context(nc.sbuf_tensor("st0", [P, T, 6], F32))
        block = ctx.enter_context(nc.Block())

        @block.sync
        def _(sp):
            for b in range(B):
                sp.dma_start(sb["x"][:, b * TB:(b + 1) * TB, :],
                             dram["x"][b].rearrange("(t p) d -> p t d", p=P)).then_inc(sb["x_in"], 16)
            sp.dma_start(sb["w1"][:], dram["w1"].rearrange("(k p) n -> p k n", p=P)).then_inc(sb["mlp_in"], 16)
            sp.dma_start(sb["w2"][:], dram["w2"].rearrange("(k p) n -> p k n", p=P)).then_inc(sb["mlp_in"], 16)
            sp.dma_start(sb["gu"][:], dram["gu"].rearrange("(k p) n -> p k n", p=P)).then_inc(sb["moe_in"], 16)
            sp.dma_start(sb["dn"][:], dram["dn"].rearrange("(c p) n -> p c n", p=P)).then_inc(sb["moe_in"], 16)
            sp.dma_start(sb["rt"][:], dram["rt"].rearrange("(k p) n -> p k n", p=P)).then_inc(sb["moe_in"], 16)

        @block.scalar
        def _(act):
            act.dma_start(sb["ctx"][:], dram["ctx"].rearrange("(k p) n -> p k n", p=P)).then_inc(sb["att_in"], 16)
            for n in range(2):
                act.dma_start(sb["aw"][n][:], dram["aw"][n].rearrange("(k p) n -> p k n", p=P)).then_inc(sb["att_in"], 16)
                act.dma_start(sb["bqk"][n][:], dram["bqk"][n].rearrange("p (a g) -> p a g", g=G)).then_inc(sb["att_in"], 16)
                act.dma_start(sb["bv"][n][:], dram["bv"][n]).then_inc(sb["att_in"], 16)
                act.dma_start(sb["bo"][n][:], dram["bo"][n].broadcast_to([P, D])).then_inc(sb["att_in"], 16)
            act.dma_start(sb["m0"][:], dram["m0"].rearrange("(t p) k -> p t k", p=P)).then_inc(sb["att_in"], 16)
            act.dma_start(sb["m1"][:], dram["m1"].rearrange("(t p) k -> p t k", p=P)).then_inc(sb["att_in"], 16)
            act.wait_ge(sb["mlp_in"], 2 * 16)
            act.activation(junk[:], sb["w1"][:].rearrange("p k n -> p (k n)"), ACT.Abs,
                           accum_out=rows[:, 0:1]).then_inc(s_abs, 1)
            act.wait_ge(s_abs, 1)
            act.activation(junk[:], sb["w2"][:].rearrange("p k n -> p (k n)"), ACT.Abs,
                           accum_out=rows[:, 1:2]).then_inc(s_sums, 1)

        @block.gpsimd
        def _(pool):
            pool.memset(sb["ones"][:], 1.0).then_inc(s_c, 1)
            pool.memset(sb["hmask"][:], 1.0).then_inc(s_c, 1)
            pool.memset(sb["kmask"][:], 1.0).then_inc(s_c, 1)
            pool.memset(sb["ident"][:], 0.0).then_inc(s_c, 1)
            pool.memset(sb["lower"][:], 1.0).then_inc(s_c, 1)
            pool.wait_ge(s_c, 5)
            pool.affine_select(out=sb["ident"][:], in_=sb["ident"][:], compare_op=ALU.not_equal, fill=1.0,
                               base=0, pattern=[[-1, P]], channel_multiplier=1).then_inc(s_c, 1)
            pool.affine_select(out=sb["hmask"][:], in_=sb["hmask"][:], compare_op=ALU.is_ge, fill=0.0,
                               base=0, pattern=[[-DH, HG]], channel_multiplier=1).then_inc(s_c, 1)
            pool.affine_select(out=sb["kmask"][:], in_=sb["kmask"][:], compare_op=ALU.is_ge, fill=0.0,
                               base=0, pattern=[[P, CK], [-SK, HG]], channel_multiplier=1).then_inc(s_c, 1)
            pool.wait_ge(s_c, 8)
            pool.affine_select(out=sb["hmask"][:], in_=sb["hmask"][:], compare_op=ALU.is_ge, fill=0.0,
                               base=DH - 1, pattern=[[DH, HG]], channel_multiplier=-1).then_inc(s_c, 1)
            pool.affine_select(out=sb["kmask"][:], in_=sb["kmask"][:], compare_op=ALU.is_ge, fill=0.0,
                               base=SK - 1, pattern=[[-P, CK], [SK, HG]], channel_multiplier=-1).then_inc(s_c, 1)
            pool.affine_select(out=sb["lower"][:], in_=sb["lower"][:], compare_op=ALU.is_ge, fill=0.0,
                               base=-1, pattern=[[1, NE], [-1, NE]], channel_multiplier=0).then_inc(s_c, 1)

        @block.tensor
        def _(pe):
            pe.wait_ge(s_c, 11)
            pe.wait_ge(s_sums, 1)
            pe.matmul(tot[:], sb["ones"][:], rows[:], start=True, stop=True).then_inc(s_tot, 1)

        @block.vector
        def _(dve):
            for t in range(T):
                dve.wait_ge(sb["x_in"], 16 * B)
                dve.bn_stats(st[:, t, :], sb["x"][:, t, :]).then_inc(s_bn, 1)
            for t in range(T):
                dve.wait_ge(s_bn, T)
                dve.bn_aggr(sb["mv"][:, t, :], st[:, t, :])
            dve.wait_ge(s_tot, 1)
            dve.tensor_scalar(sb["wsi"][:], tot[:], 1.0 / (HID * D), 1e-5, ALU.mult, ALU.max).then_inc(s_q, 1)
            dve.wait_ge(s_q, 1)
            dve.reciprocal(wsc[:], sb["wsi"][:]).then_inc(s_q, 1)
            n = 2
            for k, (raw, out) in enumerate((("w1", "q1"), ("w2", "q2"))):
                w = sb[raw][:].rearrange("p k n -> p (k n)")
                dve.wait_ge(s_q, n)
                dve.tensor_scalar(wr[:], w, wsc[:, k:k + 1], 1.0, ALU.mult, ALU.min).then_inc(s_q, 1)
                dve.wait_ge(s_q, n + 1)
                dve.tensor_scalar(wr[:], wr[:], -1.0, MAGIC, ALU.max, ALU.add).then_inc(s_q, 1)
                dve.wait_ge(s_q, n + 2)
                dve.tensor_scalar(sb[out][:].rearrange("p k n -> p (k n)"), wr[:], -MAGIC, None,
                                  ALU.add).then_inc(s_q, 1)
                n += 3
            dve.tensor_copy(sb["identb"][:], sb["ident"][:])


def norm_and_keys_phase(nc, dram, sb, layer):
    with ExitStack() as ctx:
        sem = lambda n: ctx.enter_context(nc.semaphore(n + str(layer) + sb["tag"]))
        s_sd, s_r, s_kt, s_kc, s_kb, s_rep, s_v, s_vb, s_m, s_kp = (sem(n) for n in (
            "sd", "rstd_step", "kT_ps", "kT_sb", "kbd", "ctx_rep", "v_ps", "vbd", "mask_step", "k_parts"))
        r = ctx.enter_context(nc.sbuf_tensor("r" + sb["tag"], [P, 3, T], F32))
        if layer is not None:
            rep = ctx.enter_context(nc.sbuf_tensor("rep" + sb["tag"], [P, G, CK * P], F32))
            kt = ctx.enter_context(nc.sbuf_tensor("kt" + sb["tag"], [P, B * G, SK], F32))
            kh = ctx.enter_context(nc.sbuf_tensor("kh" + sb["tag"], [P, B * G, SK], F32R))
            kl = ctx.enter_context(nc.sbuf_tensor("kl" + sb["tag"], [P, B * G, SK], F32R))
            pk = ctx.enter_context(nc.psum_tensor("pk" + sb["tag"], [P, 512], F32))
            pv = ctx.enter_context(nc.psum_tensor("pv" + sb["tag"], [P, 2, 1024], F32))
            aw, bqk, bv = sb["aw"][layer], sb["bqk"][layer], sb["bv"][layer]
        block = ctx.enter_context(nc.Block())

        per_head = lambda ap: ap.rearrange("p (h k) -> p h k", k=SK)
        every_head = lambda ap: ap.rearrange("p (a k) -> p a k", a=1).broadcast_to([P, HG, SK])
        own_rows = sb["hmask"][:].rearrange("p (h a) -> p h a", a=1).broadcast_to([P, HG, SK])

        @block.sync
        def _(sp):
            if layer == 1:
                for name in MLP_ROWS:
                    sp.dma_start(sb[name][:], dram[name].broadcast_to(list(sb[name].shape))).then_inc(sb["mlp_in"], 16)

        @block.gpsimd
        def _(pool):
            if layer is None:
                return
            for n in range(B * G):
                pool.wait_ge(s_kp, 2 * n + 2)
                pool.tensor_tensor(per_head(sb["Kl"][:, n, :]), every_head(kl[:, n, :].bitcast(F32)), own_rows, ALU.mult)

        @block.scalar
        def _(act):
            act.wait_ge(s_r, 1)
            act.activation(r[:, 1, :], r[:, 0, :], ACT.Sqrt).then_inc(s_sd, 1)

        @block.vector
        def _(dve):
            v, s, y = r[:, 0, :], r[:, 1, :], r[:, 2, :]
            dve.tensor_scalar(v, sb["mv"][:, :, 1], EPS, None, ALU.add).then_inc(s_r, 1)
            dve.wait_ge(s_sd, 1)
            steps = [lambda: dve.reciprocal(y, s),
                     lambda: dve.tensor_tensor(s, y, y, ALU.mult),
                     lambda: dve.tensor_tensor(s, s, v, ALU.mult),
                     lambda: dve.tensor_scalar(s, s, -0.5, 1.5, ALU.mult, ALU.add),
                     lambda: dve.tensor_tensor(sb["rs"][:], y, s, ALU.mult),
                     lambda: dve.tensor_tensor(v, sb["mv"][:, :, 0], sb["rs"][:], ALU.mult),
                     lambda: dve.tensor_scalar(sb["nm"][:], v, -1.0, None, ALU.mult)]
            for n, step in enumerate(steps):
                step().then_inc(s_r, 1)
                dve.wait_ge(s_r, n + 2)
            if layer is None:
                return
            dve.wait_ge(sb["att_in"], 16 * 11)
            if layer == 0:
                dve.tensor_scalar(sb["mask"][:, 0:TB, :], sb["m0"][:], NEG, None, ALU.mult).then_inc(s_m, 1)
            else:
                dve.tensor_scalar(sb["mask"][:], sb["m1"][:], 0.0, None, ALU.is_equal).then_inc(s_m, 1)
                dve.wait_ge(s_m, 1)
                dve.tensor_scalar(sb["mask"][:], sb["mask"][:], HUGE, NEG, ALU.mult, ALU.add)
            for b in range(B):
                if b:
                    dve.wait_ge(s_v, G * b)
                for k in range(G):
                    c = sb["ctx"][:, k, b * SK:(b + 1) * SK].rearrange("p (a n) -> p a n", a=1)
                    dve.tensor_copy(rep[:, k, 0:HG * SK].rearrange("p (a n) -> p a n", n=SK),
                                    c.broadcast_to([P, HG, SK]))
                    dve.tensor_copy(rep[:, k, HG * SK:CK * P], sb["ctx"][:, k, 0:CK * P - HG * SK]).then_inc(s_rep, 1)
                for g in range(G):
                    n = b * G + g
                    dve.wait_ge(s_kt, n + 1)
                    dve.tensor_scalar(kt[:, n, :], pk[:, 0:SK], bqk[:, 1, g:g + 1], SCORE,
                                      ALU.add, ALU.mult).then_inc(s_kc, 1)
                    dve.wait_ge(s_kc, n + 1)
                    dve.tensor_copy(kh[:, n, :], kt[:, n, :]).then_inc(s_kp, 1)
                    dve.wait_ge(s_kp, 2 * n + 1)
                    dve.tensor_tensor(kl[:, n, :], kt[:, n, :], kh[:, n, :].bitcast(F32), ALU.subtract).then_inc(s_kp, 1)
                    dve.tensor_tensor(per_head(sb["Kh"][:, n, :]), every_head(kh[:, n, :].bitcast(F32)), own_rows, ALU.mult)
                    dve.wait_ge(s_v, n + 1)
                    V = sb["V"][:, n, :].rearrange("p (c w) -> p c w", w=VW)
                    dve.tensor_tensor(V[:, :, 0:P].rearrange("p c (h d) -> p c h d", d=DH),
                                      pv[:, n % 2, 0:CK * P].rearrange("p (c h d) -> p c h d", d=DH, h=HG),
                                      sb["kmask"][:].rearrange("p c (h a) -> p c h a", a=1).broadcast_to([P, CK, HG, DH]),
                                      ALU.mult)
                    dve.tensor_copy(V[:, :, P:VW], sb["kmask"][:]).then_inc(s_vb, 1)

        @block.tensor
        def _(pe):
            if layer is None:
                return
            pe.wait_ge(sb["att_in"], 16 * 11)
            for b in range(B):
                for g in range(G):
                    n = b * G + g
                    if n:
                        pe.wait_ge(s_kc, n)
                    for k in range(G):
                        mm = pe.matmul(pk[:, 0:SK], aw[:, k, D + g * P:D + (g + 1) * P],
                                       sb["ctx"][:, k, b * SK:(b + 1) * SK], start=(k == 0), stop=(k == G - 1))
                    mm.then_inc(s_kt, 1)
                    pe.wait_ge(s_rep, G * (b + 1))
                    if n >= 2:
                        pe.wait_ge(s_vb, n - 1)
                    for c in range(CK):
                        out = pv[:, n % 2, c * P:(c + 1) * P]
                        for k in range(G):
                            pe.matmul(out, rep[:, k, c * P:(c + 1) * P],
                                      aw[:, k, 2 * D + g * P:2 * D + (g + 1) * P], start=(k == 0), stop=False)
                        mm = pe.matmul(out, sb["ones"][0:1, :], bv[0:1, g * P:(g + 1) * P], start=False, stop=True)
                    mm.then_inc(s_v, 1)


def attention_phase(nc, sb, layer):
    tag = sb["tag"]
    with ExitStack() as ctx:
        sem = lambda n: ctx.enter_context(nc.semaphore(n + tag))
        sbt = lambda n, s, d=F32: ctx.enter_context(nc.sbuf_tensor(n + tag, s, d))
        pst = lambda n, s, d=F32: ctx.enter_context(nc.psum_tensor(n + tag, s, d))
        (normed, xt_ps, xt_sb, q_ps, q_hi, q_sb, scored, masked, maxed, shifted, exped, pt_ps, pt_sb,
         weighed, recips, o_norm, ot_ps, ot_sb, projected, biased, added, stated) = (sem(n) for n in (
             "normed", "xt_ps", "xt_sb", "q_ps", "q_hi", "q_sb", "scored", "masked", "maxed", "shifted",
             "exped", "pt_ps", "pt_sb", "weighed", "recips", "o_norm", "ot_ps", "ot_sb", "projected",
             "biased", "added", "stated"))
        NS = HG * SK
        HS = NS // 2
        xn = [sbt(f"xn{i}", [P, D]) for i in range(2)]
        xt = [sbt(f"xt{i}", [P, D]) for i in range(2)]
        qh = [sbt(f"qh{i}", [P, D], F32R) for i in range(2)]
        ql = [sbt(f"ql{i}", [P, D], F32R) for i in range(2)]
        sm = [sbt(f"sm{i}", [P, G * NS]) for i in range(2)]
        mx = [sbt(f"mx{i}", [P, HEADS]) for i in range(2)]
        pr = [sbt(f"pr{i}", [P, G * NS]) for i in range(2)]
        pt = sbt("pt", [P, G * CK, P])
        rc = [sbt(f"rc{i}", [P, HEADS]) for i in range(2)]
        on = sbt("on", [P, D])
        ot = sbt("ot", [P, D])
        st = sbt("st", [P, 6])
        av = sbt("av", [P, 2])
        spare = sbt("spare", [P, 1])
        pA = pst("pA", [P, 512])
        pO = pst("pO", [P, 512])
        pS = pst("pS", [P, 4, 512])
        pT = pst("pT", [P, 2, 512])
        block = ctx.enter_context(nc.Block())
        aw, bqk, bo = sb["aw"][layer], sb["bqk"][layer], sb["bo"][layer]
        X = sb["x"][:].rearrange("p t d -> p (t d)")
        RS, NM = sb["rs"], sb["nm"]
        MV = sb["mv"][:].rearrange("p t a -> p (t a)")
        KH = sb["Kh"][:].rearrange("p n w -> p (n w)")
        KL = sb["Kl"][:].rearrange("p n w -> p (n w)")
        VB = sb["V"][:].rearrange("p n w -> p (n w)")
        MASK = sb["mask"][:].rearrange("p t k -> p (t k)")
        chunks = [(g, c) for g in range(G) for c in range(CK)]
        J = -(-len(chunks) // 4)
        rows = lambda c: LASTK if c == CK - 1 else P
        heads = lambda ap: ap.rearrange("p (h k) -> p h k", k=SK)
        banked = lambda ap: ap.rearrange("p (b h k) -> p b h k", b=4, k=SK)

        @block.gpsimd
        def _(pool):
            def shift(t, u):
                pool.wait_ge(maxed, t + 1)
                pool.tensor_tensor(heads(sm[u][:]), heads(sm[u][:]),
                                   mx[u][:].rearrange("p (h a) -> p h a", a=1).broadcast_to([P, HEADS, SK]),
                                   ALU.subtract).then_inc(shifted, 1)

            def bias(t):
                pool.wait_ge(normed, t + 1)
                pool.tensor_tensor(X[:, piece(t, D)], X[:, piece(t, D)], bo[:], ALU.add).then_inc(biased, 1)

            def step(t, u, has):
                if has(1):
                    shift(t + 1, 1 - u)
                    bias(t + 1)

            run_steps(pool, step, 3, 1)

        @block.tensor
        def _(pe):
            pe.sem_inc(xt_ps, 2)
            pe.sem_inc(pt_ps, 2 * J)
            pe.sem_inc(weighed, 1)

            def turn_x(t, u):
                pe.wait_ge(normed, t + 1)
                pe.wait_ge(q_sb, t + 1)
                for k in range(G):
                    mm = pe.transpose(pA[:, k * P:(k + 1) * P], xn[u][:, k * P:(k + 1) * P], sb["ident"][:])
                mm.then_inc(xt_ps, 1)

            def queries(t, u):
                pe.wait_ge(xt_sb, t + 1)
                for g in range(G):
                    for k in range(G):
                        mm = pe.matmul(pA[:, D + g * P:D + (g + 1) * P], aw[:, k, g * P:(g + 1) * P],
                                       xt[u][:, k * P:(k + 1) * P], start=(k == 0), stop=(k == G - 1))
                mm.then_inc(q_ps, 1)

            def scores(t, u):
                pe.wait_ge(q_sb, t + 2)
                pe.wait_ge(masked, t + 1)
                keys = (t // TB) * (G * NS)
                for b in range(4):
                    g = b // 2
                    h, l = qh[u][:, g * P:(g + 1) * P], ql[u][:, g * P:(g + 1) * P]
                    at = bass.ds(keys + b * HS, HS)
                    pe.matmul(pS[:, b, 0:HS], h, KH[:, at], start=True, stop=False)
                    pe.matmul(pS[:, b, 0:HS], h, KL[:, at], start=False, stop=False)
                    mm = pe.matmul(pS[:, b, 0:HS], l, KH[:, at], start=False, stop=True)
                mm.then_inc(scored, 1)

            def turn_p(t, u, j):
                if j == 0:
                    pe.wait_ge(exped, t + 3)
                pe.wait_ge(pt_sb, J * t + j + 1)
                for n in range(4 * j, min(4 * j + 4, len(chunks))):
                    g, c = chunks[n]
                    at = g * NS + c * P
                    mm = pe.transpose(pT[0:rows(c), (u + j) % 2, (n % 4) * P:(n % 4 + 1) * P],
                                      pr[u][:, at:at + rows(c)], sb["ident"][:])
                mm.then_inc(pt_ps, 1)

            def weigh(t, u, g):
                if g == 0:
                    pe.wait_ge(added, t + 1)
                vals = (t // TB) * (G * CK * VW)
                for n, (half, c) in enumerate(chunks):
                    if half != g:
                        continue
                    if c == 0 or n % 4 == 0:
                        pe.wait_ge(pt_sb, J * t + n // 4 + 3)
                    mm = pe.matmul(pO[:, g * VW:(g + 1) * VW], pt[0:rows(c), n, :],
                                   VB[0:rows(c), bass.ds(vals + n * VW, VW)],
                                   start=(c == 0), stop=(c == CK - 1))
                if g == G - 1:
                    mm.then_inc(weighed, 1)

            def turn_o(t):
                pe.wait_ge(o_norm, t + 1)
                for k in range(G):
                    mm = pe.transpose(pO[:, k * P:(k + 1) * P], on[:, k * P:(k + 1) * P], sb["ident"][:])
                mm.then_inc(ot_ps, 1)

            def project(t):
                pe.wait_ge(ot_sb, t + 1)
                for k in range(G):
                    mm = pe.matmul(pO[:, 0:D], ot[:, k * P:(k + 1) * P], aw[:, k, 3 * D:4 * D],
                                   start=(k == 0), stop=(k == G - 1))
                mm.then_inc(projected, 1)

            def step(t, u, has):
                if has(0):
                    turn_p(t, u, 0)
                if has(-1):
                    project(t - 1)
                if has(0):
                    turn_p(t, u, 1)
                    turn_p(t, u, 2)
                if has(2):
                    turn_x(t + 2, u)
                if has(0):
                    weigh(t, u, 0)
                if has(2):
                    queries(t + 2, u)
                if has(0):
                    weigh(t, u, 1)
                if has(2):
                    scores(t + 2, u)
                if has(0):
                    turn_o(t)

            run_steps(pe, step, 3, 1)

        @block.scalar
        def _(act):
            act.sem_inc(pt_sb, 2)
            act.sem_inc(exped, 2)

            def xt_out(t, u):
                act.wait_ge(xt_ps, t + 3)
                act.activation(xt[u][:], pA[:, 0:D], ACT.Copy).then_inc(xt_sb, 1)

            def exp(t, u):
                act.wait_ge(shifted, t + 1)
                act.wait_ge(pt_ps, J * (t + 1))
                act.activation(pr[u][:], sm[u][:], ACT.Exp).then_inc(exped, 1)

            def pt_out(t, u, j):
                if j == 0:
                    act.wait_ge(weighed, t + 1)
                act.wait_ge(pt_ps, J * t + j + 1 + 2 * J)
                runs = []
                for n in range(4 * j, min(4 * j + 4, len(chunks))):
                    r = rows(chunks[n][1])
                    if runs and r == P and runs[-1][2] == P and runs[-1][1] == n:
                        runs[-1][1] = n + 1
                    else:
                        runs.append([n, n + 1, r])
                for lo, hi, r in runs:
                    last = act.activation(pt[0:r, lo:hi, :].rearrange("p n t -> p (n t)"),
                                          pT[0:r, (u + j) % 2, (lo % 4) * P:(lo % 4 + hi - lo) * P], ACT.Copy)
                last.then_inc(pt_sb, 1)

            def ot_out(t):
                act.wait_ge(ot_ps, t + 1)
                act.activation(ot[:], pO[:, 0:D], ACT.Copy).then_inc(ot_sb, 1)

            def step(t, u, has):
                if has(0):
                    for j in range(J):
                        pt_out(t, u, j)
                if has(2):
                    xt_out(t + 2, u)
                if has(1):
                    exp(t + 1, 1 - u)
                if has(0):
                    ot_out(t)

            run_steps(act, step, 3, 1)

        @block.vector
        def _(dve):
            dve.sem_inc(q_sb, 1)
            dve.sem_inc(masked, 1)
            dve.sem_inc(added, 1)

            def norm(t, u):
                dve.wait_ge(xt_ps, t + 1)
                dve.tensor_scalar(xn[u][:], X[:, piece(t, D)], RS[:, bass.ds(t, 1)], NM[:, bass.ds(t, 1)],
                                  ALU.mult, ALU.add).then_inc(normed, 1)

            def q_out(t, u):
                dve.wait_ge(q_ps, t + 1)
                dve.tensor_tensor(qh[u][:].rearrange("p (g n) -> p g n", g=G),
                                  pA[:, D:2 * D].rearrange("p (g n) -> p g n", g=G),
                                  bqk[:, 0, :].rearrange("p (g a) -> p g a", a=1).broadcast_to([P, G, P]),
                                  ALU.add).then_inc(q_hi, 1)
                dve.wait_ge(q_hi, t + 1)
                for g in range(G):
                    half = slice(g * P, (g + 1) * P)
                    last = dve.scalar_tensor_tensor(ql[u][:, half], pA[:, D + g * P:D + (g + 1) * P],
                                                    bqk[:, 0, g:g + 1], qh[u][:, half].bitcast(F32),
                                                    ALU.add, ALU.subtract)
                last.then_inc(q_sb, 1)

            def mask(t, u):
                dve.wait_ge(scored, t + 1)
                dve.wait_ge(exped, t + 1)
                at = (t % TB) * SK if layer == 0 else t * SK
                every = MASK[:, bass.ds(at, SK)].rearrange("p (a b k) -> p a b k", a=1, b=1)
                dve.tensor_tensor(banked(sm[u][:]), pS[:, :, 0:HS].rearrange("p b (h k) -> p b h k", k=SK),
                                  every.broadcast_to([P, 4, HEADS // 4, SK]),
                                  ALU.add if layer == 0 else ALU.min).then_inc(masked, 1)

            def largest(t, u):
                dve.wait_ge(masked, t + 2)
                dve.tensor_reduce(mx[u][:], heads(sm[u][:]), AX.X, ALU.max).then_inc(maxed, 1)

            def normalise(t, u):
                dve.wait_ge(weighed, t + 2)
                o = pO[:, 0:G * VW].rearrange("p (g w) -> p g w", g=G)
                dve.reciprocal(rc[u][:].rearrange("p (g h) -> p g h", g=G), o[:, :, P:VW]).then_inc(recips, 1)
                dve.wait_ge(recips, t + 1)
                dve.tensor_tensor(on[:].rearrange("p (g h d) -> p g h d", g=G, d=DH),
                                  o[:, :, 0:P].rearrange("p g (h d) -> p g h d", d=DH),
                                  rc[u][:].rearrange("p (g h a) -> p g h a", g=G, a=1).broadcast_to([P, G, HG, DH]),
                                  ALU.mult).then_inc(o_norm, 1)

            def add(t):
                dve.wait_ge(projected, t + 1)
                dve.wait_ge(biased, t + 1)
                dve.tensor_tensor(X[:, piece(t, D)], pO[:, 0:D], X[:, piece(t, D)], ALU.add).then_inc(added, 1)

            def stats(t):
                hold(dve, added, t + 2, spare[:])
                dve.bn_stats(st[:], X[:, piece(t, D)]).then_inc(stated, 1)
                hold(dve, stated, 2 * t + 1, spare[:])
                dve.bn_aggr(av[:], st[:]).then_inc(stated, 1)
                dve.wait_ge(stated, 2 * t + 2)
                dve.tensor_copy(MV[:, piece(t, 2)], av[:])

            def step(t, u, has):
                if has(-1):
                    add(t - 1)
                if has(1):
                    largest(t + 1, 1 - u)
                if has(-1):
                    stats(t - 1)
                if has(3):
                    norm(t + 3, 1 - u)
                if has(2):
                    q_out(t + 2, u)
                if has(0):
                    normalise(t, u)
                if has(2):
                    mask(t + 2, u)

            run_steps(dve, step, 3, 1)


def moe_phase(nc, sb):
    tag = sb["tag"]
    with ExitStack() as ctx:
        sem = lambda n: ctx.enter_context(nc.semaphore(n + tag))
        sbt = lambda n, s, d=F32: ctx.enter_context(nc.sbuf_tensor(n + tag, s, d))
        pst = lambda n, s, d=F32: ctx.enter_context(nc.psum_tensor(n + tag, s, d))
        (w_hi, w_ready, normed, xt_ps, xh_ok, xt_ok, l_ps, l_sb, lt_ps, r_step, dist, exped, r_chain,
         gu_ps, silued, h_ok, hh_ok, hl_ok, dn_ps, added, stated) = (sem(n) for n in (
             "w_hi", "w_ready", "normed", "xt_ps", "xh_ok", "xt_ok", "l_ps", "l_sb", "lt_ps", "r_step",
             "dist", "exped", "r_chain", "gu_ps", "silued", "h_ok", "hh_ok", "hl_ok", "dn_ps", "added",
             "stated"))
        NGU = CH * 2 * P
        wgh, wgl = sbt("wgh", [P, G, NGU], F32R), sbt("wgl", [P, G, NGU], F32R)
        wdh, wdl = sbt("wdh", [P, CH, D], F32R), sbt("wdl", [P, CH, D], F32R)
        wrh, wrl = sbt("wrh", [P, G, P], F32R), sbt("wrl", [P, G, P], F32R)
        xn = [sbt(f"xn{i}", [P, D]) for i in range(2)]
        xh, xl = sbt("xh", [P, 2 * G * GW], F32R), sbt("xl", [P, 2 * G * GW], F32R)
        lg = sbt("lg", [P, GW])
        lt = sbt("lt", [P, ST, NE])
        top = sbt("top", [P, ST])
        rank = sbt("rank", [P, ST, NE])
        gt, eq = sbt("gt", [P, ST, NE, NE]), sbt("eq", [P, ST, NE, NE])
        ds_ = sbt("ds", [P, ST, NE])
        ex = sbt("ex", [P, ST, NE])
        sums = sbt("sums", [P, 2, ST])
        coef = sbt("coef", [P, 2 * ST * NE])
        sg = [sbt(f"sg{i}", [P, GW]) for i in range(2)]
        hf = [sbt(f"hf{i}", [P, GW]) for i in range(2)]
        hh = [sbt(f"hh{i}", [P, GW], F32R) for i in range(2)]
        hl = [sbt(f"hl{i}", [P, GW], F32R) for i in range(2)]
        st = sbt("st", [P, ST, 6])
        av = sbt("av", [P, ST, 2])
        spare = sbt("spare", [P, 1])
        pGU = [pst(f"pGU{i}", [P, 2, GW]) for i in range(2)]
        pD = pst("pD", [P, ST, D])
        pX = pst("pX", [P, 512])
        pL = pst("pL", [P, 512])
        block = ctx.enter_context(nc.Block())
        X = sb["x"][:].rearrange("p t d -> p (t d)")
        MV = sb["mv"][:].rearrange("p t a -> p (t a)")
        RS, NM = sb["rs"], sb["nm"]
        f32 = lambda ap: ap.bitcast(F32)

        def xpart(buf, s, k, lo=0, n=GW):
            return buf[:, bass.ds((s % 2) * (G * GW) + (k * GW + lo), n)]

        @block.gpsimd
        def _(pool):
            def low(n, u):
                pool.wait_ge(hh_ok, n + 1)
                pool.wait_ge(dn_ps, n + 1)
                pool.tensor_tensor(hl[u][:], hf[u][:], f32(hh[u][:]), ALU.subtract).then_inc(hl_ok, 1)

            pool.sem_inc(hl_ok, 2)
            with pool.Fori(0, NG) as s:
                for c in range(CH):
                    low(s * CH + c, c % 2)

        @block.tensor
        def _(pe):
            pe.sem_inc(xt_ps, 2)
            pe.sem_inc(dn_ps, 2)

            def turn(s):
                for j in range(ST):
                    t = ST * s + j
                    pe.wait_ge(normed, t + 1)
                    pe.wait_ge(xt_ok, t + 1)
                    for k in range(G):
                        mm = pe.transpose(pX[:, k * P:(k + 1) * P], xn[j % 2][:, k * P:(k + 1) * P], sb["ident"][:])
                    mm.then_inc(xt_ps, 1)

            def three(out, ah, al, bh, bl, first, last):
                pe.matmul(out, ah, bh, start=first, stop=False)
                pe.matmul(out, ah, bl, start=False, stop=False)
                return pe.matmul(out, al, bh, start=False, stop=last)

            def route(s):
                pe.wait_ge(xt_ok, ST * s + ST + 1)
                pe.wait_ge(r_step, s + 1)
                for k in range(G):
                    mm = three(pL[:], wrh[:, k, :], wrl[:, k, :], xpart(xh, s, k), xpart(xl, s, k),
                               k == 0, k == G - 1)
                mm.then_inc(l_ps, 1)

            def route_back(s):
                pe.wait_ge(l_sb, s + 1)
                for j in range(ST):
                    mm = pe.transpose(pL[:, j * P:(j + 1) * P], lg[:, j * P:(j + 1) * P], sb["ident"][:])
                mm.then_inc(lt_ps, 1)

            def gate_up(s, c):
                n = s * CH + c
                pe.wait_ge(xt_ok, ST * s + ST + 1)
                pe.wait_ge(h_ok, n + 1)
                for a in range(2):
                    at = (2 * c + a) * P
                    for k in range(G):
                        mm = three(pGU[c % 2][:, a, :], wgh[:, k, at:at + P], wgl[:, k, at:at + P],
                                   xpart(xh, s, k), xpart(xl, s, k), k == 0, k == G - 1)
                mm.then_inc(gu_ps, 1)

            def down(s, c):
                n = s * CH + c
                pe.wait_ge(hl_ok, n + 3)
                if c != CH - 1:
                    pe.wait_ge(added, s * (CH - 1) + c + 1)
                for j in range(ST):
                    first = c != CH - 1 and j % 2 == 0
                    h, l = hh[c % 2][:, j * P:(j + 1) * P], hl[c % 2][:, j * P:(j + 1) * P]
                    pe.matmul(pD[:, j, :], h, wdh[:, c, :], start=first, stop=False, skip_group_check=True)
                    pe.matmul(pD[:, j, :], h, wdl[:, c, :], start=False, stop=False, skip_group_check=True)
                    mm = pe.matmul(pD[:, j, :], l, wdh[:, c, :], start=False, stop=(c != CH - 2),
                                   skip_group_check=True)
                mm.then_inc(dn_ps, 1)

            pe.wait_ge(w_ready, 1)
            turn(0)
            route(0)
            route_back(0)
            gate_up(0, 0)
            with pe.Fori(0, NG - 1) as s:
                for c in range(CH):
                    if c == 2:
                        turn(s + 1)
                    if c == 4:
                        route(s + 1)
                    if c == 5:
                        route_back(s + 1)
                    if c < CH - 1:
                        gate_up(s, c + 1)
                    else:
                        gate_up(s + 1, 0)
                    down(s, c)
            for c in range(CH):
                if c < CH - 1:
                    gate_up(NG - 1, c + 1)
                down(NG - 1, c)

        @block.scalar
        def _(act):
            act.wait_ge(sb["moe_in"], 48)
            act.activation(wgh[:], sb["gu"][:], ACT.Copy).then_inc(w_hi, 1)
            act.activation(wdh[:], sb["dn"][:], ACT.Copy).then_inc(w_hi, 1)

            def x_high(s):
                for j in range(ST):
                    act.wait_ge(xt_ps, ST * s + j + 3)
                    for k in range(G):
                        last = act.activation(xpart(xh, s, k, j * P, P), pX[:, k * P:(k + 1) * P], ACT.Copy)
                    last.then_inc(xh_ok, 1)

            def logits_out(s):
                act.wait_ge(l_ps, s + 1)
                act.activation(lg[:], pL[:], ACT.Copy).then_inc(l_sb, 1)

            def soft(s):
                act.wait_ge(dist, s + 1)
                act.activation(ex[:], ds_[:], ACT.Exp).then_inc(exped, 1)

            def silu(n, u):
                act.wait_ge(gu_ps, n + 1)
                act.activation(sg[u][:], pGU[u][:, 0, :], ACT.Silu).then_inc(silued, 1)

            def high(n, u):
                act.wait_ge(h_ok, n + 3)
                act.wait_ge(dn_ps, n + 1)
                act.activation(hh[u][:], hf[u][:], ACT.Copy).then_inc(hh_ok, 1)

            x_high(0)
            logits_out(0)
            soft(0)
            silu(0, 0)
            with act.Fori(0, NG - 1) as s:
                for c in range(CH):
                    if c == 2:
                        x_high(s + 1)
                    if c == 4:
                        logits_out(s + 1)
                    high(s * CH + c, c % 2)
                    if c == 6:
                        soft(s + 1)
                    silu(s * CH + c + 1, (c + 1) % 2)
            for c in range(CH):
                high((NG - 1) * CH + c, c % 2)
                if c < CH - 1:
                    silu((NG - 1) * CH + c + 1, (c + 1) % 2)

        @block.vector
        def _(dve):
            dve.sem_inc(xt_ok, 1)
            dve.sem_inc(r_step, 1)
            dve.sem_inc(h_ok, 2)
            dve.sem_inc(added, 1)
            dve.wait_ge(sb["moe_in"], 48)
            dve.memset(f32(wrh[:, :, NE:P]), 0.0)
            dve.memset(f32(wrl[:, :, NE:P]), 0.0)
            dve.tensor_copy(wrh[:, :, 0:NE], sb["rt"][:]).then_inc(w_hi, 1)
            dve.wait_ge(w_hi, 3)
            dve.tensor_tensor(wrl[:, :, 0:NE], sb["rt"][:], f32(wrh[:, :, 0:NE]), ALU.subtract)
            dve.tensor_tensor(wgl[:], sb["gu"][:], f32(wgh[:]), ALU.subtract)
            dve.tensor_tensor(wdl[:], sb["dn"][:], f32(wdh[:]), ALU.subtract).then_inc(w_ready, 1)

            def norm(s, j):
                t = ST * s + j
                dve.wait_ge(xt_ps, t + 1)
                dve.tensor_scalar(xn[j % 2][:], X[:, piece(t, D)], RS[:, bass.ds(t, 1)],
                                  NM[:, bass.ds(t, 1)], ALU.mult, ALU.add).then_inc(normed, 1)

            def x_low(s):
                for j in range(ST):
                    if j + 2 < ST:
                        norm(s, j + 2)
                    dve.wait_ge(xh_ok, ST * s + j + 1)
                    for k in range(G):
                        last = dve.tensor_tensor(xpart(xl, s, k, j * P, P), pX[:, k * P:(k + 1) * P],
                                                 f32(xpart(xh, s, k, j * P, P)), ALU.subtract)
                    last.then_inc(xt_ok, 1)

            R = 10

            def route_a(s):
                dve.wait_ge(lt_ps, s + 1)
                dve.tensor_copy(lt[:], pL[:].rearrange("p (j e) -> p j e", e=P)[:, :, 0:NE]).then_inc(r_step, 1)
                dve.wait_ge(r_step, s + 2)
                dve.tensor_reduce(top[:], lt[:], AX.X, ALU.max).then_inc(r_chain, 1)
                mine = lt[:].rearrange("p j (e a) -> p j e a", a=1).broadcast_to([P, ST, NE, NE])
                other = lt[:].rearrange("p j (a e) -> p j a e", a=1).broadcast_to([P, ST, NE, NE])
                dve.tensor_tensor(gt[:], other, mine, ALU.is_gt).then_inc(r_chain, 1)
                dve.tensor_tensor(eq[:], other, mine, ALU.is_equal).then_inc(r_chain, 1)
                dve.wait_ge(r_chain, s * R + 3)
                dve.tensor_tensor(ds_[:], lt[:], top[:].rearrange("p (j a) -> p j a", a=1).broadcast_to([P, ST, NE]),
                                  ALU.subtract).then_inc(dist, 1)
                dve.tensor_tensor(eq[:], eq[:], sb["lower"][:].rearrange("p (a i) j -> p a (i j)", a=1)
                                  .broadcast_to([P, ST, NE * NE]).rearrange("p a (i j) -> p a i j", j=NE),
                                  ALU.mult).then_inc(r_chain, 1)
                dve.wait_ge(r_chain, s * R + 4)
                dve.tensor_tensor(gt[:], gt[:], eq[:], ALU.add).then_inc(r_chain, 1)

            def route_b(s):
                dve.wait_ge(r_chain, s * R + 5)
                dve.tensor_reduce(rank[:], gt[:], AX.X, ALU.add).then_inc(r_chain, 1)
                dve.wait_ge(exped, s + 1)
                dve.tensor_reduce(sums[:, 0, :], ex[:], AX.X, ALU.add).then_inc(r_chain, 1)
                dve.wait_ge(r_chain, s * R + 7)
                dve.reciprocal(sums[:, 1, :], sums[:, 0, :]).then_inc(r_chain, 1)
                dve.scalar_tensor_tensor(ex[:], rank[:], float(TOPK), ex[:], ALU.is_lt, ALU.mult).then_inc(r_chain, 1)
                dve.wait_ge(r_chain, s * R + 9)
                dve.tensor_tensor(coef[:, bass.ds((s % 2) * (ST * NE), ST * NE)].rearrange("p (j e) -> p j e", e=NE),
                                  ex[:], sums[:, 1, :].rearrange("p (j a) -> p j a", a=1).broadcast_to([P, ST, NE]),
                                  ALU.mult).then_inc(r_chain, 1)

            def product(n, u):
                dve.wait_ge(silued, n + 1)
                dve.wait_ge(hl_ok, n + 1)
                dve.tensor_tensor(hf[u][:], pGU[u][:, 1, :], sg[u][:], ALU.mult).then_inc(h_ok, 1)

            def add(s, c):
                dve.wait_ge(dn_ps, s * CH + c + 3)
                dve.wait_ge(r_chain, (s + 1) * R)
                dve.wait_ge(added, s * (CH - 1) + (c if c < NE else NE) + 1)
                for j in range(ST):
                    xs = X[:, bass.ds((s * ST + j) * D, D)]
                    if c < NE:
                        last = dve.scalar_tensor_tensor(
                            xs, pD[:, j, :], coef[:, bass.ds((s % 2) * (ST * NE) + (j * NE + c), 1)], xs,
                            ALU.mult, ALU.add)
                    else:
                        last = dve.tensor_tensor(xs, pD[:, j, :], xs, ALU.add)
                last.then_inc(added, 1)

            def stats(s):
                hold(dve, added, (s + 1) * (CH - 1) + 1, spare[:])
                for j in range(ST):
                    last = dve.bn_stats(st[:, j, :], X[:, bass.ds((s * ST + j) * D, D)])
                last.then_inc(stated, 1)
                hold(dve, stated, 2 * s + 1, spare[:])
                for j in range(ST):
                    last = dve.bn_aggr(av[:, j, :], st[:, j, :])
                last.then_inc(stated, 1)
                dve.wait_ge(stated, 2 * s + 2)
                dve.tensor_copy(MV[:, bass.ds(s * (2 * ST), 2 * ST)], av[:].rearrange("p j a -> p (j a)"))

            norm(0, 0)
            norm(0, 1)
            x_low(0)
            route_a(0)
            route_b(0)
            product(0, 0)
            with dve.Fori(0, NG - 1) as s:
                for c in range(CH):
                    if c == 1:
                        norm(s + 1, 0)
                        norm(s + 1, 1)
                    if c == 2:
                        x_low(s + 1)
                    if c == 5:
                        route_a(s + 1)
                    if c == 7:
                        route_b(s + 1)
                    product(s * CH + c + 1, (c + 1) % 2)
                    if c != CH - 2:
                        add(s, c)
                stats(s)
            for c in range(CH):
                if c < CH - 1:
                    product((NG - 1) * CH + c + 1, (c + 1) % 2)
                if c != CH - 2:
                    add(NG - 1, c)
            stats(NG - 1)


def mlp_phase(nc, dram, sb):
    with ExitStack() as ctx:
        sem = lambda n: ctx.enter_context(nc.semaphore(n + "_m"))
        sbt = lambda n, s, d=F32: ctx.enter_context(nc.sbuf_tensor(n + "_m", s, d))
        pst = lambda n, s, d=F32: ctx.enter_context(nc.psum_tensor(n + "_m", s, d))
        (a_step, qa_ok, qat_ps, qat_sb, up_ps, up_ok, gelu_ok, e_step, power, b_step, normed, gained,
         shifted, c_step, qc_ok, qct_ps, qct_sb, down_ps, y_ok) = (sem(n) for n in (
             "a_step", "qa_ok", "qat_ps", "qat_sb", "up_ps", "up_ok", "gelu_ok", "e_step", "power",
             "b_step", "normed", "gained", "shifted", "c_step", "qc_ok", "qct_ps", "qct_sb", "down_ps",
             "y_ok"))
        stored = [sem(f"stored{u}") for u in range(2)]
        ha = [sbt(f"ha{i}", [P, D]) for i in range(2)]
        sa = [sbt(f"sa{i}", [P, 8]) for i in range(2)]
        qa = [sbt(f"qa{i}", [P, D], BF16) for i in range(2)]
        qat = [sbt(f"qat{i}", [P, G, P], BF16) for i in range(2)]
        hb = [sbt(f"hb{i}", [P, HID]) for i in range(2)]
        ge = [sbt(f"ge{i}", [P, HID]) for i in range(2)]
        hn = [sbt(f"hn{i}", [P, HID]) for i in range(2)]
        st = [sbt(f"st{i}", [P, 2, 6]) for i in range(2)]
        se = [sbt(f"se{i}", [P, 8]) for i in range(2)]
        sc = [sbt(f"sc{i}", [P, 8]) for i in range(2)]
        half = sbt("half", [P, 1])
        spare = sbt("spare", [P, 1])
        qc = [sbt(f"qc{i}", [P, HID], BF16) for i in range(2)]
        qct = [sbt(f"qct{i}", [P, KH, P], BF16) for i in range(2)]
        y = [sbt(f"y{i}", [P, D]) for i in range(2)]
        pU = [pst(f"pU{i}", [P, HID]) for i in range(2)]
        pA = pst("pA", [P, G * P], BF16)
        pC = pst("pC", [P, HID], BF16)
        pY = pst("pY", [P, 512])
        block = ctx.enter_context(nc.Block())
        X = sb["x"][:].rearrange("p t d -> p (t d)")
        MV = sb["mv"][:].rearrange("p t a -> p (t a)")
        out = dram["out"].rearrange("b s d -> (b s) d")
        A, E, BS, CS = 9, 4, 0, 7

        @block.sync
        def _(sp):
            def store(t, u):
                sp.wait_ge(y_ok, 2 * t + 3)
                sp.dma_start(out[bass.ds(t * P, P), :], y[u][:]).then_inc(stored[u], 16)
            with sp.Fori(0, T // 2) as i:
                for u in range(2):
                    store(2 * i + u, u)
            for u in range(2):
                sp.wait_ge(stored[u], 16 * (T // 2 + 1))

        @block.gpsimd
        def _(pool):
            pool.wait_ge(sb["mlp_in"], 16 * (2 + len(MLP_ROWS)))
            pool.memset(half[:], -0.5).then_inc(power, 1)
            for u in range(2):
                pool.sem_inc(stored[u], 16)

            def gain(t, u):
                pool.wait_ge(normed, t + 1)
                pool.tensor_tensor(hn[u][:], hn[u][:], sb["g2"][:], ALU.mult).then_inc(gained, 1)

            def root(t, u):
                pool.wait_ge(e_step, t * E + 3)
                pool.wait_ge(power, 1)
                pool.tensor_tensor(se[u][:, 3:4], se[u][:, 2:3], half[:], ALU.pow).then_inc(power, 1)

            def offset(t, u):
                pool.wait_ge(gained, t + 1)
                pool.tensor_tensor(hn[u][:], hn[u][:], sb["c2"][:], ALU.add).then_inc(shifted, 1)

            def step(t, u, has):
                if has(1):
                    gain(t + 1, 1 - u)
                if has(2):
                    root(t + 2, u)
                if has(1):
                    offset(t + 1, 1 - u)

            run_steps(pool, step, 3)

        @block.tensor
        def _(pe):
            def front(t, u):
                pe.wait_ge(qa_ok, t + 3)
                pe.wait_ge(qat_sb, t + 1)
                for k in range(G):
                    mm = pe.transpose(pA[:, k * P:(k + 1) * P], qa[u][:, k * P:(k + 1) * P], sb["identb"][:])
                mm.then_inc(qat_ps, 1)
                pe.wait_ge(qat_sb, t + 2)
                pe.wait_ge(up_ok, t + 1)
                for n in range(2):
                    for k in range(G):
                        mm = pe.matmul(pU[u][:, n * 512:(n + 1) * 512], qat[u][:, k, :],
                                       sb["q1"][:, k, n * 512:(n + 1) * 512], start=(k == 0), stop=(k == G - 1))
                mm.then_inc(up_ps, 1)

            def back(t, u):
                pe.wait_ge(qc_ok, t + 3)
                pe.wait_ge(qct_sb, t + 1)
                for k in range(KH):
                    mm = pe.transpose(pC[:, k * P:(k + 1) * P], qc[u][:, k * P:(k + 1) * P], sb["identb"][:])
                mm.then_inc(qct_ps, 1)

            def last(t, u):
                pe.wait_ge(qct_sb, t + 2)
                pe.wait_ge(y_ok, 2 * t + 1)
                for k in range(KH):
                    mm = pe.matmul(pY[:, 0:D], qct[u][:, k, :], sb["q2"][:, k, :], start=(k == 0), stop=(k == KH - 1))
                mm.then_inc(down_ps, 1)

            def step(t, u, has):
                if has(3):
                    front(t + 3, 1 - u)
                if has(0):
                    back(t, u)
                    last(t, u)

            run_steps(pe, step, 3)

        @block.scalar
        def _(act):
            act.sem_inc(qa_ok, 2)
            act.sem_inc(qc_ok, 2)
            act.sem_inc(qat_sb, 1)
            act.sem_inc(qct_sb, 1)

            def front(t, u):
                act.wait_ge(a_step, t * A + A)
                act.activation(qa[u][:], ha[u][:], ACT.Copy, bias=-MAGIC).then_inc(qa_ok, 1)
                act.wait_ge(qat_ps, t + 1)
                act.activation(qat[u][:].rearrange("p k n -> p (k n)"), pA[:], ACT.Copy).then_inc(qat_sb, 1)

            def middle(t, u):
                act.wait_ge(up_ok, t + 3)
                act.activation(ge[u][:], hb[u][:], ACT.Gelu).then_inc(gelu_ok, 1)

            def centre(t, u):
                act.wait_ge(e_step, t * E + E)
                act.wait_ge(qc_ok, t + 1)
                act.activation(hn[u][:], ge[u][:], ACT.Identity, scale=se[u][:, 3:4],
                               bias=se[u][:, 4:5]).then_inc(normed, 1)

            def integers(t, u):
                act.wait_ge(c_step, t * CS + CS)
                act.activation(qc[u][:], hn[u][:], ACT.Copy, bias=-MAGIC).then_inc(qc_ok, 1)

            def turned(t, u):
                act.wait_ge(qct_ps, t + 1)
                act.activation(qct[u][:].rearrange("p k n -> p (k n)"), pC[:], ACT.Copy).then_inc(qct_sb, 1)

            def step(t, u, has):
                if has(2):
                    middle(t + 2, u)
                if has(3):
                    front(t + 3, 1 - u)
                if has(0):
                    integers(t, u)
                if has(2):
                    centre(t + 2, u)
                if has(0):
                    turned(t, u)

            run_steps(act, step, 3)

        @block.vector
        def _(dve):
            dve.wait_ge(sb["mlp_in"], 16 * (2 + len(MLP_ROWS)))
            dve.sem_inc(up_ok, 2)
            dve.sem_inc(y_ok, 1)

            def quant(h, s, k, sem_, n):
                dve.tensor_reduce(s[:, 0:1], h, AX.X, ALU.max, apply_absolute_value=True).then_inc(sem_, 1)
                dve.wait_ge(sem_, n + 1)
                dve.tensor_scalar(s[:, 1:2], s[:, 0:1], 1e-5, None, ALU.max).then_inc(sem_, 1)
                dve.wait_ge(sem_, n + 2)
                dve.reciprocal(s[:, 2:3], s[:, 1:2]).then_inc(sem_, 1)
                dve.tensor_scalar(s[:, 4:5], s[:, 1:2], 1.0 / 127.0, sb["wsi"][:, k:k + 1],
                                  ALU.mult, ALU.mult).then_inc(sem_, 1)
                dve.wait_ge(sem_, n + 3)
                dve.tensor_scalar(s[:, 3:4], s[:, 2:3], 127.0, None, ALU.mult).then_inc(sem_, 1)
                dve.wait_ge(sem_, n + 5)
                dve.tensor_scalar(h, h, s[:, 3:4], 127.0, ALU.mult, ALU.min).then_inc(sem_, 1)
                dve.wait_ge(sem_, n + 6)
                dve.tensor_scalar(h, h, -128.0, MAGIC, ALU.max, ALU.add).then_inc(sem_, 1)

            def front(t, u):
                dve.wait_ge(qa_ok, t + 1)
                dve.scalar_tensor_tensor(ha[u][:], X[:, piece(t, D)], MV[:, bass.ds(t * 2, 1)], sb["g1"][:],
                                         ALU.subtract, ALU.mult).then_inc(a_step, 1)
                dve.wait_ge(a_step, t * A + 1)
                dve.scalar_tensor_tensor(ha[u][:], ha[u][:], sb["rs"][:, bass.ds(t, 1)], sb["c1"][:],
                                         ALU.mult, ALU.add).then_inc(a_step, 1)
                dve.wait_ge(a_step, t * A + 2)
                quant(ha[u][:], sa[u], 0, a_step, t * A + 2)

            def middle(t, u):
                dve.wait_ge(up_ps, t + 1)
                dve.scalar_tensor_tensor(hb[u][:], pU[u][:], sa[u][:, 4:5], sb["b1"][:],
                                         ALU.mult, ALU.add).then_inc(up_ok, 1)

            def stats(t, u):
                dve.wait_ge(gelu_ok, t + 1)
                for n in range(2):
                    last = dve.bn_stats(st[u][:, n, :], ge[u][:, n * 512:(n + 1) * 512])
                last.then_inc(e_step, 1)
                hold(dve, e_step, t * E + 1, spare[:])
                dve.bn_aggr(se[u][:, 0:2], st[u][:].rearrange("p a b -> p (a b)")).then_inc(e_step, 1)
                dve.wait_ge(e_step, t * E + 2)
                dve.tensor_scalar(se[u][:, 2:3], se[u][:, 1:2], EPS, None, ALU.add).then_inc(e_step, 1)

            def factor(t, u):
                dve.wait_ge(power, t + 2)
                dve.tensor_scalar(se[u][:, 4:5], se[u][:, 0:1], se[u][:, 3:4], -1.0, ALU.mult, ALU.mult).then_inc(e_step, 1)

            def result(t, u):
                dve.wait_ge(down_ps, t + 1)
                dve.wait_ge(stored[u], 16 * (t // 2) + 16)
                dve.scalar_tensor_tensor(y[u][:], pY[:, 0:D], sc[u][:, 4:5], sb["b2"][:],
                                         ALU.mult, ALU.add).then_inc(y_ok, 1)
                dve.wait_ge(y_ok, 2 * t + 2)
                dve.tensor_tensor(y[u][:], y[u][:], X[:, piece(t, D)], ALU.add).then_inc(y_ok, 1)

            def step(t, u, has):
                if has(2):
                    middle(t + 2, u)
                if has(3):
                    front(t + 3, 1 - u)
                if has(0):
                    dve.wait_ge(shifted, t + 1)
                    quant(hn[u][:], sc[u], 1, c_step, t * CS)
                if has(2):
                    stats(t + 2, u)
                    factor(t + 2, u)
                if has(0):
                    result(t, u)

            run_steps(dve, step, 3)


def build(nc, dram):
    with ExitStack() as ctx:
        sb = {}

        def keep(name, shape, dt=F32):
            sb[name] = ctx.enter_context(nc.sbuf_tensor(name, shape, dt))

        keep("x", [P, T, D])
        keep("mv", [P, T, 2])
        keep("rs", [P, T])
        keep("nm", [P, T])
        keep("ident", [P, P])
        keep("identb", [P, P], BF16)
        keep("ones", [P, P])
        keep("hmask", [P, HG])
        keep("kmask", [P, CK, HG])
        keep("lower", [P, NE, NE])
        keep("ctx", [P, G, B * SK])
        keep("m1", [P, T, SK], U8)
        keep("wsi", [P, 2])
        keep("q1", [P, G, HID], BF16)
        keep("q2", [P, KH, D], BF16)
        for name in ("x_in", "att_in", "moe_in", "mlp_in"):
            sb[name] = ctx.enter_context(nc.semaphore(name))
        for name in ("aw", "bqk", "bv", "bo"):
            sb[name] = [None, None]

        def attention_weights(stack, layer):
            for name, shape in (("aw", [P, G, 4 * D]), ("bqk", [P, 2, G]), ("bv", [1, D]), ("bo", [P, D])):
                sb[name][layer] = stack.enter_context(nc.sbuf_tensor(f"{name}{layer}", shape, F32))

        def attention(layer):
            with ExitStack() as att:
                sb["tag"] = f"_a{layer}"
                for part in ("Kh", "Kl"):
                    sb[part] = att.enter_context(nc.sbuf_tensor(f"{part}{layer}", [P, B * G, HG * SK], F32R))
                sb["V"] = att.enter_context(nc.sbuf_tensor(f"V{layer}", [P, B * G, CK * VW], F32))
                sb["mask"] = att.enter_context(nc.sbuf_tensor(f"mask{layer}", [P, T if layer else TB, SK], F32))
                norm_and_keys_phase(nc, dram, sb, layer)
                attention_phase(nc, sb, layer)

        attention_weights(ctx, 1)
        moe = ExitStack()
        for name, shape in (("gu", [P, G, CH * 2 * P]), ("dn", [P, CH, D]), ("rt", [P, G, NE])):
            sb[name] = moe.enter_context(nc.sbuf_tensor(name, shape, F32))
        with ExitStack() as first:
            attention_weights(first, 0)
            sb["m0"] = first.enter_context(nc.sbuf_tensor("m0", [P, TB, SK], F32))
            with ExitStack() as raw:
                sb["w1"] = raw.enter_context(nc.sbuf_tensor("w1", [P, G, HID], F32))
                sb["w2"] = raw.enter_context(nc.sbuf_tensor("w2", [P, KH, D], F32))
                load_phase(nc, dram, sb)
            attention(0)
        sb["tag"] = "_f0"
        norm_and_keys_phase(nc, dram, sb, None)
        moe_phase(nc, sb)
        moe.close()
        for name, w in zip(MLP_ROWS, (D, D, HID, HID, HID, D)):
            keep(name, [P, w])
        attention(1)
        sb["tag"] = "_f1"
        norm_and_keys_phase(nc, dram, sb, None)
        mlp_phase(nc, dram, sb)


def kernel(**inputs):
    import concourse.bacc as bacc
    from concourse.bass_utils import run_bass_kernel_spmd

    a = {k: np.asarray(v) for k, v in inputs.items()}
    keep = {
        "x": a["x"],
        "ctx": a["ctx_1024"].transpose(2, 0, 1).reshape(D, B * SK),
        "m0": a["mask_1x1xSxS2_fk1"].reshape(SQ, SK),
        "m1": a["mask_Bx1xSxS2_bk1"].reshape(B * SQ, SK),
        "aw0": np.concatenate([a[f"L0_xattn_w{n}_w"] for n in "qkvo"], axis=1),
        "aw1": np.concatenate([a[f"L1_xattn_W{n}"].T for n in "qkvo"], axis=1),
        "bqk0": np.concatenate([a["L0_xattn_wq_b"], a["L0_xattn_wk_b"]]).reshape(2 * G, P).T,
        "bqk1": np.concatenate([a["L1_xattn_bq"], a["L1_xattn_bk"]]).reshape(2 * G, P).T,
        "bv0": a["L0_xattn_wv_b"].reshape(1, D), "bv1": a["L1_xattn_bv"].reshape(1, D),
        "bo0": a["L0_xattn_wo_b"].reshape(1, D), "bo1": a["L1_xattn_bo"].reshape(1, D),
        "rt": a["L0_ffn_router"],
        "gu": np.stack([
            np.concatenate([a["L0_ffn_experts_gate"].transpose(1, 0, 2), a["L0_ffn_shared_gate"].reshape(D, DS // P, P)], axis=1),
            np.concatenate([a["L0_ffn_experts_up"].transpose(1, 0, 2), a["L0_ffn_shared_up"].reshape(D, DS // P, P)], axis=1),
        ], axis=2).reshape(D, CH * 2 * P),
        "dn": np.concatenate([a["L0_ffn_experts_down"].reshape(NE * DE, D), a["L0_ffn_shared_down"]], axis=0),
        "w1": a["L1_ffn_w1"].T, "w2": a["L1_ffn_w2"].T,
        "g1": a["L1_ffn_ln1_g"].reshape(1, D), "c1": a["L1_ffn_ln1_b"].reshape(1, D),
        "b1": a["L1_ffn_b1"].reshape(1, HID), "g2": a["L1_ffn_ln2_g"].reshape(1, HID),
        "c2": a["L1_ffn_ln2_b"].reshape(1, HID), "b2": a["L1_ffn_b2"].reshape(1, D),
    }
    nc = bacc.Bacc("TRN2", target_bir_lowering=False, num_devices=1)
    arrays, dram = {}, {}
    for name, v in keep.items():
        arrays[name + "_in"] = np.ascontiguousarray(v)
        dram[name] = nc.dram_tensor(name + "_in", v.shape, mybir.dt.from_np(v.dtype), kind="ExternalInput").ap()
    dram["out"] = nc.dram_tensor("out_x", (B, SQ, D), F32, kind="ExternalOutput").ap()
    for name in ("aw", "bqk", "bv", "bo"):
        dram[name] = [dram[name + "0"], dram[name + "1"]]
    build(nc, dram)
    return run_bass_kernel_spmd(nc, [arrays], core_ids=[0]).results[0]["out_x"]
```

```python
from contextlib import ExitStack

import numpy as np
import concourse.bass as bass
from concourse import mybir

F32 = mybir.dt.float32
F32R = mybir.dt.float32r
BF16 = mybir.dt.bfloat16
U8 = mybir.dt.uint8
U32 = mybir.dt.uint32
ALU = mybir.AluOpType
ACT = mybir.ActivationFunctionType
AX = mybir.AxisListType

P = 128
B, SQ, D = 4, 1024, 256
SK = 77
HEADS, DH = 16, 16
G = D // P
HG = HEADS // G
T = B * SQ // P
TB = SQ // P
CK = -(-HG * SK // P)
LASTK = HG * SK - (CK - 1) * P
VW = P + HG
NE, TOPK, DE, DS = 8, 2, 128, 256
CH = NE + DS // P
ST = 4
NG = T // ST
GW = ST * P
HID = 1024
KH = HID // P
MLP_ROWS = ("g1", "c1", "b1", "g2", "c2", "b2")
EPS = 1e-5
NEG = -1e9
HUGE = 3e38
MAGIC = 1.5 * 2.0 ** 23
SCORE = DH ** -0.5


def piece(t, width):
    return bass.ds(t * width, width)


def hold(dve, sem, value, spare):
    dve.wait_ge(sem, value)
    dve.memset(spare, 0.0)


def run_steps(eng, step, lead, lag=0):
    first, last = lag, T - lead
    some = lambda t: lambda k: 0 <= t + k < T
    for t in range(-lead, first):
        step(t, t % 2, some(t))
    pairs = (last - first) // 2
    with eng.Fori(0, pairs) as i:
        for u in range(2):
            step(2 * i + (first + u), (first + u) % 2, lambda k: True)
    for t in range(first + 2 * pairs, T + lag):
        step(t, t % 2, some(t))


def load_phase(nc, dram, sb):
    with ExitStack() as ctx:
        sem = lambda n: ctx.enter_context(nc.semaphore(n))
        s_c, s_m, s_bn, s_sums, s_tot, s_q, s_abs = (sem(n) for n in (
            "const_step", "lnw_step", "tile_stats", "abs_sums", "abs_total", "quant_step", "abs_row"))
        junk = ctx.enter_context(nc.sbuf_tensor("w_abs", [P, 2 * HID], F32))
        wr = ctx.enter_context(nc.sbuf_tensor("w_round", [P, 2 * HID], F32))
        rows = ctx.enter_context(nc.sbuf_tensor("w_rowsum", [P, 2], F32))
        wsc = ctx.enter_context(nc.sbuf_tensor("w_scale", [P, 2], F32))
        tot = ctx.enter_context(nc.psum_tensor("w_total", [P, 2], F32))
        st = ctx.enter_context(nc.sbuf_tensor("st0", [P, T, 6], F32))
        block = ctx.enter_context(nc.Block())

        @block.sync
        def _(sp):
            for b in range(B):
                sp.dma_start(sb["x"][:, b * TB:(b + 1) * TB, :],
                             dram["x"][b].rearrange("(t p) d -> p t d", p=P)).then_inc(sb["x_in"], 16)
            sp.dma_start(sb["w1"][:], dram["w1"].rearrange("(k p) n -> p k n", p=P)).then_inc(sb["mlp_in"], 16)
            sp.dma_start(sb["w2"][:], dram["w2"].rearrange("(k p) n -> p k n", p=P)).then_inc(sb["mlp_in"], 16)
            sp.dma_start(sb["gu"][:], dram["gu"].rearrange("(k p) n -> p k n", p=P)).then_inc(sb["moe_in"], 16)
            sp.dma_start(sb["dn"][:], dram["dn"].rearrange("(c p) n -> p c n", p=P)).then_inc(sb["moe_in"], 16)
            sp.dma_start(sb["rt"][:], dram["rt"].rearrange("(k p) n -> p k n", p=P)).then_inc(sb["moe_in"], 16)

        @block.scalar
        def _(act):
            act.dma_start(sb["ctx"][:], dram["ctx"].rearrange("(k p) n -> p k n", p=P)).then_inc(sb["att_in"], 16)
            for n in range(2):
                act.dma_start(sb["aw"][n][:], dram["aw"][n].rearrange("(k p) n -> p k n", p=P)).then_inc(sb["att_in"], 16)
                act.dma_start(sb["bqk"][n][:], dram["bqk"][n].rearrange("p (a g) -> p a g", g=G)).then_inc(sb["att_in"], 16)
                act.dma_start(sb["bv"][n][:], dram["bv"][n]).then_inc(sb["att_in"], 16)
                act.dma_start(sb["bo"][n][:], dram["bo"][n].broadcast_to([P, D])).then_inc(sb["att_in"], 16)
            act.dma_start(sb["m0"][:], dram["m0"].rearrange("(t p) k -> p t k", p=P)).then_inc(sb["att_in"], 16)
            act.dma_start(sb["m1"][:], dram["m1"].rearrange("(t p) k -> p t k", p=P)).then_inc(sb["att_in"], 16)
            act.wait_ge(sb["mlp_in"], 2 * 16)
            act.activation(junk[:], sb["w1"][:].rearrange("p k n -> p (k n)"), ACT.Abs,
                           accum_out=rows[:, 0:1]).then_inc(s_abs, 1)
            act.wait_ge(s_abs, 1)
            act.activation(junk[:], sb["w2"][:].rearrange("p k n -> p (k n)"), ACT.Abs,
                           accum_out=rows[:, 1:2]).then_inc(s_sums, 1)

        @block.gpsimd
        def _(pool):
            pool.memset(sb["ones"][:], 1.0).then_inc(s_c, 1)
            pool.memset(sb["hmask"][:], 1.0).then_inc(s_c, 1)
            pool.memset(sb["kmask"][:], 1.0).then_inc(s_c, 1)
            pool.memset(sb["ident"][:], 0.0).then_inc(s_c, 1)
            pool.memset(sb["lower"][:], 1.0).then_inc(s_c, 1)
            pool.wait_ge(s_c, 5)
            pool.affine_select(out=sb["ident"][:], in_=sb["ident"][:], compare_op=ALU.not_equal, fill=1.0,
                               base=0, pattern=[[-1, P]], channel_multiplier=1).then_inc(s_c, 1)
            pool.affine_select(out=sb["hmask"][:], in_=sb["hmask"][:], compare_op=ALU.is_ge, fill=0.0,
                               base=0, pattern=[[-DH, HG]], channel_multiplier=1).then_inc(s_c, 1)
            pool.affine_select(out=sb["kmask"][:], in_=sb["kmask"][:], compare_op=ALU.is_ge, fill=0.0,
                               base=0, pattern=[[P, CK], [-SK, HG]], channel_multiplier=1).then_inc(s_c, 1)
            pool.wait_ge(s_c, 8)
            pool.affine_select(out=sb["hmask"][:], in_=sb["hmask"][:], compare_op=ALU.is_ge, fill=0.0,
                               base=DH - 1, pattern=[[DH, HG]], channel_multiplier=-1).then_inc(s_c, 1)
            pool.affine_select(out=sb["kmask"][:], in_=sb["kmask"][:], compare_op=ALU.is_ge, fill=0.0,
                               base=SK - 1, pattern=[[-P, CK], [SK, HG]], channel_multiplier=-1).then_inc(s_c, 1)
            pool.affine_select(out=sb["lower"][:], in_=sb["lower"][:], compare_op=ALU.is_ge, fill=0.0,
                               base=-1, pattern=[[1, NE], [-1, NE]], channel_multiplier=0).then_inc(s_c, 1)

        @block.tensor
        def _(pe):
            pe.wait_ge(s_c, 11)
            pe.wait_ge(s_sums, 1)
            pe.matmul(tot[:], sb["ones"][:], rows[:], start=True, stop=True).then_inc(s_tot, 1)

        @block.vector
        def _(dve):
            for t in range(T):
                dve.wait_ge(sb["x_in"], 16 * B)
                dve.bn_stats(st[:, t, :], sb["x"][:, t, :]).then_inc(s_bn, 1)
            for t in range(T):
                dve.wait_ge(s_bn, T)
                dve.bn_aggr(sb["mv"][:, t, :], st[:, t, :])
            dve.wait_ge(s_tot, 1)
            dve.tensor_scalar(sb["wsi"][:], tot[:], 1.0 / (HID * D), 1e-5, ALU.mult, ALU.max).then_inc(s_q, 1)
            dve.wait_ge(s_q, 1)
            dve.reciprocal(wsc[:], sb["wsi"][:]).then_inc(s_q, 1)
            n = 2
            for k, (raw, out) in enumerate((("w1", "q1"), ("w2", "q2"))):
                w = sb[raw][:].rearrange("p k n -> p (k n)")
                dve.wait_ge(s_q, n)
                dve.tensor_scalar(wr[:], w, wsc[:, k:k + 1], 1.0, ALU.mult, ALU.min).then_inc(s_q, 1)
                dve.wait_ge(s_q, n + 1)
                dve.tensor_scalar(wr[:], wr[:], -1.0, MAGIC, ALU.max, ALU.add).then_inc(s_q, 1)
                dve.wait_ge(s_q, n + 2)
                dve.tensor_scalar(sb[out][:].rearrange("p k n -> p (k n)"), wr[:], -MAGIC, None,
                                  ALU.add).then_inc(s_q, 1)
                n += 3
            dve.tensor_copy(sb["identb"][:], sb["ident"][:])


def norm_and_keys_phase(nc, dram, sb, layer):
    with ExitStack() as ctx:
        sem = lambda n: ctx.enter_context(nc.semaphore(n + str(layer) + sb["tag"]))
        s_sd, s_r, s_kt, s_kc, s_kb, s_rep, s_v, s_vb, s_m, s_kp = (sem(n) for n in (
            "sd", "rstd_step", "kT_ps", "kT_sb", "kbd", "ctx_rep", "v_ps", "vbd", "mask_step", "k_parts"))
        r = ctx.enter_context(nc.sbuf_tensor("r" + sb["tag"], [P, 3, T], F32))
        if layer is not None:
            rep = ctx.enter_context(nc.sbuf_tensor("rep" + sb["tag"], [P, G, CK * P], F32))
            kt = ctx.enter_context(nc.sbuf_tensor("kt" + sb["tag"], [P, B * G, SK], F32))
            kh = ctx.enter_context(nc.sbuf_tensor("kh" + sb["tag"], [P, B * G, SK], F32R))
            kl = ctx.enter_context(nc.sbuf_tensor("kl" + sb["tag"], [P, B * G, SK], F32R))
            pk = ctx.enter_context(nc.psum_tensor("pk" + sb["tag"], [P, 512], F32))
            pv = ctx.enter_context(nc.psum_tensor("pv" + sb["tag"], [P, 2, 1024], F32))
            aw, bqk, bv = sb["aw"][layer], sb["bqk"][layer], sb["bv"][layer]
        block = ctx.enter_context(nc.Block())

        per_head = lambda ap: ap.rearrange("p (h k) -> p h k", k=SK)
        every_head = lambda ap: ap.rearrange("p (a k) -> p a k", a=1).broadcast_to([P, HG, SK])
        own_rows = sb["hmask"][:].rearrange("p (h a) -> p h a", a=1).broadcast_to([P, HG, SK])

        @block.sync
        def _(sp):
            if layer == 1:
                for name in MLP_ROWS:
                    sp.dma_start(sb[name][:], dram[name].broadcast_to(list(sb[name].shape))).then_inc(sb["mlp_in"], 16)

        @block.gpsimd
        def _(pool):
            if layer is None:
                return
            for n in range(B * G):
                pool.wait_ge(s_kp, 2 * n + 2)
                pool.tensor_tensor(per_head(sb["Kl"][:, n, :]), every_head(kl[:, n, :].bitcast(F32)), own_rows, ALU.mult)

        @block.scalar
        def _(act):
            act.wait_ge(s_r, 1)
            act.activation(r[:, 1, :], r[:, 0, :], ACT.Sqrt).then_inc(s_sd, 1)

        @block.vector
        def _(dve):
            v, s, y = r[:, 0, :], r[:, 1, :], r[:, 2, :]
            dve.tensor_scalar(v, sb["mv"][:, :, 1], EPS, None, ALU.add).then_inc(s_r, 1)
            dve.wait_ge(s_sd, 1)
            steps = [lambda: dve.reciprocal(y, s),
                     lambda: dve.tensor_tensor(s, y, y, ALU.mult),
                     lambda: dve.tensor_tensor(s, s, v, ALU.mult),
                     lambda: dve.tensor_scalar(s, s, -0.5, 1.5, ALU.mult, ALU.add),
                     lambda: dve.tensor_tensor(sb["rs"][:], y, s, ALU.mult),
                     lambda: dve.tensor_tensor(v, sb["mv"][:, :, 0], sb["rs"][:], ALU.mult),
                     lambda: dve.tensor_scalar(sb["nm"][:], v, -1.0, None, ALU.mult)]
            for n, step in enumerate(steps):
                step().then_inc(s_r, 1)
                dve.wait_ge(s_r, n + 2)
            if layer is None:
                return
            dve.wait_ge(sb["att_in"], 16 * 11)
            if layer == 0:
                dve.tensor_scalar(sb["mask"][:, 0:TB, :], sb["m0"][:], NEG, None, ALU.mult).then_inc(s_m, 1)
            else:
                dve.tensor_scalar(sb["mask"][:], sb["m1"][:], 0.0, None, ALU.is_equal).then_inc(s_m, 1)
                dve.wait_ge(s_m, 1)
                dve.tensor_scalar(sb["mask"][:], sb["mask"][:], HUGE, NEG, ALU.mult, ALU.add)
            for b in range(B):
                if b:
                    dve.wait_ge(s_v, G * b)
                for k in range(G):
                    c = sb["ctx"][:, k, b * SK:(b + 1) * SK].rearrange("p (a n) -> p a n", a=1)
                    dve.tensor_copy(rep[:, k, 0:HG * SK].rearrange("p (a n) -> p a n", n=SK),
                                    c.broadcast_to([P, HG, SK]))
                    dve.tensor_copy(rep[:, k, HG * SK:CK * P], sb["ctx"][:, k, 0:CK * P - HG * SK]).then_inc(s_rep, 1)
                for g in range(G):
                    n = b * G + g
                    dve.wait_ge(s_kt, n + 1)
                    dve.tensor_scalar(kt[:, n, :], pk[:, 0:SK], bqk[:, 1, g:g + 1], SCORE,
                                      ALU.add, ALU.mult).then_inc(s_kc, 1)
                    dve.wait_ge(s_kc, n + 1)
                    dve.tensor_copy(kh[:, n, :], kt[:, n, :]).then_inc(s_kp, 1)
                    dve.wait_ge(s_kp, 2 * n + 1)
                    dve.tensor_tensor(kl[:, n, :], kt[:, n, :], kh[:, n, :].bitcast(F32), ALU.subtract).then_inc(s_kp, 1)
                    dve.tensor_tensor(per_head(sb["Kh"][:, n, :]), every_head(kh[:, n, :].bitcast(F32)), own_rows, ALU.mult)
                    dve.wait_ge(s_v, n + 1)
                    V = sb["V"][:, n, :].rearrange("p (c w) -> p c w", w=VW)
                    dve.tensor_tensor(V[:, :, 0:P].rearrange("p c (h d) -> p c h d", d=DH),
                                      pv[:, n % 2, 0:CK * P].rearrange("p (c h d) -> p c h d", d=DH, h=HG),
                                      sb["kmask"][:].rearrange("p c (h a) -> p c h a", a=1).broadcast_to([P, CK, HG, DH]),
                                      ALU.mult)
                    dve.tensor_copy(V[:, :, P:VW], sb["kmask"][:]).then_inc(s_vb, 1)

        @block.tensor
        def _(pe):
            if layer is None:
                return
            pe.wait_ge(sb["att_in"], 16 * 11)
            for b in range(B):
                for g in range(G):
                    n = b * G + g
                    if n:
                        pe.wait_ge(s_kc, n)
                    for k in range(G):
                        mm = pe.matmul(pk[:, 0:SK], aw[:, k, D + g * P:D + (g + 1) * P],
                                       sb["ctx"][:, k, b * SK:(b + 1) * SK], start=(k == 0), stop=(k == G - 1))
                    mm.then_inc(s_kt, 1)
                    pe.wait_ge(s_rep, G * (b + 1))
                    if n >= 2:
                        pe.wait_ge(s_vb, n - 1)
                    for c in range(CK):
                        out = pv[:, n % 2, c * P:(c + 1) * P]
                        for k in range(G):
                            pe.matmul(out, rep[:, k, c * P:(c + 1) * P],
                                      aw[:, k, 2 * D + g * P:2 * D + (g + 1) * P], start=(k == 0), stop=False)
                        mm = pe.matmul(out, sb["ones"][0:1, :], bv[0:1, g * P:(g + 1) * P], start=False, stop=True)
                    mm.then_inc(s_v, 1)


def attention_phase(nc, sb, layer):
    tag = sb["tag"]
    with ExitStack() as ctx:
        sem = lambda n: ctx.enter_context(nc.semaphore(n + tag))
        sbt = lambda n, s, d=F32: ctx.enter_context(nc.sbuf_tensor(n + tag, s, d))
        pst = lambda n, s, d=F32: ctx.enter_context(nc.psum_tensor(n + tag, s, d))
        (normed, xt_ps, xt_sb, q_ps, q_hi, q_sb, scored, masked, maxed, shifted, exped, pt_ps, pt_sb,
         weighed, recips, o_norm, ot_ps, ot_sb, projected, biased, added, stated) = (sem(n) for n in (
             "normed", "xt_ps", "xt_sb", "q_ps", "q_hi", "q_sb", "scored", "masked", "maxed", "shifted",
             "exped", "pt_ps", "pt_sb", "weighed", "recips", "o_norm", "ot_ps", "ot_sb", "projected",
             "biased", "added", "stated"))
        NS = HG * SK
        HS = NS // 2
        xn = [sbt(f"xn{i}", [P, D]) for i in range(2)]
        xt = [sbt(f"xt{i}", [P, D]) for i in range(2)]
        qh = [sbt(f"qh{i}", [P, D], F32R) for i in range(2)]
        ql = [sbt(f"ql{i}", [P, D], F32R) for i in range(2)]
        sm = [sbt(f"sm{i}", [P, G * NS]) for i in range(2)]
        mx = [sbt(f"mx{i}", [P, HEADS]) for i in range(2)]
        pr = [sbt(f"pr{i}", [P, G * NS]) for i in range(2)]
        pt = sbt("pt", [P, G * CK, P])
        rc = [sbt(f"rc{i}", [P, HEADS]) for i in range(2)]
        on = sbt("on", [P, D])
        ot = sbt("ot", [P, D])
        st = sbt("st", [P, 6])
        av = sbt("av", [P, 2])
        spare = sbt("spare", [P, 1])
        pA = pst("pA", [P, 512])
        pO = pst("pO", [P, 512])
        pS = pst("pS", [P, 4, 512])
        pT = pst("pT", [P, 2, 512])
        block = ctx.enter_context(nc.Block())
        aw, bqk, bo = sb["aw"][layer], sb["bqk"][layer], sb["bo"][layer]
        X = sb["x"][:].rearrange("p t d -> p (t d)")
        RS, NM = sb["rs"], sb["nm"]
        MV = sb["mv"][:].rearrange("p t a -> p (t a)")
        KH = sb["Kh"][:].rearrange("p n w -> p (n w)")
        KL = sb["Kl"][:].rearrange("p n w -> p (n w)")
        VB = sb["V"][:].rearrange("p n w -> p (n w)")
        MASK = sb["mask"][:].rearrange("p t k -> p (t k)")
        chunks = [(g, c) for g in range(G) for c in range(CK)]
        J = -(-len(chunks) // 4)
        rows = lambda c: LASTK if c == CK - 1 else P
        heads = lambda ap: ap.rearrange("p (h k) -> p h k", k=SK)
        banked = lambda ap: ap.rearrange("p (b h k) -> p b h k", b=4, k=SK)

        @block.gpsimd
        def _(pool):
            def shift(t, u):
                pool.wait_ge(maxed, t + 1)
                pool.tensor_tensor(heads(sm[u][:]), heads(sm[u][:]),
                                   mx[u][:].rearrange("p (h a) -> p h a", a=1).broadcast_to([P, HEADS, SK]),
                                   ALU.subtract).then_inc(shifted, 1)

            def bias(t):
                pool.wait_ge(normed, t + 1)
                pool.tensor_tensor(X[:, piece(t, D)], X[:, piece(t, D)], bo[:], ALU.add).then_inc(biased, 1)

            def step(t, u, has):
                if has(1):
                    shift(t + 1, 1 - u)
                    bias(t + 1)

            run_steps(pool, step, 3, 1)

        @block.tensor
        def _(pe):
            pe.sem_inc(xt_ps, 2)
            pe.sem_inc(pt_ps, 2 * J)
            pe.sem_inc(weighed, 1)

            def turn_x(t, u):
                pe.wait_ge(normed, t + 1)
                pe.wait_ge(q_sb, t + 1)
                for k in range(G):
                    mm = pe.transpose(pA[:, k * P:(k + 1) * P], xn[u][:, k * P:(k + 1) * P], sb["ident"][:])
                mm.then_inc(xt_ps, 1)

            def queries(t, u):
                pe.wait_ge(xt_sb, t + 1)
                for g in range(G):
                    for k in range(G):
                        mm = pe.matmul(pA[:, D + g * P:D + (g + 1) * P], aw[:, k, g * P:(g + 1) * P],
                                       xt[u][:, k * P:(k + 1) * P], start=(k == 0), stop=(k == G - 1))
                mm.then_inc(q_ps, 1)

            def scores(t, u):
                pe.wait_ge(q_sb, t + 2)
                pe.wait_ge(masked, t + 1)
                keys = (t // TB) * (G * NS)
                for b in range(4):
                    g = b // 2
                    h, l = qh[u][:, g * P:(g + 1) * P], ql[u][:, g * P:(g + 1) * P]
                    at = bass.ds(keys + b * HS, HS)
                    pe.matmul(pS[:, b, 0:HS], h, KH[:, at], start=True, stop=False)
                    pe.matmul(pS[:, b, 0:HS], h, KL[:, at], start=False, stop=False)
                    mm = pe.matmul(pS[:, b, 0:HS], l, KH[:, at], start=False, stop=True)
                mm.then_inc(scored, 1)

            def turn_p(t, u, j):
                if j == 0:
                    pe.wait_ge(exped, t + 3)
                pe.wait_ge(pt_sb, J * t + j + 1)
                for n in range(4 * j, min(4 * j + 4, len(chunks))):
                    g, c = chunks[n]
                    at = g * NS + c * P
                    mm = pe.transpose(pT[0:rows(c), (u + j) % 2, (n % 4) * P:(n % 4 + 1) * P],
                                      pr[u][:, at:at + rows(c)], sb["ident"][:])
                mm.then_inc(pt_ps, 1)

            def weigh(t, u, g):
                if g == 0:
                    pe.wait_ge(added, t + 1)
                vals = (t // TB) * (G * CK * VW)
                for n, (half, c) in enumerate(chunks):
                    if half != g:
                        continue
                    if c == 0 or n % 4 == 0:
                        pe.wait_ge(pt_sb, J * t + n // 4 + 3)
                    mm = pe.matmul(pO[:, g * VW:(g + 1) * VW], pt[0:rows(c), n, :],
                                   VB[0:rows(c), bass.ds(vals + n * VW, VW)],
                                   start=(c == 0), stop=(c == CK - 1))
                if g == G - 1:
                    mm.then_inc(weighed, 1)

            def turn_o(t):
                pe.wait_ge(o_norm, t + 1)
                for k in range(G):
                    mm = pe.transpose(pO[:, k * P:(k + 1) * P], on[:, k * P:(k + 1) * P], sb["ident"][:])
                mm.then_inc(ot_ps, 1)

            def project(t):
                pe.wait_ge(ot_sb, t + 1)
                for k in range(G):
                    mm = pe.matmul(pO[:, 0:D], ot[:, k * P:(k + 1) * P], aw[:, k, 3 * D:4 * D],
                                   start=(k == 0), stop=(k == G - 1))
                mm.then_inc(projected, 1)

            def step(t, u, has):
                if has(0):
                    turn_p(t, u, 0)
                if has(-1):
                    project(t - 1)
                if has(0):
                    turn_p(t, u, 1)
                    turn_p(t, u, 2)
                if has(2):
                    turn_x(t + 2, u)
                if has(0):
                    weigh(t, u, 0)
                if has(2):
                    queries(t + 2, u)
                if has(0):
                    weigh(t, u, 1)
                if has(2):
                    scores(t + 2, u)
                if has(0):
                    turn_o(t)

            run_steps(pe, step, 3, 1)

        @block.scalar
        def _(act):
            act.sem_inc(pt_sb, 2)
            act.sem_inc(exped, 2)

            def xt_out(t, u):
                act.wait_ge(xt_ps, t + 3)
                act.activation(xt[u][:], pA[:, 0:D], ACT.Copy).then_inc(xt_sb, 1)

            def exp(t, u):
                act.wait_ge(shifted, t + 1)
                act.wait_ge(pt_ps, J * (t + 1))
                act.activation(pr[u][:], sm[u][:], ACT.Exp).then_inc(exped, 1)

            def pt_out(t, u, j):
                if j == 0:
                    act.wait_ge(weighed, t + 1)
                act.wait_ge(pt_ps, J * t + j + 1 + 2 * J)
                runs = []
                for n in range(4 * j, min(4 * j + 4, len(chunks))):
                    r = rows(chunks[n][1])
                    if runs and r == P and runs[-1][2] == P and runs[-1][1] == n:
                        runs[-1][1] = n + 1
                    else:
                        runs.append([n, n + 1, r])
                for lo, hi, r in runs:
                    last = act.activation(pt[0:r, lo:hi, :].rearrange("p n t -> p (n t)"),
                                          pT[0:r, (u + j) % 2, (lo % 4) * P:(lo % 4 + hi - lo) * P], ACT.Copy)
                last.then_inc(pt_sb, 1)

            def ot_out(t):
                act.wait_ge(ot_ps, t + 1)
                act.activation(ot[:], pO[:, 0:D], ACT.Copy).then_inc(ot_sb, 1)

            def step(t, u, has):
                if has(0):
                    for j in range(J):
                        pt_out(t, u, j)
                if has(2):
                    xt_out(t + 2, u)
                if has(1):
                    exp(t + 1, 1 - u)
                if has(0):
                    ot_out(t)

            run_steps(act, step, 3, 1)

        @block.vector
        def _(dve):
            dve.sem_inc(q_sb, 1)
            dve.sem_inc(masked, 1)
            dve.sem_inc(added, 1)

            def norm(t, u):
                dve.wait_ge(xt_ps, t + 1)
                dve.tensor_scalar(xn[u][:], X[:, piece(t, D)], RS[:, bass.ds(t, 1)], NM[:, bass.ds(t, 1)],
                                  ALU.mult, ALU.add).then_inc(normed, 1)

            def q_out(t, u):
                dve.wait_ge(q_ps, t + 1)
                dve.tensor_tensor(qh[u][:].rearrange("p (g n) -> p g n", g=G),
                                  pA[:, D:2 * D].rearrange("p (g n) -> p g n", g=G),
                                  bqk[:, 0, :].rearrange("p (g a) -> p g a", a=1).broadcast_to([P, G, P]),
                                  ALU.add).then_inc(q_hi, 1)
                dve.wait_ge(q_hi, t + 1)
                for g in range(G):
                    half = slice(g * P, (g + 1) * P)
                    last = dve.scalar_tensor_tensor(ql[u][:, half], pA[:, D + g * P:D + (g + 1) * P],
                                                    bqk[:, 0, g:g + 1], qh[u][:, half].bitcast(F32),
                                                    ALU.add, ALU.subtract)
                last.then_inc(q_sb, 1)

            def mask(t, u):
                dve.wait_ge(scored, t + 1)
                dve.wait_ge(exped, t + 1)
                at = (t % TB) * SK if layer == 0 else t * SK
                every = MASK[:, bass.ds(at, SK)].rearrange("p (a b k) -> p a b k", a=1, b=1)
                dve.tensor_tensor(banked(sm[u][:]), pS[:, :, 0:HS].rearrange("p b (h k) -> p b h k", k=SK),
                                  every.broadcast_to([P, 4, HEADS // 4, SK]),
                                  ALU.add if layer == 0 else ALU.min).then_inc(masked, 1)

            def largest(t, u):
                dve.wait_ge(masked, t + 2)
                dve.tensor_reduce(mx[u][:], heads(sm[u][:]), AX.X, ALU.max).then_inc(maxed, 1)

            def normalise(t, u):
                dve.wait_ge(weighed, t + 2)
                o = pO[:, 0:G * VW].rearrange("p (g w) -> p g w", g=G)
                dve.reciprocal(rc[u][:].rearrange("p (g h) -> p g h", g=G), o[:, :, P:VW]).then_inc(recips, 1)
                dve.wait_ge(recips, t + 1)
                dve.tensor_tensor(on[:].rearrange("p (g h d) -> p g h d", g=G, d=DH),
                                  o[:, :, 0:P].rearrange("p g (h d) -> p g h d", d=DH),
                                  rc[u][:].rearrange("p (g h a) -> p g h a", g=G, a=1).broadcast_to([P, G, HG, DH]),
                                  ALU.mult).then_inc(o_norm, 1)

            def add(t):
                dve.wait_ge(projected, t + 1)
                dve.wait_ge(biased, t + 1)
                dve.tensor_tensor(X[:, piece(t, D)], pO[:, 0:D], X[:, piece(t, D)], ALU.add).then_inc(added, 1)

            def stats(t):
                hold(dve, added, t + 2, spare[:])
                dve.bn_stats(st[:], X[:, piece(t, D)]).then_inc(stated, 1)
                hold(dve, stated, 2 * t + 1, spare[:])
                dve.bn_aggr(av[:], st[:]).then_inc(stated, 1)
                dve.wait_ge(stated, 2 * t + 2)
                dve.tensor_copy(MV[:, piece(t, 2)], av[:])

            def step(t, u, has):
                if has(-1):
                    add(t - 1)
                if has(1):
                    largest(t + 1, 1 - u)
                if has(-1):
                    stats(t - 1)
                if has(3):
                    norm(t + 3, 1 - u)
                if has(2):
                    q_out(t + 2, u)
                if has(0):
                    normalise(t, u)
                if has(2):
                    mask(t + 2, u)

            run_steps(dve, step, 3, 1)


def moe_phase(nc, sb):
    tag = sb["tag"]
    with ExitStack() as ctx:
        sem = lambda n: ctx.enter_context(nc.semaphore(n + tag))
        sbt = lambda n, s, d=F32: ctx.enter_context(nc.sbuf_tensor(n + tag, s, d))
        pst = lambda n, s, d=F32: ctx.enter_context(nc.psum_tensor(n + tag, s, d))
        (w_hi, w_ready, normed, xt_ps, xh_ok, xt_ok, l_ps, l_sb, lt_ps, r_step, dist, exped, r_chain,
         gu_ps, silued, h_ok, hh_ok, hl_ok, dn_ps, added, stated) = (sem(n) for n in (
             "w_hi", "w_ready", "normed", "xt_ps", "xh_ok", "xt_ok", "l_ps", "l_sb", "lt_ps", "r_step",
             "dist", "exped", "r_chain", "gu_ps", "silued", "h_ok", "hh_ok", "hl_ok", "dn_ps", "added",
             "stated"))
        NGU = CH * 2 * P
        wgh, wgl = sbt("wgh", [P, G, NGU], F32R), sbt("wgl", [P, G, NGU], F32R)
        wdh, wdl = sbt("wdh", [P, CH, D], F32R), sbt("wdl", [P, CH, D], F32R)
        wrh, wrl = sbt("wrh", [P, G, P], F32R), sbt("wrl", [P, G, P], F32R)
        xn = [sbt(f"xn{i}", [P, D]) for i in range(2)]
        xh, xl = sbt("xh", [P, 2 * G * GW], F32R), sbt("xl", [P, 2 * G * GW], F32R)
        lg = sbt("lg", [P, GW])
        lt = sbt("lt", [P, ST, NE])
        top = sbt("top", [P, ST])
        rank = sbt("rank", [P, ST, NE])
        gt, eq = sbt("gt", [P, ST, NE, NE]), sbt("eq", [P, ST, NE, NE])
        ds_ = sbt("ds", [P, ST, NE])
        ex = sbt("ex", [P, ST, NE])
        en = sbt("en", [P, ST, NE])
        sums = sbt("sums", [P, 2, ST])
        coef = sbt("coef", [P, 2 * ST * NE])
        sg = [sbt(f"sg{i}", [P, GW]) for i in range(2)]
        hf = [sbt(f"hf{i}", [P, GW]) for i in range(2)]
        hh = [sbt(f"hh{i}", [P, GW], F32R) for i in range(2)]
        hl = [sbt(f"hl{i}", [P, GW], F32R) for i in range(2)]
        st = sbt("st", [P, ST, 6])
        av = sbt("av", [P, ST, 2])
        spare = sbt("spare", [P, 1])
        pGU = [pst(f"pGU{i}", [P, 2, GW]) for i in range(2)]
        pD = pst("pD", [P, ST, D])
        pX = pst("pX", [P, 512])
        pL = pst("pL", [P, 512])
        block = ctx.enter_context(nc.Block())
        X = sb["x"][:].rearrange("p t d -> p (t d)")
        MV = sb["mv"][:].rearrange("p t a -> p (t a)")
        RS, NM = sb["rs"], sb["nm"]
        f32 = lambda ap: ap.bitcast(F32)
        TURNS, ROUTE = (1, 2, 3, 4), 6

        def xpart(buf, s, k, lo=0, n=GW):
            return buf[:, bass.ds((s % 2) * (G * GW) + (k * GW + lo), n)]

        @block.gpsimd
        def _(pool):
            def low(n, u):
                pool.wait_ge(hh_ok, n + 1)
                pool.wait_ge(dn_ps, n + 1)
                pool.tensor_tensor(hl[u][:], hf[u][:], f32(hh[u][:]), ALU.subtract).then_inc(hl_ok, 1)

            pool.sem_inc(hl_ok, 2)
            with pool.Fori(0, NG) as s:
                for c in range(CH):
                    low(s * CH + c, c % 2)

        @block.tensor
        def _(pe):
            pe.sem_inc(xt_ps, 2)
            pe.sem_inc(dn_ps, 2)

            def turn(s, j):
                t = ST * s + j
                pe.wait_ge(normed, t + 1)
                pe.wait_ge(xt_ok, t + 1)
                for k in range(G):
                    mm = pe.transpose(pX[:, k * P:(k + 1) * P], xn[j % 2][:, k * P:(k + 1) * P], sb["ident"][:])
                mm.then_inc(xt_ps, 1)

            def three(out, ah, al, bh, bl, first, last):
                pe.matmul(out, ah, bh, start=first, stop=False)
                pe.matmul(out, ah, bl, start=False, stop=False)
                return pe.matmul(out, al, bh, start=False, stop=last)

            def route(s):
                pe.wait_ge(xt_ok, ST * s + ST + 1)
                pe.wait_ge(r_step, s + 1)
                for k in range(G):
                    mm = three(pL[:], wrh[:, k, :], wrl[:, k, :], xpart(xh, s, k), xpart(xl, s, k),
                               k == 0, k == G - 1)
                mm.then_inc(l_ps, 1)

            def route_back(s):
                pe.wait_ge(l_sb, s + 1)
                for j in range(ST):
                    mm = pe.transpose(pL[:, j * P:(j + 1) * P], lg[:, j * P:(j + 1) * P], sb["ident"][:])
                mm.then_inc(lt_ps, 1)

            def gate_up(s, c):
                n = s * CH + c
                pe.wait_ge(xt_ok, ST * s + ST + 1)
                pe.wait_ge(h_ok, n + 1)
                for a in range(2):
                    at = (2 * c + a) * P
                    for k in range(G):
                        mm = three(pGU[c % 2][:, a, :], wgh[:, k, at:at + P], wgl[:, k, at:at + P],
                                   xpart(xh, s, k), xpart(xl, s, k), k == 0, k == G - 1)
                mm.then_inc(gu_ps, 1)

            def down(s, c):
                n = s * CH + c
                pe.wait_ge(hl_ok, n + 3)
                if c != CH - 1:
                    pe.wait_ge(added, s * (CH - 1) + c + 1)
                for j in range(ST):
                    first = c != CH - 1 and j % 2 == 0
                    h, l = hh[c % 2][:, j * P:(j + 1) * P], hl[c % 2][:, j * P:(j + 1) * P]
                    pe.matmul(pD[:, j, :], h, wdh[:, c, :], start=first, stop=False, skip_group_check=True)
                    pe.matmul(pD[:, j, :], h, wdl[:, c, :], start=False, stop=False, skip_group_check=True)
                    mm = pe.matmul(pD[:, j, :], l, wdh[:, c, :], start=False, stop=(c != CH - 2),
                                   skip_group_check=True)
                mm.then_inc(dn_ps, 1)

            pe.wait_ge(w_ready, 1)
            for j in range(ST):
                turn(0, j)
            route(0)
            route_back(0)
            gate_up(0, 0)
            with pe.Fori(0, NG - 1) as s:
                for c in range(CH):
                    if c in TURNS:
                        turn(s + 1, TURNS.index(c))
                    if c == ROUTE:
                        route(s + 1)
                    if c == ROUTE + 1:
                        route_back(s + 1)
                    if c < CH - 1:
                        gate_up(s, c + 1)
                    else:
                        gate_up(s + 1, 0)
                    down(s, c)
            for c in range(CH):
                if c < CH - 1:
                    gate_up(NG - 1, c + 1)
                down(NG - 1, c)

        @block.scalar
        def _(act):
            act.wait_ge(sb["moe_in"], 48)
            act.activation(wgh[:], sb["gu"][:], ACT.Copy).then_inc(w_hi, 1)
            act.activation(wdh[:], sb["dn"][:], ACT.Copy).then_inc(w_hi, 1)

            def x_high(s, j):
                act.wait_ge(xt_ps, ST * s + j + 3)
                for k in range(G):
                    last = act.activation(xpart(xh, s, k, j * P, P), pX[:, k * P:(k + 1) * P], ACT.Copy)
                last.then_inc(xh_ok, 1)

            def logits_out(s):
                act.wait_ge(l_ps, s + 1)
                act.activation(lg[:], pL[:], ACT.Copy).then_inc(l_sb, 1)

            def soft(s):
                act.wait_ge(dist, s + 1)
                act.activation(ex[:], ds_[:], ACT.Silu)
                act.activation(en[:], ds_[:], ACT.Silu, scale=-1.0).then_inc(exped, 1)

            def silu(n, u):
                act.wait_ge(gu_ps, n + 1)
                act.activation(sg[u][:], pGU[u][:, 0, :], ACT.Silu).then_inc(silued, 1)

            def high(n, u):
                act.wait_ge(h_ok, n + 3)
                act.wait_ge(dn_ps, n + 1)
                act.activation(hh[u][:], hf[u][:], ACT.Copy).then_inc(hh_ok, 1)

            for j in range(ST):
                x_high(0, j)
            logits_out(0)
            soft(0)
            silu(0, 0)
            with act.Fori(0, NG - 1) as s:
                for c in range(CH):
                    high(s * CH + c, c % 2)
                    if c in TURNS:
                        x_high(s + 1, TURNS.index(c))
                    if c == ROUTE:
                        logits_out(s + 1)
                    if c == ROUTE + 2:
                        soft(s + 1)
                    silu(s * CH + c + 1, (c + 1) % 2)
            for c in range(CH):
                high((NG - 1) * CH + c, c % 2)
                if c < CH - 1:
                    silu((NG - 1) * CH + c + 1, (c + 1) % 2)

        @block.vector
        def _(dve):
            dve.sem_inc(xt_ok, 1)
            dve.sem_inc(r_step, 1)
            dve.sem_inc(h_ok, 2)
            dve.sem_inc(added, 1)
            dve.wait_ge(sb["moe_in"], 48)
            dve.memset(f32(wrh[:, :, NE:P]), 0.0)
            dve.memset(f32(wrl[:, :, NE:P]), 0.0)
            dve.tensor_copy(wrh[:, :, 0:NE], sb["rt"][:]).then_inc(w_hi, 1)
            dve.wait_ge(w_hi, 3)
            dve.tensor_tensor(wrl[:, :, 0:NE], sb["rt"][:], f32(wrh[:, :, 0:NE]), ALU.subtract)
            dve.tensor_tensor(wgl[:], sb["gu"][:], f32(wgh[:]), ALU.subtract)
            dve.tensor_tensor(wdl[:], sb["dn"][:], f32(wdh[:]), ALU.subtract).then_inc(w_ready, 1)

            def norm(s, j):
                t = ST * s + j
                dve.wait_ge(xt_ps, t + 1)
                dve.tensor_scalar(xn[j % 2][:], X[:, piece(t, D)], RS[:, bass.ds(t, 1)],
                                  NM[:, bass.ds(t, 1)], ALU.mult, ALU.add).then_inc(normed, 1)

            def x_low(s, j):
                dve.wait_ge(xh_ok, ST * s + j + 1)
                for k in range(G):
                    last = dve.tensor_tensor(xpart(xl, s, k, j * P, P), pX[:, k * P:(k + 1) * P],
                                             f32(xpart(xh, s, k, j * P, P)), ALU.subtract)
                last.then_inc(xt_ok, 1)

            R = 12

            def route_a(s):
                dve.wait_ge(lt_ps, s + 1)
                dve.tensor_copy(lt[:], pL[:].rearrange("p (j e) -> p j e", e=P)[:, :, 0:NE]).then_inc(r_step, 1)
                dve.wait_ge(r_step, s + 2)
                dve.tensor_reduce(top[:], lt[:], AX.X, ALU.max).then_inc(r_chain, 1)
                mine = lt[:].rearrange("p j (e a) -> p j e a", a=1).broadcast_to([P, ST, NE, NE])
                other = lt[:].rearrange("p j (a e) -> p j a e", a=1).broadcast_to([P, ST, NE, NE])
                dve.tensor_tensor(gt[:], other, mine, ALU.is_gt).then_inc(r_chain, 1)
                dve.tensor_tensor(eq[:], other, mine, ALU.is_equal).then_inc(r_chain, 1)
                dve.wait_ge(r_chain, s * R + 3)
                dve.scalar_tensor_tensor(ds_[:], lt[:], -1.0,
                                         top[:].rearrange("p (j a) -> p j a", a=1).broadcast_to([P, ST, NE]),
                                         ALU.add, ALU.subtract).then_inc(dist, 1)
                dve.tensor_tensor(eq[:], eq[:], sb["lower"][:].rearrange("p (a i) j -> p a (i j)", a=1)
                                  .broadcast_to([P, ST, NE * NE]).rearrange("p a (i j) -> p a i j", j=NE),
                                  ALU.mult).then_inc(r_chain, 1)
                dve.wait_ge(r_chain, s * R + 4)
                dve.tensor_tensor(gt[:], gt[:], eq[:], ALU.add).then_inc(r_chain, 1)

            def route_b(s):
                dve.wait_ge(r_chain, s * R + 5)
                dve.tensor_reduce(rank[:], gt[:], AX.X, ALU.add).then_inc(r_chain, 1)
                dve.wait_ge(exped, s + 1)
                dve.reciprocal(en[:], en[:]).then_inc(r_chain, 1)
                dve.wait_ge(r_chain, s * R + 7)
                dve.tensor_tensor(ex[:], ex[:], en[:], ALU.mult).then_inc(r_chain, 1)
                dve.wait_ge(r_chain, s * R + 8)
                dve.tensor_reduce(sums[:, 0, :], ex[:], AX.X, ALU.add).then_inc(r_chain, 1)
                dve.wait_ge(r_chain, s * R + 9)
                dve.reciprocal(sums[:, 1, :], sums[:, 0, :]).then_inc(r_chain, 1)
                dve.scalar_tensor_tensor(ex[:], rank[:], float(TOPK), ex[:], ALU.is_lt, ALU.mult).then_inc(r_chain, 1)
                dve.wait_ge(r_chain, s * R + 11)
                dve.tensor_tensor(coef[:, bass.ds((s % 2) * (ST * NE), ST * NE)].rearrange("p (j e) -> p j e", e=NE),
                                  ex[:], sums[:, 1, :].rearrange("p (j a) -> p j a", a=1).broadcast_to([P, ST, NE]),
                                  ALU.mult).then_inc(r_chain, 1)

            def product(n, u):
                dve.wait_ge(silued, n + 1)
                dve.wait_ge(hl_ok, n + 1)
                dve.tensor_tensor(hf[u][:], pGU[u][:, 1, :], sg[u][:], ALU.mult).then_inc(h_ok, 1)

            def add(s, c):
                dve.wait_ge(dn_ps, s * CH + c + 3)
                dve.wait_ge(r_chain, (s + 1) * R)
                dve.wait_ge(added, s * (CH - 1) + (c if c < NE else NE) + 1)
                for j in range(ST):
                    xs = X[:, bass.ds((s * ST + j) * D, D)]
                    if c < NE:
                        last = dve.scalar_tensor_tensor(
                            xs, pD[:, j, :], coef[:, bass.ds((s % 2) * (ST * NE) + (j * NE + c), 1)], xs,
                            ALU.mult, ALU.add)
                    else:
                        last = dve.tensor_tensor(xs, pD[:, j, :], xs, ALU.add)
                last.then_inc(added, 1)

            def stats(s):
                hold(dve, added, (s + 1) * (CH - 1) + 1, spare[:])
                for j in range(ST):
                    last = dve.bn_stats(st[:, j, :], X[:, bass.ds((s * ST + j) * D, D)])
                last.then_inc(stated, 1)
                hold(dve, stated, 2 * s + 1, spare[:])
                for j in range(ST):
                    last = dve.bn_aggr(av[:, j, :], st[:, j, :])
                last.then_inc(stated, 1)
                dve.wait_ge(stated, 2 * s + 2)
                dve.tensor_copy(MV[:, bass.ds(s * (2 * ST), 2 * ST)], av[:].rearrange("p j a -> p (j a)"))

            def group(s, first):
                for c in range(CH):
                    if c in TURNS:
                        x_low(s + 1, TURNS.index(c))
                    if c + 1 in TURNS:
                        norm(s + 1, TURNS.index(c + 1))
                    if c == ROUTE + 3:
                        route_b(s + 1)
                    product(s * CH + c + 1, (c + 1) % 2)
                    if c == ROUTE + 1:
                        route_a(s + 1)
                    if c != CH - 2:
                        add(s, c)
                    elif not first:
                        stats(s - 1)

            norm(0, 0)
            norm(0, 1)
            for j in range(ST):
                x_low(0, j)
                if j + 2 < ST:
                    norm(0, j + 2)
            route_a(0)
            route_b(0)
            product(0, 0)
            group(0, True)
            with dve.Fori(1, NG - 1) as s:
                group(s, False)
            for c in range(CH):
                if c < CH - 1:
                    product((NG - 1) * CH + c + 1, (c + 1) % 2)
                if c != CH - 2:
                    add(NG - 1, c)
                else:
                    stats(NG - 2)
            stats(NG - 1)


def mlp_phase(nc, dram, sb):
    with ExitStack() as ctx:
        sem = lambda n: ctx.enter_context(nc.semaphore(n + "_m"))
        sbt = lambda n, s, d=F32: ctx.enter_context(nc.sbuf_tensor(n + "_m", s, d))
        pst = lambda n, s, d=F32: ctx.enter_context(nc.psum_tensor(n + "_m", s, d))
        (x_normed, x_affine, biased, a_step, qa_ok, qat_ps, qat_sb, up_ps, up_ok, gelu_ok, e_step, half_ok,
         rooted, normed, gained, shifted, c_step, qc_ok, qct_ps, qct_sb, down_ps, y_ok) = (sem(n) for n in (
             "x_normed", "x_affine", "biased", "a_step", "qa_ok", "qat_ps", "qat_sb", "up_ps", "up_ok",
             "gelu_ok", "e_step", "half_ok", "rooted", "normed", "gained", "shifted", "c_step", "qc_ok",
             "qct_ps", "qct_sb", "down_ps", "y_ok"))
        stored = sem("stored")
        ha = [sbt(f"ha{i}", [P, D]) for i in range(2)]
        sa = [sbt(f"sa{i}", [P, 8]) for i in range(2)]
        qa = [sbt(f"qa{i}", [P, D], BF16) for i in range(2)]
        qat = [sbt(f"qat{i}", [P, G, P], BF16) for i in range(2)]
        hb = [sbt(f"hb{i}", [P, HID]) for i in range(2)]
        ge = [sbt(f"ge{i}", [P, HID]) for i in range(2)]
        hn = [sbt(f"hn{i}", [P, HID]) for i in range(2)]
        st = [sbt(f"st{i}", [P, 2, 6]) for i in range(2)]
        se = [sbt(f"se{i}", [P, 8]) for i in range(2)]
        sc = [sbt(f"sc{i}", [P, 8]) for i in range(2)]
        half = sbt("half", [P, 1])
        spare = sbt("spare", [P, 1])
        qc = [sbt(f"qc{i}", [P, HID], BF16) for i in range(2)]
        qct = [sbt(f"qct{i}", [P, KH, P], BF16) for i in range(2)]
        pU = [pst(f"pU{i}", [P, HID]) for i in range(2)]
        pA = pst("pA", [P, G * P], BF16)
        pC = pst("pC", [P, HID], BF16)
        pY = pst("pY", [P, 512])
        block = ctx.enter_context(nc.Block())
        X = sb["x"][:].rearrange("p t d -> p (t d)")
        out = dram["out"].rearrange("b s d -> (b s) d")
        A, E, C = 6, 4, 6
        LEAD, LAG = 5, 1

        @block.sync
        def _(sp):
            with sp.Fori(0, T) as t:
                sp.wait_ge(y_ok, t + 2)
                sp.dma_start(out[bass.ds(t * P, P), :], X[:, piece(t, D)]).then_inc(stored, 16)
            sp.wait_ge(stored, 16 * T)

        @block.gpsimd
        def _(pool):
            pool.wait_ge(sb["mlp_in"], 16 * (2 + len(MLP_ROWS)))
            pool.memset(half[:], -0.5).then_inc(half_ok, 1)
            pool.wait_ge(half_ok, 1)

            def x_gain(t, u):
                pool.wait_ge(x_normed, t + 1)
                pool.tensor_tensor(ha[u][:], ha[u][:], sb["g1"][:], ALU.mult).then_inc(x_affine, 1)

            def x_offset(t, u):
                pool.wait_ge(x_affine, 2 * t + 1)
                pool.tensor_tensor(ha[u][:], ha[u][:], sb["c1"][:], ALU.add).then_inc(x_affine, 1)

            def bias(t):
                pool.wait_ge(x_normed, t + 1)
                pool.tensor_tensor(X[:, piece(t, D)], X[:, piece(t, D)], sb["b2"][:], ALU.add).then_inc(biased, 1)

            def gain(t, u):
                pool.wait_ge(normed, t + 1)
                pool.tensor_tensor(hn[u][:], hn[u][:], sb["g2"][:], ALU.mult).then_inc(gained, 1)

            def root(t, u):
                pool.wait_ge(e_step, t * E + 3)
                pool.tensor_tensor(se[u][:, 3:4], se[u][:, 2:3], half[:], ALU.pow).then_inc(rooted, 1)

            def offset(t, u):
                pool.wait_ge(gained, t + 1)
                pool.tensor_tensor(hn[u][:], hn[u][:], sb["c2"][:], ALU.add).then_inc(shifted, 1)

            def step(t, u, has):
                if has(4):
                    x_gain(t + 4, u)
                if has(4):
                    x_offset(t + 4, u)
                if has(1):
                    gain(t + 1, 1 - u)
                if has(2):
                    root(t + 2, u)
                if has(1):
                    offset(t + 1, 1 - u)
                if has(4):
                    bias(t + 4)

            run_steps(pool, step, LEAD, LAG)

        @block.tensor
        def _(pe):
            def turn_x(t, u):
                pe.wait_ge(qa_ok, t + 3)
                pe.wait_ge(qat_sb, t + 1)
                for k in range(G):
                    mm = pe.transpose(pA[:, k * P:(k + 1) * P], qa[u][:, k * P:(k + 1) * P], sb["identb"][:])
                mm.then_inc(qat_ps, 1)

            def up(t, u):
                pe.wait_ge(qat_sb, t + 2)
                pe.wait_ge(up_ok, t + 1)
                for n in range(2):
                    for k in range(G):
                        mm = pe.matmul(pU[u][:, n * 512:(n + 1) * 512], qat[u][:, k, :],
                                       sb["q1"][:, k, n * 512:(n + 1) * 512], start=(k == 0), stop=(k == G - 1))
                mm.then_inc(up_ps, 1)

            def turn_h(t, u):
                pe.wait_ge(qc_ok, t + 3)
                pe.wait_ge(qct_sb, t + 1)
                for k in range(KH):
                    mm = pe.transpose(pC[:, k * P:(k + 1) * P], qc[u][:, k * P:(k + 1) * P], sb["identb"][:])
                mm.then_inc(qct_ps, 1)

            def down(t, u):
                pe.wait_ge(qct_sb, t + 2)
                pe.wait_ge(y_ok, t + 1)
                for k in range(KH):
                    mm = pe.matmul(pY[:, 0:D], qct[u][:, k, :], sb["q2"][:, k, :], start=(k == 0), stop=(k == KH - 1))
                mm.then_inc(down_ps, 1)

            def step(t, u, has):
                if has(3):
                    turn_x(t + 3, 1 - u)
                if has(3):
                    up(t + 3, 1 - u)
                if has(-1):
                    down(t - 1, 1 - u)
                if has(0):
                    turn_h(t, u)

            run_steps(pe, step, LEAD, LAG)

        @block.scalar
        def _(act):
            act.sem_inc(qa_ok, 2)
            act.sem_inc(qc_ok, 2)
            act.sem_inc(qat_sb, 1)
            act.sem_inc(qct_sb, 1)

            def x_norm(t, u):
                act.wait_ge(qa_ok, t + 1)
                act.activation(ha[u][:], X[:, piece(t, D)], ACT.Identity, scale=sb["rs"][:, bass.ds(t, 1)],
                               bias=sb["nm"][:, bass.ds(t, 1)]).then_inc(x_normed, 1)

            def x_integers(t, u):
                act.wait_ge(a_step, t * A + A)
                act.wait_ge(qat_ps, t + 1)
                act.activation(qa[u][:], ha[u][:], ACT.Copy, bias=-MAGIC).then_inc(qa_ok, 1)

            def x_turned(t, u):
                act.wait_ge(qat_ps, t + 3)
                act.wait_ge(up_ps, t + 1)
                act.activation(qat[u][:].rearrange("p k n -> p (k n)"), pA[:], ACT.Copy).then_inc(qat_sb, 1)

            def gelu(t, u):
                act.wait_ge(up_ok, t + 3)
                act.activation(ge[u][:], hb[u][:], ACT.Gelu).then_inc(gelu_ok, 1)

            def h_norm(t, u):
                act.wait_ge(e_step, t * E + E)
                act.wait_ge(qc_ok, t + 1)
                act.activation(hn[u][:], ge[u][:], ACT.Identity, scale=se[u][:, 3:4],
                               bias=se[u][:, 4:5]).then_inc(normed, 1)

            def h_integers(t, u):
                act.wait_ge(c_step, t * C + C)
                act.activation(qc[u][:], hn[u][:], ACT.Copy, bias=-MAGIC).then_inc(qc_ok, 1)

            def h_turned(t, u):
                act.wait_ge(qct_ps, t + 1)
                act.activation(qct[u][:].rearrange("p k n -> p (k n)"), pC[:], ACT.Copy).then_inc(qct_sb, 1)

            def step(t, u, has):
                if has(-1):
                    h_turned(t - 1, 1 - u)
                if has(3):
                    x_integers(t + 3, 1 - u)
                if has(5):
                    x_norm(t + 5, 1 - u)
                if has(3):
                    x_turned(t + 3, 1 - u)
                if has(0):
                    h_integers(t, u)
                if has(3):
                    gelu(t + 3, 1 - u)
                if has(2):
                    h_norm(t + 2, u)

            run_steps(act, step, LEAD, LAG)

        @block.vector
        def _(dve):
            dve.wait_ge(sb["mlp_in"], 16 * (2 + len(MLP_ROWS)))
            dve.sem_inc(up_ok, 2)
            dve.sem_inc(y_ok, 1)
            dve.sem_inc(qat_ps, 2)
            dve.sem_inc(up_ps, 2)

            def scales(sides):
                for h, s, k, sem_, n in sides:
                    dve.tensor_reduce(s[:, 0:1], h, AX.X, ALU.max, apply_absolute_value=True).then_inc(sem_, 1)
                for h, s, k, sem_, n in sides:
                    dve.wait_ge(sem_, n + 1)
                    dve.tensor_scalar(s[:, 1:2], s[:, 0:1], 1e-5, None, ALU.max).then_inc(sem_, 1)
                for h, s, k, sem_, n in sides:
                    dve.wait_ge(sem_, n + 2)
                    dve.reciprocal(s[:, 2:3], s[:, 1:2]).then_inc(sem_, 1)
                for h, s, k, sem_, n in sides:
                    dve.wait_ge(sem_, n + 3)
                    dve.tensor_scalar(s[:, 3:4], s[:, 2:3], 127.0, None, ALU.mult).then_inc(sem_, 1)
                for h, s, k, sem_, n in sides:
                    dve.tensor_scalar(s[:, 4:5], s[:, 1:2], 1.0 / 127.0, sb["wsi"][:, k:k + 1],
                                      ALU.mult, ALU.mult).then_inc(sem_, 1)

            def round_up(side):
                h, s, k, sem_, n = side
                dve.wait_ge(sem_, n + 5)
                dve.tensor_scalar(h, h, s[:, 3:4], MAGIC, ALU.mult, ALU.add).then_inc(sem_, 1)

            def hidden(t, u):
                dve.wait_ge(up_ps, t + 3)
                dve.scalar_tensor_tensor(hb[u][:], pU[u][:], sa[u][:, 4:5], sb["b1"][:],
                                         ALU.mult, ALU.add).then_inc(up_ok, 1)

            def stats(t, u):
                dve.wait_ge(gelu_ok, t + 1)
                for n in range(2):
                    last = dve.bn_stats(st[u][:, n, :], ge[u][:, n * 512:(n + 1) * 512])
                last.then_inc(e_step, 1)
                hold(dve, e_step, t * E + 1, spare[:])
                dve.bn_aggr(se[u][:, 0:2], st[u][:].rearrange("p a b -> p (a b)")).then_inc(e_step, 1)
                dve.wait_ge(e_step, t * E + 2)
                dve.tensor_scalar(se[u][:, 2:3], se[u][:, 1:2], EPS, None, ALU.add).then_inc(e_step, 1)

            def factor(t, u):
                dve.wait_ge(rooted, t + 1)
                dve.tensor_scalar(se[u][:, 4:5], se[u][:, 0:1], se[u][:, 3:4], -1.0, ALU.mult, ALU.mult).then_inc(e_step, 1)

            def result(t, u):
                dve.wait_ge(down_ps, t + 1)
                dve.wait_ge(biased, t + 1)
                dve.scalar_tensor_tensor(X[:, piece(t, D)], pY[:, 0:D], sc[u][:, 4:5], X[:, piece(t, D)],
                                         ALU.mult, ALU.add).then_inc(y_ok, 1)

            def step(t, u, has):
                sides = []
                if has(2):
                    stats(t + 2, u)
                if has(0):
                    dve.wait_ge(shifted, t + 1)
                    sides.append((hn[u][:], sc[u], 1, c_step, t * C))
                if has(4):
                    dve.wait_ge(x_affine, 2 * (t + 4) + 2)
                    sides.append((ha[u][:], sa[u], 0, a_step, (t + 4) * A))
                scales(sides)
                if has(0):
                    round_up(sides[0])
                if has(2):
                    factor(t + 2, u)
                if has(3):
                    hidden(t + 3, 1 - u)
                if has(4):
                    round_up(sides[-1])
                if has(-1):
                    result(t - 1, 1 - u)

            run_steps(dve, step, LEAD, LAG)


def build(nc, dram):
    with ExitStack() as ctx:
        sb = {}

        def keep(name, shape, dt=F32):
            sb[name] = ctx.enter_context(nc.sbuf_tensor(name, shape, dt))

        keep("x", [P, T, D])
        keep("mv", [P, T, 2])
        keep("rs", [P, T])
        keep("nm", [P, T])
        keep("ident", [P, P])
        keep("identb", [P, P], BF16)
        keep("ones", [P, P])
        keep("hmask", [P, HG])
        keep("kmask", [P, CK, HG])
        keep("lower", [P, NE, NE])
        keep("ctx", [P, G, B * SK])
        keep("m1", [P, T, SK], U8)
        keep("wsi", [P, 2])
        keep("q1", [P, G, HID], BF16)
        keep("q2", [P, KH, D], BF16)
        for name in ("x_in", "att_in", "moe_in", "mlp_in"):
            sb[name] = ctx.enter_context(nc.semaphore(name))
        for name in ("aw", "bqk", "bv", "bo"):
            sb[name] = [None, None]

        def attention_weights(stack, layer):
            for name, shape in (("aw", [P, G, 4 * D]), ("bqk", [P, 2, G]), ("bv", [1, D]), ("bo", [P, D])):
                sb[name][layer] = stack.enter_context(nc.sbuf_tensor(f"{name}{layer}", shape, F32))

        def attention(layer):
            with ExitStack() as att:
                sb["tag"] = f"_a{layer}"
                for part in ("Kh", "Kl"):
                    sb[part] = att.enter_context(nc.sbuf_tensor(f"{part}{layer}", [P, B * G, HG * SK], F32R))
                sb["V"] = att.enter_context(nc.sbuf_tensor(f"V{layer}", [P, B * G, CK * VW], F32))
                sb["mask"] = att.enter_context(nc.sbuf_tensor(f"mask{layer}", [P, T if layer else TB, SK], F32))
                norm_and_keys_phase(nc, dram, sb, layer)
                attention_phase(nc, sb, layer)

        attention_weights(ctx, 1)
        moe = ExitStack()
        for name, shape in (("gu", [P, G, CH * 2 * P]), ("dn", [P, CH, D]), ("rt", [P, G, NE])):
            sb[name] = moe.enter_context(nc.sbuf_tensor(name, shape, F32))
        with ExitStack() as first:
            attention_weights(first, 0)
            sb["m0"] = first.enter_context(nc.sbuf_tensor("m0", [P, TB, SK], F32))
            with ExitStack() as raw:
                sb["w1"] = raw.enter_context(nc.sbuf_tensor("w1", [P, G, HID], F32))
                sb["w2"] = raw.enter_context(nc.sbuf_tensor("w2", [P, KH, D], F32))
                load_phase(nc, dram, sb)
            attention(0)
        sb["tag"] = "_f0"
        norm_and_keys_phase(nc, dram, sb, None)
        moe_phase(nc, sb)
        moe.close()
        for name, w in zip(MLP_ROWS, (D, D, HID, HID, HID, D)):
            keep(name, [P, w])
        attention(1)
        sb["tag"] = "_f1"
        norm_and_keys_phase(nc, dram, sb, None)
        mlp_phase(nc, dram, sb)


def kernel(**inputs):
    import concourse.bacc as bacc
    from concourse.bass_utils import run_bass_kernel_spmd

    a = {k: np.asarray(v) for k, v in inputs.items()}
    keep = {
        "x": a["x"],
        "ctx": a["ctx_1024"].transpose(2, 0, 1).reshape(D, B * SK),
        "m0": a["mask_1x1xSxS2_fk1"].reshape(SQ, SK),
        "m1": a["mask_Bx1xSxS2_bk1"].reshape(B * SQ, SK),
        "aw0": np.concatenate([a[f"L0_xattn_w{n}_w"] for n in "qkvo"], axis=1),
        "aw1": np.concatenate([a[f"L1_xattn_W{n}"].T for n in "qkvo"], axis=1),
        "bqk0": np.concatenate([a["L0_xattn_wq_b"], a["L0_xattn_wk_b"]]).reshape(2 * G, P).T,
        "bqk1": np.concatenate([a["L1_xattn_bq"], a["L1_xattn_bk"]]).reshape(2 * G, P).T,
        "bv0": a["L0_xattn_wv_b"].reshape(1, D), "bv1": a["L1_xattn_bv"].reshape(1, D),
        "bo0": a["L0_xattn_wo_b"].reshape(1, D), "bo1": a["L1_xattn_bo"].reshape(1, D),
        "rt": a["L0_ffn_router"],
        "gu": np.stack([
            np.concatenate([a["L0_ffn_experts_gate"].transpose(1, 0, 2), a["L0_ffn_shared_gate"].reshape(D, DS // P, P)], axis=1),
            np.concatenate([a["L0_ffn_experts_up"].transpose(1, 0, 2), a["L0_ffn_shared_up"].reshape(D, DS // P, P)], axis=1),
        ], axis=2).reshape(D, CH * 2 * P),
        "dn": np.concatenate([a["L0_ffn_experts_down"].reshape(NE * DE, D), a["L0_ffn_shared_down"]], axis=0),
        "w1": a["L1_ffn_w1"].T, "w2": a["L1_ffn_w2"].T,
        "g1": a["L1_ffn_ln1_g"].reshape(1, D), "c1": a["L1_ffn_ln1_b"].reshape(1, D),
        "b1": a["L1_ffn_b1"].reshape(1, HID), "g2": a["L1_ffn_ln2_g"].reshape(1, HID),
        "c2": a["L1_ffn_ln2_b"].reshape(1, HID), "b2": a["L1_ffn_b2"].reshape(1, D),
    }
    nc = bacc.Bacc("TRN2", target_bir_lowering=False, num_devices=1)
    arrays, dram = {}, {}
    for name, v in keep.items():
        arrays[name + "_in"] = np.ascontiguousarray(v)
        dram[name] = nc.dram_tensor(name + "_in", v.shape, mybir.dt.from_np(v.dtype), kind="ExternalInput").ap()
    dram["out"] = nc.dram_tensor("out_x", (B, SQ, D), F32, kind="ExternalOutput").ap()
    for name in ("aw", "bqk", "bv", "bo"):
        dram[name] = [dram[name + "0"], dram[name + "1"]]
    build(nc, dram)
    return run_bass_kernel_spmd(nc, [arrays], core_ids=[0]).results[0]["out_x"]
```

```python
from contextlib import ExitStack

import numpy as np
import concourse.bass as bass
from concourse import mybir

F32 = mybir.dt.float32
F32R = mybir.dt.float32r
BF16 = mybir.dt.bfloat16
U8 = mybir.dt.uint8
ALU = mybir.AluOpType
ACT = mybir.ActivationFunctionType
AX = mybir.AxisListType

P = 128
B, SQ, D = 4, 1024, 256
SK = 77
HEADS, DH = 16, 16
G = D // P
HG = HEADS // G
T = B * SQ // P
TB = SQ // P
CK = -(-HG * SK // P)
LASTK = HG * SK - (CK - 1) * P
VW = P + HG
NE, TOPK, DE, DS = 8, 2, 128, 256
CH = NE + DS // P
ST = 4
NG = T // ST
GW = ST * P
HID = 1024
KH = HID // P
MLP_ROWS = ("g1", "c1", "b1", "g2", "c2", "b2")
EPS = 1e-5
NEG = -1e9
HUGE = 3e38
MAGIC = 1.5 * 2.0 ** 23
SCORE = DH ** -0.5


def piece(t, width):
    return bass.ds(t * width, width)


def hold(dve, sem, value, spare):
    dve.wait_ge(sem, value)
    dve.memset(spare, 0.0)


def run_steps(eng, step, lead, lag=0):
    first, last = lag, T - lead
    some = lambda t: lambda k: 0 <= t + k < T
    for t in range(-lead, first):
        step(t, t % 2, some(t))
    pairs = (last - first) // 2
    with eng.Fori(0, pairs) as i:
        for u in range(2):
            step(2 * i + (first + u), (first + u) % 2, lambda k: True)
    for t in range(first + 2 * pairs, T + lag):
        step(t, t % 2, some(t))


NORM_STEPS = 8


def norm_variance(dve, sb, r, s_r):
    dve.tensor_scalar(r[:, 0, :], sb["mv"][:, :, 1], EPS, None, ALU.add).then_inc(s_r, 1)


def norm_root(act, r, s_r, s_sd):
    act.wait_ge(s_r, 1)
    act.activation(r[:, 1, :], r[:, 0, :], ACT.Sqrt).then_inc(s_sd, 1)


def norm_factors(dve, sb, r, s_r, s_sd):
    v, s, y = r[:, 0, :], r[:, 1, :], r[:, 2, :]
    dve.wait_ge(s_sd, 1)
    steps = [lambda: dve.reciprocal(y, s),
             lambda: dve.tensor_tensor(s, y, y, ALU.mult),
             lambda: dve.tensor_tensor(s, s, v, ALU.mult),
             lambda: dve.tensor_scalar(s, s, -0.5, 1.5, ALU.mult, ALU.add),
             lambda: dve.tensor_tensor(sb["rs"][:], y, s, ALU.mult),
             lambda: dve.tensor_tensor(v, sb["mv"][:, :, 0], sb["rs"][:], ALU.mult),
             lambda: dve.tensor_scalar(sb["nm"][:], v, -1.0, None, ALU.mult)]
    for n, step in enumerate(steps):
        step().then_inc(s_r, 1)
        dve.wait_ge(s_r, n + 2)


def load_phase(nc, dram, sb):
    with ExitStack() as ctx:
        s_c = ctx.enter_context(nc.semaphore("const_step"))
        block = ctx.enter_context(nc.Block())

        rows = lambda ap: ap.rearrange("(k p) n -> p k n", p=P)

        @block.sync
        def _(sp):
            sp.dma_start(sb["ctx"][:], rows(dram["ctx"])).then_inc(sb["att_in"][0], 16)
            sp.dma_start(sb["aw"][0][:], rows(dram["aw"][0])).then_inc(sb["att_in"][0], 16)
            for b in range(B):
                sp.dma_start(sb["x"][:, b * TB:(b + 1) * TB, :],
                             dram["x"][b].rearrange("(t p) d -> p t d", p=P)).then_inc(sb["x_in"][b], 16)
            sp.dma_start(sb["gu"][:], rows(dram["gu"])).then_inc(sb["moe_in"], 16)
            sp.dma_start(sb["dn"][:], rows(dram["dn"])).then_inc(sb["moe_in"], 16)
            sp.dma_start(sb["rt"][:], rows(dram["rt"])).then_inc(sb["moe_in"], 16)
            sp.dma_start(sb["aw"][1][:], rows(dram["aw"][1])).then_inc(sb["att_in"][1], 16)
            sp.dma_start(sb["m1"][:], rows(dram["m1"])).then_inc(sb["att_in"][1], 16)

        @block.scalar
        def _(act):
            for n in range(2):
                done = sb["att_in"][n]
                act.dma_start(sb["bqkv"][n][:], dram["bqkv"][n].rearrange("p (a g) -> p a g", g=G)).then_inc(done, 16)
                act.dma_start(sb["bo"][n][:], dram["bo"][n].broadcast_to([P, D])).then_inc(done, 16)
                if n == 0:
                    act.dma_start(sb["m0"][:], rows(dram["m0"])).then_inc(done, 16)

        @block.gpsimd
        def _(pool):
            pool.memset(sb["ones"][:], 1.0).then_inc(s_c, 1)
            pool.memset(sb["hmask"][:], 1.0).then_inc(s_c, 1)
            pool.memset(sb["kmask"][:], 1.0).then_inc(s_c, 1)
            pool.memset(sb["ident"][:], 0.0).then_inc(s_c, 1)
            pool.memset(sb["lower"][:], 1.0).then_inc(s_c, 1)
            pool.wait_ge(s_c, 5)
            pool.affine_select(out=sb["ident"][:], in_=sb["ident"][:], compare_op=ALU.not_equal, fill=1.0,
                               base=0, pattern=[[-1, P]], channel_multiplier=1).then_inc(s_c, 1)
            pool.affine_select(out=sb["hmask"][:], in_=sb["hmask"][:], compare_op=ALU.is_ge, fill=0.0,
                               base=0, pattern=[[-DH, HG]], channel_multiplier=1).then_inc(s_c, 1)
            pool.affine_select(out=sb["kmask"][:], in_=sb["kmask"][:], compare_op=ALU.is_ge, fill=0.0,
                               base=0, pattern=[[P, CK], [-SK, HG]], channel_multiplier=1).then_inc(s_c, 1)
            pool.wait_ge(s_c, 8)
            pool.affine_select(out=sb["hmask"][:], in_=sb["hmask"][:], compare_op=ALU.is_ge, fill=0.0,
                               base=DH - 1, pattern=[[DH, HG]], channel_multiplier=-1).then_inc(s_c, 1)
            pool.affine_select(out=sb["kmask"][:], in_=sb["kmask"][:], compare_op=ALU.is_ge, fill=0.0,
                               base=SK - 1, pattern=[[-P, CK], [SK, HG]], channel_multiplier=-1).then_inc(s_c, 1)
            pool.affine_select(out=sb["lower"][:], in_=sb["lower"][:], compare_op=ALU.is_ge, fill=0.0,
                               base=-1, pattern=[[1, NE], [-1, NE]], channel_multiplier=0)


def norm_and_keys_phase(nc, dram, sb, layer):
    with ExitStack() as ctx:
        sem = lambda n: ctx.enter_context(nc.semaphore(n + str(layer) + sb["tag"]))
        sbt = lambda n, s, d=F32: ctx.enter_context(nc.sbuf_tensor(n + sb["tag"], s, d))
        s_sd, s_r = sem("sd"), sem("rstd_step")
        r = sbt("r", [P, 3, T])
        if layer == 0:
            s_bn = sem("tile_stats")
            st = sbt("tile_st", [P, T, 6])
        if layer == 1:
            s_abs, s_tot, s_q, s_clip = (sem(n) for n in ("abs_sums", "abs_total", "quant_step", "clipped"))
            rows = sbt("w_rowsum", [P, 2])
            wsc = sbt("w_scale", [P, 2])
        s_kt, s_kc, s_rep, s_v, s_vb, s_m, s_kp, s_bvb, s_bo = (sem(n) for n in (
            "kT_ps", "kT_sb", "ctx_rep", "v_ps", "vbd", "mask_step", "k_parts", "bv_cols", "bo_ps"))
        rep = [sbt(f"rep{i}", [P, G, CK * P]) for i in range(2)]
        kt = sbt("kt", [P, G, B * SK])
        kh = sbt("kh", [P, G, B * SK], F32R)
        kl = sbt("kl", [P, G, B * SK], F32R)
        bvb = sbt("bvb", [P, G, P])
        pst = lambda n, s: ctx.enter_context(nc.psum_tensor(n + sb["tag"], s, F32))
        pk = pst("pk", [P, G, 512])
        pv = pst("pv", [P, 2, 3 * 512])
        po = pk[:, G - 1, :]
        aw, bqkv, bo = sb["aw"][layer], sb["bqkv"][layer], sb["bo"][layer]
        arrived = lambda eng: eng.wait_ge(sb["att_in"][layer], 16 * (5 if layer == 0 else 4))
        block = ctx.enter_context(nc.Block())

        per_head = lambda ap: ap.rearrange("p (h k) -> p h k", k=SK)
        every_head = lambda ap: ap.rearrange("p (a k) -> p a k", a=1).broadcast_to([P, HG, SK])
        own_rows = sb["hmask"][:].rearrange("p (h a) -> p h a", a=1).broadcast_to([P, HG, SK])
        of_batch = lambda part, b, g: every_head(part[:, g, b * SK:(b + 1) * SK].bitcast(F32))
        raw = lambda n: sb[("w1", "w2")[n]][:].rearrange("p k n -> p (k n)")
        rounded = lambda n: sb[("q1", "q2")[n]][:].rearrange("p k n -> p (k n)")

        @block.sync
        def _(sp):
            if layer == 1:
                for name in ("w1", "w2"):
                    sp.dma_start(sb[name][:], dram[name].rearrange("(k p) n -> p k n", p=P)).then_inc(sb["w_in"], 16)
                for name in MLP_ROWS:
                    sp.dma_start(sb[name][:], dram[name].broadcast_to(list(sb[name].shape))).then_inc(sb["mlp_in"], 16)

        @block.gpsimd
        def _(pool):
            pool.wait_ge(s_kp, 2 * G)
            for b in range(B):
                for g in range(G):
                    pool.tensor_tensor(per_head(sb["Kl"][:, b * G + g, :]), of_batch(kl, b, g), own_rows, ALU.mult)
                    if g:
                        pool.tensor_tensor(per_head(sb["Kh"][:, b * G + g, :]), of_batch(kh, b, g), own_rows, ALU.mult)

        @block.scalar
        def _(act):
            if layer == 1:
                norm_root(act, r, s_r, s_sd)
            arrived(act)
            for b in range(B):
                if b >= 2:
                    act.wait_ge(s_v, b - 1)
                for k in range(G):
                    c = sb["ctx"][:, k, b * SK:(b + 1) * SK].rearrange("p (a n) -> p a n", a=1)
                    act.activation(rep[b % 2][:, k, 0:HG * SK].rearrange("p (a n) -> p a n", n=SK),
                                   c.broadcast_to([P, HG, SK]), ACT.Copy)
                    act.activation(rep[b % 2][:, k, HG * SK:CK * P], sb["ctx"][:, k, 0:CK * P - HG * SK],
                                   ACT.Copy).then_inc(s_rep, 1)
                if layer == 1 and b == 1:
                    act.wait_ge(sb["w_in"], 2 * 16)
                    for n in range(2):
                        act.activation(rounded(n), raw(n), ACT.Abs, accum_out=rows[:, n:n + 1]).then_inc(s_abs, 1)
            if layer == 0:
                norm_root(act, r, s_r, s_sd)
            else:
                for n in range(2):
                    act.wait_ge(s_abs, 2)
                    act.wait_ge(s_clip, n + 1)
                    act.activation(rounded(n), raw(n), ACT.Copy, bias=-MAGIC)

        @block.vector
        def _(dve):
            def keys():
                for g in range(G):
                    dve.wait_ge(s_kt, g + 1)
                    dve.tensor_scalar(kt[:, g, :], pk[:, g, 0:B * SK], bqkv[:, 1, g:g + 1], SCORE,
                                      ALU.add, ALU.mult).then_inc(s_kc, 1)
                for g in range(G):
                    dve.wait_ge(s_kc, g + 1)
                    dve.tensor_copy(kh[:, g, :], kt[:, g, :]).then_inc(s_kp, 1)
                    dve.wait_ge(s_kp, 2 * g + 1)
                    dve.tensor_tensor(kl[:, g, :], kt[:, g, :], kh[:, g, :].bitcast(F32), ALU.subtract).then_inc(s_kp, 1)

            def values(b):
                dve.tensor_tensor(per_head(sb["Kh"][:, b * G, :]), of_batch(kh, b, 0), own_rows, ALU.mult)
                dve.wait_ge(s_v, b + 1)
                own_pairs = sb["kmask"][:].rearrange("p c (h a) -> p c h a", a=1).broadcast_to([P, CK, HG, DH])
                for g in range(G):
                    V = sb["V"][:, b * G + g, :].rearrange("p (c w) -> p c w", w=VW)
                    v = pv[:, b % 2, 0:CK * D].rearrange("p (c w) -> p c w", w=D)[:, :, g * P:(g + 1) * P]
                    last = dve.tensor_tensor(V[:, :, 0:P].rearrange("p c (h d) -> p c h d", d=DH),
                                             v.rearrange("p c (h d) -> p c h d", d=DH), own_pairs, ALU.mult)
                last.then_inc(s_vb, 1)

            def weights():
                dve.wait_ge(s_tot, 1)
                dve.tensor_scalar(sb["wsi"][:], po[:, 0:2], 1.0 / (HID * D), 1e-5, ALU.mult, ALU.max).then_inc(s_q, 1)
                dve.wait_ge(s_q, 1)
                dve.reciprocal(wsc[:], sb["wsi"][:]).then_inc(s_q, 1)
                dve.wait_ge(s_q, 2)
                for n in range(2):
                    dve.tensor_scalar(raw(n), raw(n), wsc[:, n:n + 1], 1.0, ALU.mult, ALU.min).then_inc(s_q, 1)
                for n in range(2):
                    dve.wait_ge(s_q, 3 + n)
                    dve.tensor_scalar(raw(n), raw(n), -1.0, MAGIC, ALU.max, ALU.add).then_inc(s_clip, 1)
                dve.tensor_copy(sb["identb"][:], sb["ident"][:])

            def stats(b):
                dve.wait_ge(sb["x_in"][b], 16)
                for t in range(b * TB, (b + 1) * TB):
                    last = dve.bn_stats(st[:, t, :], sb["x"][:, t, :])
                last.then_inc(s_bn, 1)

            if layer == 1:
                norm_variance(dve, sb, r, s_r)
            arrived(dve)
            for k in range(G):
                last = dve.tensor_scalar(bvb[:, k, :], sb["ones"][:], bqkv[:, 2, k:k + 1], None, ALU.mult)
            last.then_inc(s_bvb, 1)
            dve.wait_ge(s_bo, 1)
            dve.tensor_tensor(bo[:], bo[:], po[:, 0:D], ALU.add).then_inc(s_bo, 1)
            if layer == 0:
                dve.tensor_scalar(sb["mask"][:, 0:TB, :], sb["m0"][:], NEG, None, ALU.mult).then_inc(s_m, 1)
            else:
                dve.tensor_scalar(sb["mask"][:], sb["m1"][:], 0.0, None, ALU.is_equal).then_inc(s_m, 1)
                dve.wait_ge(s_m, 1)
                dve.tensor_scalar(sb["mask"][:], sb["mask"][:], HUGE, NEG, ALU.mult, ALU.add)
            for n in range(B * G):
                V = sb["V"][:, n, :].rearrange("p (c w) -> p c w", w=VW)
                dve.tensor_copy(V[:, :, P:VW], sb["kmask"][:])
            keys()
            if layer == 1:
                norm_factors(dve, sb, r, s_r, s_sd)
            for b in range(B):
                if layer == 1 and b == B - 1:
                    weights()
                values(b)
                if layer == 0:
                    stats(b)
            if layer == 0:
                dve.wait_ge(s_bn, B)
                for t in range(T):
                    last = dve.bn_aggr(sb["mv"][:, t, :], st[:, t, :])
                last.then_inc(s_bn, 1)
                dve.wait_ge(s_bn, B + 1)
                norm_variance(dve, sb, r, s_r)
                norm_factors(dve, sb, r, s_r, s_sd)

        @block.tensor
        def _(pe):
            pe.wait_ge(s_bvb, 1)
            for k in range(G):
                mm = pe.matmul(po[:, 0:D], bvb[:, k, :], aw[:, k, 3 * D:4 * D], start=(k == 0), stop=(k == G - 1))
            mm.then_inc(s_bo, 1)
            for g in range(G):
                if g == G - 1:
                    pe.wait_ge(s_bo, 2)
                for k in range(G):
                    mm = pe.matmul(pk[:, g, 0:B * SK], aw[:, k, D + g * P:D + (g + 1) * P], sb["ctx"][:, k, :],
                                   start=(k == 0), stop=(k == G - 1))
                mm.then_inc(s_kt, 1)
            for b in range(B):
                if layer == 1 and b == B - 1:
                    pe.wait_ge(s_kc, G)
                    pe.wait_ge(s_abs, 2)
                    pe.matmul(po[:, 0:2], sb["ones"][:], rows[:], start=True, stop=True).then_inc(s_tot, 1)
                pe.wait_ge(s_rep, G * (b + 1))
                if b >= 2:
                    pe.wait_ge(s_vb, b - 1)
                for c in range(CK):
                    for k in range(G):
                        mm = pe.matmul(pv[:, b % 2, c * D:(c + 1) * D], rep[b % 2][:, k, c * P:(c + 1) * P],
                                       aw[:, k, 2 * D:3 * D], start=(k == 0), stop=(k == G - 1))
                mm.then_inc(s_v, 1)


def attention_phase(nc, sb, layer):
    tag = sb["tag"]
    with ExitStack() as ctx:
        sem = lambda n: ctx.enter_context(nc.semaphore(n + tag))
        sbt = lambda n, s, d=F32: ctx.enter_context(nc.sbuf_tensor(n + tag, s, d))
        pst = lambda n, s, d=F32: ctx.enter_context(nc.psum_tensor(n + tag, s, d))
        (normed, xt_ps, xt_sb, q_ps, q_hi, q_sb, scored, masked, maxed, shifted, exped, pt_ps, pt_sb,
         weighed, recips, o_norm, ot_ps, ot_sb, projected, biased, added, stated) = (sem(n) for n in (
             "normed", "xt_ps", "xt_sb", "q_ps", "q_hi", "q_sb", "scored", "masked", "maxed", "shifted",
             "exped", "pt_ps", "pt_sb", "weighed", "recips", "o_norm", "ot_ps", "ot_sb", "projected",
             "biased", "added", "stated"))
        NS = HG * SK
        HS = NS // 2
        xn = [sbt(f"xn{i}", [P, D]) for i in range(2)]
        xt = [sbt(f"xt{i}", [P, D]) for i in range(2)]
        qh = [sbt(f"qh{i}", [P, D], F32R) for i in range(2)]
        ql = [sbt(f"ql{i}", [P, D], F32R) for i in range(2)]
        sm = [sbt(f"sm{i}", [P, G * NS]) for i in range(2)]
        mx = [sbt(f"mx{i}", [P, HEADS]) for i in range(2)]
        pr = [sbt(f"pr{i}", [P, G * NS]) for i in range(2)]
        pt = sbt("pt", [P, G * CK, P])
        rc = [sbt(f"rc{i}", [P, HEADS]) for i in range(2)]
        on = sbt("on", [P, D])
        ot = sbt("ot", [P, D])
        st = sbt("st", [P, 6])
        av = sbt("av", [P, 2])
        spare = sbt("spare", [P, 1])
        pA = pst("pA", [P, 512])
        pO = pst("pO", [P, 512])
        pS = pst("pS", [P, 4, 512])
        pT = pst("pT", [P, 2, 512])
        block = ctx.enter_context(nc.Block())
        aw, bqkv, bo = sb["aw"][layer], sb["bqkv"][layer], sb["bo"][layer]
        X = sb["x"][:].rearrange("p t d -> p (t d)")
        RS, NM = sb["rs"], sb["nm"]
        MV = sb["mv"][:].rearrange("p t a -> p (t a)")
        KH = sb["Kh"][:].rearrange("p n w -> p (n w)")
        KL = sb["Kl"][:].rearrange("p n w -> p (n w)")
        VB = sb["V"][:].rearrange("p n w -> p (n w)")
        MASK = sb["mask"][:].rearrange("p t k -> p (t k)")
        chunks = [(g, c) for g in range(G) for c in range(CK)]
        J = -(-len(chunks) // 4)
        rows = lambda c: LASTK if c == CK - 1 else P
        heads = lambda ap: ap.rearrange("p (h k) -> p h k", k=SK)
        banked = lambda ap: ap.rearrange("p (b h k) -> p b h k", b=4, k=SK)

        @block.gpsimd
        def _(pool):
            def shift(t, u):
                pool.wait_ge(maxed, t + 1)
                pool.tensor_tensor(heads(sm[u][:]), heads(sm[u][:]),
                                   mx[u][:].rearrange("p (h a) -> p h a", a=1).broadcast_to([P, HEADS, SK]),
                                   ALU.subtract).then_inc(shifted, 1)

            def bias(t):
                pool.wait_ge(normed, t + 1)
                pool.tensor_tensor(X[:, piece(t, D)], X[:, piece(t, D)], bo[:], ALU.add).then_inc(biased, 1)

            def step(t, u, has):
                if has(1):
                    shift(t + 1, 1 - u)
                    bias(t + 1)

            run_steps(pool, step, 3, 1)

        @block.tensor
        def _(pe):
            pe.sem_inc(xt_ps, 2)
            pe.sem_inc(pt_ps, 2 * J)
            pe.sem_inc(weighed, 1)

            def turn_x(t, u):
                pe.wait_ge(normed, t + 1)
                pe.wait_ge(q_sb, t + 1)
                for k in range(G):
                    mm = pe.transpose(pA[:, k * P:(k + 1) * P], xn[u][:, k * P:(k + 1) * P], sb["ident"][:])
                mm.then_inc(xt_ps, 1)

            def queries(t, u):
                pe.wait_ge(xt_sb, t + 1)
                for g in range(G):
                    for k in range(G):
                        mm = pe.matmul(pA[:, D + g * P:D + (g + 1) * P], aw[:, k, g * P:(g + 1) * P],
                                       xt[u][:, k * P:(k + 1) * P], start=(k == 0), stop=(k == G - 1))
                mm.then_inc(q_ps, 1)

            def scores(t, u):
                pe.wait_ge(q_sb, t + 2)
                pe.wait_ge(masked, t + 1)
                keys = (t // TB) * (G * NS)
                for b in range(4):
                    g = b // 2
                    h, l = qh[u][:, g * P:(g + 1) * P], ql[u][:, g * P:(g + 1) * P]
                    at = bass.ds(keys + b * HS, HS)
                    pe.matmul(pS[:, b, 0:HS], h, KH[:, at], start=True, stop=False)
                    pe.matmul(pS[:, b, 0:HS], h, KL[:, at], start=False, stop=False)
                    mm = pe.matmul(pS[:, b, 0:HS], l, KH[:, at], start=False, stop=True)
                mm.then_inc(scored, 1)

            def turn_p(t, u, j):
                if j == 0:
                    pe.wait_ge(exped, t + 3)
                pe.wait_ge(pt_sb, J * t + j + 1)
                for n in range(4 * j, min(4 * j + 4, len(chunks))):
                    g, c = chunks[n]
                    at = g * NS + c * P
                    mm = pe.transpose(pT[0:rows(c), (u + j) % 2, (n % 4) * P:(n % 4 + 1) * P],
                                      pr[u][:, at:at + rows(c)], sb["ident"][:])
                mm.then_inc(pt_ps, 1)

            def weigh(t, u, g):
                if g == 0:
                    pe.wait_ge(added, t + 1)
                vals = (t // TB) * (G * CK * VW)
                for n, (half, c) in enumerate(chunks):
                    if half != g:
                        continue
                    if c == 0 or n % 4 == 0:
                        pe.wait_ge(pt_sb, J * t + n // 4 + 3)
                    mm = pe.matmul(pO[:, g * VW:(g + 1) * VW], pt[0:rows(c), n, :],
                                   VB[0:rows(c), bass.ds(vals + n * VW, VW)],
                                   start=(c == 0), stop=(c == CK - 1))
                if g == G - 1:
                    mm.then_inc(weighed, 1)

            def turn_o(t):
                pe.wait_ge(o_norm, t + 1)
                for k in range(G):
                    mm = pe.transpose(pO[:, k * P:(k + 1) * P], on[:, k * P:(k + 1) * P], sb["ident"][:])
                mm.then_inc(ot_ps, 1)

            def project(t):
                pe.wait_ge(ot_sb, t + 1)
                for k in range(G):
                    mm = pe.matmul(pO[:, 0:D], ot[:, k * P:(k + 1) * P], aw[:, k, 3 * D:4 * D],
                                   start=(k == 0), stop=(k == G - 1))
                mm.then_inc(projected, 1)

            def step(t, u, has):
                if has(0):
                    turn_p(t, u, 0)
                if has(2):
                    turn_x(t + 2, u)
                if has(-1):
                    project(t - 1)
                if has(0):
                    turn_p(t, u, 1)
                if has(2):
                    queries(t + 2, u)
                if has(0):
                    turn_p(t, u, 2)
                    weigh(t, u, 0)
                    weigh(t, u, 1)
                if has(2):
                    scores(t + 2, u)
                if has(0):
                    turn_o(t)

            run_steps(pe, step, 3, 1)

        @block.scalar
        def _(act):
            act.sem_inc(pt_sb, 2)
            act.sem_inc(exped, 2)

            def xt_out(t, u):
                act.wait_ge(xt_ps, t + 3)
                act.activation(xt[u][:], pA[:, 0:D], ACT.Copy).then_inc(xt_sb, 1)

            def exp(t, u):
                act.wait_ge(shifted, t + 1)
                act.wait_ge(pt_ps, J * (t + 1))
                act.activation(pr[u][:], sm[u][:], ACT.Exp).then_inc(exped, 1)

            def pt_out(t, u, j):
                if j == 0:
                    act.wait_ge(weighed, t + 1)
                act.wait_ge(pt_ps, J * t + j + 1 + 2 * J)
                runs = []
                for n in range(4 * j, min(4 * j + 4, len(chunks))):
                    r = rows(chunks[n][1])
                    if runs and r == P and runs[-1][2] == P and runs[-1][1] == n:
                        runs[-1][1] = n + 1
                    else:
                        runs.append([n, n + 1, r])
                for lo, hi, r in runs:
                    last = act.activation(pt[0:r, lo:hi, :].rearrange("p n t -> p (n t)"),
                                          pT[0:r, (u + j) % 2, (lo % 4) * P:(lo % 4 + hi - lo) * P], ACT.Copy)
                last.then_inc(pt_sb, 1)

            def ot_out(t):
                act.wait_ge(ot_ps, t + 1)
                act.activation(ot[:], pO[:, 0:D], ACT.Copy).then_inc(ot_sb, 1)

            def step(t, u, has):
                if has(0):
                    pt_out(t, u, 0)
                if has(2):
                    xt_out(t + 2, u)
                if has(0):
                    pt_out(t, u, 1)
                    pt_out(t, u, 2)
                if has(1):
                    exp(t + 1, 1 - u)
                if has(0):
                    ot_out(t)

            run_steps(act, step, 3, 1)

        @block.vector
        def _(dve):
            dve.sem_inc(q_sb, 1)
            dve.sem_inc(masked, 1)
            dve.sem_inc(added, 1)

            def norm(t, u):
                dve.wait_ge(xt_ps, t + 1)
                dve.tensor_scalar(xn[u][:], X[:, piece(t, D)], RS[:, bass.ds(t, 1)], NM[:, bass.ds(t, 1)],
                                  ALU.mult, ALU.add).then_inc(normed, 1)

            def q_out(t, u):
                dve.wait_ge(q_ps, t + 1)
                dve.tensor_tensor(qh[u][:].rearrange("p (g n) -> p g n", g=G),
                                  pA[:, D:2 * D].rearrange("p (g n) -> p g n", g=G),
                                  bqkv[:, 0, :].rearrange("p (g a) -> p g a", a=1).broadcast_to([P, G, P]),
                                  ALU.add).then_inc(q_hi, 1)
                dve.wait_ge(q_hi, t + 1)
                for g in range(G):
                    half = slice(g * P, (g + 1) * P)
                    last = dve.scalar_tensor_tensor(ql[u][:, half], pA[:, D + g * P:D + (g + 1) * P],
                                                    bqkv[:, 0, g:g + 1], qh[u][:, half].bitcast(F32),
                                                    ALU.add, ALU.subtract)
                last.then_inc(q_sb, 1)

            def mask(t, u):
                dve.wait_ge(scored, t + 1)
                dve.wait_ge(exped, t + 1)
                at = (t % TB) * SK if layer == 0 else t * SK
                every = MASK[:, bass.ds(at, SK)].rearrange("p (a b k) -> p a b k", a=1, b=1)
                dve.tensor_tensor(banked(sm[u][:]), pS[:, :, 0:HS].rearrange("p b (h k) -> p b h k", k=SK),
                                  every.broadcast_to([P, 4, HEADS // 4, SK]),
                                  ALU.add if layer == 0 else ALU.min).then_inc(masked, 1)

            def largest(t, u, g):
                if g == 0:
                    dve.wait_ge(masked, t + 2)
                last = dve.tensor_reduce(mx[u][:, g * HG:(g + 1) * HG], heads(sm[u][:, g * NS:(g + 1) * NS]),
                                         AX.X, ALU.max)
                if g == G - 1:
                    last.then_inc(maxed, 1)

            def normalise(t, u):
                dve.wait_ge(weighed, t + 2)
                o = pO[:, 0:G * VW].rearrange("p (g w) -> p g w", g=G)
                dve.reciprocal(rc[u][:].rearrange("p (g h) -> p g h", g=G), o[:, :, P:VW]).then_inc(recips, 1)
                dve.wait_ge(recips, t + 1)
                dve.tensor_tensor(on[:].rearrange("p (g h d) -> p g h d", g=G, d=DH),
                                  o[:, :, 0:P].rearrange("p g (h d) -> p g h d", d=DH),
                                  rc[u][:].rearrange("p (g h a) -> p g h a", g=G, a=1).broadcast_to([P, G, HG, DH]),
                                  ALU.mult).then_inc(o_norm, 1)

            def add(t):
                dve.wait_ge(projected, t + 1)
                dve.wait_ge(biased, t + 1)
                dve.tensor_tensor(X[:, piece(t, D)], pO[:, 0:D], X[:, piece(t, D)], ALU.add).then_inc(added, 1)

            def stats(t):
                hold(dve, added, t + 2, spare[:])
                dve.bn_stats(st[:], X[:, piece(t, D)]).then_inc(stated, 1)
                hold(dve, stated, 2 * t + 1, spare[:])
                dve.bn_aggr(av[:], st[:]).then_inc(stated, 1)
                dve.wait_ge(stated, 2 * t + 2)
                dve.tensor_copy(MV[:, piece(t, 2)], av[:])

            def step(t, u, has):
                if has(1):
                    largest(t + 1, 1 - u, 0)
                if has(-1):
                    add(t - 1)
                if has(1):
                    largest(t + 1, 1 - u, 1)
                if has(2):
                    q_out(t + 2, u)
                if has(3):
                    norm(t + 3, 1 - u)
                if has(-1):
                    stats(t - 1)
                if has(0):
                    normalise(t, u)
                if has(2):
                    mask(t + 2, u)

            run_steps(dve, step, 3, 1)


def moe_phase(nc, sb):
    tag = sb["tag"]
    with ExitStack() as ctx:
        sem = lambda n: ctx.enter_context(nc.semaphore(n + tag))
        sbt = lambda n, s, d=F32: ctx.enter_context(nc.sbuf_tensor(n + tag, s, d))
        pst = lambda n, s, d=F32: ctx.enter_context(nc.psum_tensor(n + tag, s, d))
        r, s_r, s_sd = sbt("r", [P, 3, T]), sem("rstd_step"), sem("sd")
        (rt_hi, gu_hi, dn_hi, gu_ready, dn_ready, normed, xt_ps, xh_ok, xt_ok, l_ps, l_sb, lt_ps, r_step, dist, exped, r_chain,
         gu_ps, silued, h_ok, hh_ok, hl_ok, dn_ps, added, stated) = (sem(n) for n in (
             "rt_hi", "gu_hi", "dn_hi", "gu_ready", "dn_ready", "normed", "xt_ps", "xh_ok", "xt_ok", "l_ps", "l_sb", "lt_ps", "r_step",
             "dist", "exped", "r_chain", "gu_ps", "silued", "h_ok", "hh_ok", "hl_ok", "dn_ps", "added",
             "stated"))
        NGU = CH * 2 * P
        wgh, wgl = sbt("wgh", [P, G, NGU], F32R), sbt("wgl", [P, G, NGU], F32R)
        wdh, wdl = sbt("wdh", [P, CH, D], F32R), sbt("wdl", [P, CH, D], F32R)
        wrh, wrl = sbt("wrh", [P, G, P], F32R), sbt("wrl", [P, G, P], F32R)
        xn = [sbt(f"xn{i}", [P, D]) for i in range(2)]
        xh, xl = sbt("xh", [P, 2 * G * GW], F32R), sbt("xl", [P, 2 * G * GW], F32R)
        lg = sbt("lg", [P, GW])
        lt = sbt("lt", [P, ST, NE])
        top = sbt("top", [P, ST])
        rank = sbt("rank", [P, ST, NE])
        gt, eq = sbt("gt", [P, ST, NE, NE]), sbt("eq", [P, ST, NE, NE])
        ds_ = sbt("ds", [P, ST, NE])
        ex = sbt("ex", [P, ST, NE])
        en = sbt("en", [P, ST, NE])
        sums = sbt("sums", [P, 2, ST])
        coef = sbt("coef", [P, 2 * ST * NE])
        sg = [sbt(f"sg{i}", [P, GW]) for i in range(2)]
        hf = [sbt(f"hf{i}", [P, GW]) for i in range(2)]
        hh = [sbt(f"hh{i}", [P, GW], F32R) for i in range(2)]
        hl = [sbt(f"hl{i}", [P, GW], F32R) for i in range(2)]
        st = sbt("st", [P, ST, 6])
        av = sbt("av", [P, ST, 2])
        spare = sbt("spare", [P, 1])
        pGU = [pst(f"pGU{i}", [P, 2, GW]) for i in range(2)]
        pD = pst("pD", [P, ST, D])
        pX = pst("pX", [P, 512])
        pL = pst("pL", [P, 512])
        block = ctx.enter_context(nc.Block())
        X = sb["x"][:].rearrange("p t d -> p (t d)")
        MV = sb["mv"][:].rearrange("p t a -> p (t a)")
        RS, NM = sb["rs"], sb["nm"]
        f32 = lambda ap: ap.bitcast(F32)
        TURNS, ROUTE = (1, 2, 3, 4), 6

        def part(j):
            return slice(j * (NGU // ST), (j + 1) * (NGU // ST))

        def xpart(buf, s, k, lo=0, n=GW):
            return buf[:, bass.ds((s % 2) * (G * GW) + (k * GW + lo), n)]

        @block.gpsimd
        def _(pool):
            def low(n, u):
                pool.wait_ge(hh_ok, n + 1)
                pool.wait_ge(dn_ps, n + 1)
                pool.tensor_tensor(hl[u][:], hf[u][:], f32(hh[u][:]), ALU.subtract).then_inc(hl_ok, 1)

            pool.sem_inc(hl_ok, 2)
            pool.wait_ge(dn_hi, 1)
            pool.tensor_tensor(wdl[:], sb["dn"][:], f32(wdh[:]), ALU.subtract).then_inc(dn_ready, 1)
            with pool.Fori(0, NG) as s:
                for c in range(CH):
                    low(s * CH + c, c % 2)

        @block.tensor
        def _(pe):
            pe.sem_inc(xt_ps, 2)
            pe.sem_inc(dn_ps, 2)

            def turn(s, j):
                t = ST * s + j
                pe.wait_ge(normed, t + 1)
                pe.wait_ge(xt_ok, t + 1)
                for k in range(G):
                    mm = pe.transpose(pX[:, k * P:(k + 1) * P], xn[j % 2][:, k * P:(k + 1) * P], sb["ident"][:])
                mm.then_inc(xt_ps, 1)

            def three(out, ah, al, bh, bl, first, last):
                pe.matmul(out, ah, bh, start=first, stop=False)
                pe.matmul(out, ah, bl, start=False, stop=False)
                return pe.matmul(out, al, bh, start=False, stop=last)

            def route(s):
                pe.wait_ge(xt_ok, ST * s + ST + 1)
                pe.wait_ge(r_step, s + 1)
                for k in range(G):
                    mm = three(pL[:], wrh[:, k, :], wrl[:, k, :], xpart(xh, s, k), xpart(xl, s, k),
                               k == 0, k == G - 1)
                mm.then_inc(l_ps, 1)

            def route_back(s):
                pe.wait_ge(l_sb, s + 1)
                for j in range(ST):
                    mm = pe.transpose(pL[:, j * P:(j + 1) * P], lg[:, j * P:(j + 1) * P], sb["ident"][:])
                mm.then_inc(lt_ps, 1)

            def gate_up(s, c):
                n = s * CH + c
                pe.wait_ge(xt_ok, ST * s + ST + 1)
                pe.wait_ge(h_ok, n + 1)
                for a in range(2):
                    at = (2 * c + a) * P
                    for k in range(G):
                        mm = three(pGU[c % 2][:, a, :], wgh[:, k, at:at + P], wgl[:, k, at:at + P],
                                   xpart(xh, s, k), xpart(xl, s, k), k == 0, k == G - 1)
                mm.then_inc(gu_ps, 1)

            def down(s, c):
                n = s * CH + c
                pe.wait_ge(hl_ok, n + 3)
                if c != CH - 1:
                    pe.wait_ge(added, s * (CH - 1) + c + 1)
                for j in range(ST):
                    first = c != CH - 1 and j % 2 == 0
                    h, l = hh[c % 2][:, j * P:(j + 1) * P], hl[c % 2][:, j * P:(j + 1) * P]
                    pe.matmul(pD[:, j, :], h, wdh[:, c, :], start=first, stop=False, skip_group_check=True)
                    pe.matmul(pD[:, j, :], h, wdl[:, c, :], start=False, stop=False, skip_group_check=True)
                    mm = pe.matmul(pD[:, j, :], l, wdh[:, c, :], start=False, stop=(c != CH - 2),
                                   skip_group_check=True)
                mm.then_inc(dn_ps, 1)

            for j in range(ST):
                turn(0, j)
            route(0)
            pe.wait_ge(gu_ready, ST)
            gate_up(0, 0)
            route_back(0)
            pe.wait_ge(dn_ready, 1)
            with pe.Fori(0, NG - 1) as s:
                for c in range(CH):
                    if c in TURNS:
                        turn(s + 1, TURNS.index(c))
                    if c == ROUTE:
                        route(s + 1)
                    if c == ROUTE + 1:
                        route_back(s + 1)
                    if c < CH - 1:
                        gate_up(s, c + 1)
                    else:
                        gate_up(s + 1, 0)
                    down(s, c)
            for c in range(CH):
                if c < CH - 1:
                    gate_up(NG - 1, c + 1)
                down(NG - 1, c)

        @block.scalar
        def _(act):
            norm_root(act, r, s_r, s_sd)
            act.wait_ge(sb["moe_in"], 48)
            act.activation(wdh[:], sb["dn"][:], ACT.Copy).then_inc(dn_hi, 1)

            def weights_high(j):
                act.activation(wgh[:, :, part(j)], sb["gu"][:, :, part(j)], ACT.Copy).then_inc(gu_hi, 1)

            def x_high(s, j):
                act.wait_ge(xt_ps, ST * s + j + 3)
                for k in range(G):
                    last = act.activation(xpart(xh, s, k, j * P, P), pX[:, k * P:(k + 1) * P], ACT.Copy)
                last.then_inc(xh_ok, 1)

            def logits_out(s):
                act.wait_ge(l_ps, s + 1)
                act.activation(lg[:], pL[:], ACT.Copy).then_inc(l_sb, 1)

            def soft(s):
                act.wait_ge(dist, s + 1)
                act.activation(ex[:], ds_[:], ACT.Silu)
                act.activation(en[:], ds_[:], ACT.Silu, scale=-1.0).then_inc(exped, 1)

            def silu(n, u):
                act.wait_ge(gu_ps, n + 1)
                act.activation(sg[u][:], pGU[u][:, 0, :], ACT.Silu).then_inc(silued, 1)

            def high(n, u):
                act.wait_ge(h_ok, n + 3)
                act.wait_ge(dn_ps, n + 1)
                act.activation(hh[u][:], hf[u][:], ACT.Copy).then_inc(hh_ok, 1)

            for j in range(ST):
                weights_high(j)
                x_high(0, j)
            logits_out(0)
            silu(0, 0)
            soft(0)
            with act.Fori(0, NG - 1) as s:
                for c in range(CH):
                    high(s * CH + c, c % 2)
                    if c in TURNS:
                        x_high(s + 1, TURNS.index(c))
                    if c == ROUTE:
                        logits_out(s + 1)
                    silu(s * CH + c + 1, (c + 1) % 2)
                    if c == ROUTE + 2:
                        soft(s + 1)
            for c in range(CH):
                high((NG - 1) * CH + c, c % 2)
                if c < CH - 1:
                    silu((NG - 1) * CH + c + 1, (c + 1) % 2)

        @block.vector
        def _(dve):
            dve.sem_inc(xt_ok, 1)
            dve.sem_inc(r_step, 1)
            dve.sem_inc(h_ok, 2)
            dve.sem_inc(added, 1)
            norm_variance(dve, sb, r, s_r)
            norm_factors(dve, sb, r, s_r, s_sd)
            dve.wait_ge(sb["moe_in"], 48)
            dve.memset(f32(wrh[:, :, NE:P]), 0.0)
            dve.memset(f32(wrl[:, :, NE:P]), 0.0)
            dve.tensor_copy(wrh[:, :, 0:NE], sb["rt"][:]).then_inc(rt_hi, 1)
            dve.wait_ge(rt_hi, 1)
            dve.tensor_tensor(wrl[:, :, 0:NE], sb["rt"][:], f32(wrh[:, :, 0:NE]), ALU.subtract)

            def weights_low(j):
                dve.wait_ge(gu_hi, j + 1)
                dve.tensor_tensor(wgl[:, :, part(j)], sb["gu"][:, :, part(j)], f32(wgh[:, :, part(j)]),
                                  ALU.subtract).then_inc(gu_ready, 1)

            def norm(s, j):
                t = ST * s + j
                dve.wait_ge(xt_ps, t + 1)
                dve.tensor_scalar(xn[j % 2][:], X[:, piece(t, D)], RS[:, bass.ds(t, 1)],
                                  NM[:, bass.ds(t, 1)], ALU.mult, ALU.add).then_inc(normed, 1)

            def x_low(s, j):
                dve.wait_ge(xh_ok, ST * s + j + 1)
                for k in range(G):
                    last = dve.tensor_tensor(xpart(xl, s, k, j * P, P), pX[:, k * P:(k + 1) * P],
                                             f32(xpart(xh, s, k, j * P, P)), ALU.subtract)
                last.then_inc(xt_ok, 1)

            R = 12

            def route_a(s):
                dve.wait_ge(lt_ps, s + 1)
                dve.tensor_copy(lt[:], pL[:].rearrange("p (j e) -> p j e", e=P)[:, :, 0:NE]).then_inc(r_step, 1)
                dve.wait_ge(r_step, s + 2)
                dve.tensor_reduce(top[:], lt[:], AX.X, ALU.max).then_inc(r_chain, 1)
                mine = lt[:].rearrange("p j (e a) -> p j e a", a=1).broadcast_to([P, ST, NE, NE])
                other = lt[:].rearrange("p j (a e) -> p j a e", a=1).broadcast_to([P, ST, NE, NE])
                dve.tensor_tensor(gt[:], other, mine, ALU.is_gt).then_inc(r_chain, 1)
                dve.tensor_tensor(eq[:], other, mine, ALU.is_equal).then_inc(r_chain, 1)
                dve.wait_ge(r_chain, s * R + 3)
                dve.scalar_tensor_tensor(ds_[:], lt[:], -1.0,
                                         top[:].rearrange("p (j a) -> p j a", a=1).broadcast_to([P, ST, NE]),
                                         ALU.add, ALU.subtract).then_inc(dist, 1)

            def route_b(s):
                dve.wait_ge(r_chain, s * R + 3)
                dve.tensor_tensor(eq[:], eq[:], sb["lower"][:].rearrange("p (a i) j -> p a (i j)", a=1)
                                  .broadcast_to([P, ST, NE * NE]).rearrange("p a (i j) -> p a i j", j=NE),
                                  ALU.mult).then_inc(r_chain, 1)
                dve.wait_ge(r_chain, s * R + 4)
                dve.tensor_tensor(gt[:], gt[:], eq[:], ALU.add).then_inc(r_chain, 1)

            def route_c(s):
                dve.wait_ge(r_chain, s * R + 5)
                dve.tensor_reduce(rank[:], gt[:], AX.X, ALU.add).then_inc(r_chain, 1)
                dve.wait_ge(exped, s + 1)
                dve.reciprocal(en[:], en[:]).then_inc(r_chain, 1)
                dve.wait_ge(r_chain, s * R + 7)
                dve.tensor_tensor(ex[:], ex[:], en[:], ALU.mult).then_inc(r_chain, 1)
                dve.wait_ge(r_chain, s * R + 8)
                dve.tensor_reduce(sums[:, 0, :], ex[:], AX.X, ALU.add).then_inc(r_chain, 1)
                dve.wait_ge(r_chain, s * R + 9)
                dve.reciprocal(sums[:, 1, :], sums[:, 0, :]).then_inc(r_chain, 1)
                dve.scalar_tensor_tensor(ex[:], rank[:], float(TOPK), ex[:], ALU.is_lt, ALU.mult).then_inc(r_chain, 1)
                dve.wait_ge(r_chain, s * R + 11)
                dve.tensor_tensor(coef[:, bass.ds((s % 2) * (ST * NE), ST * NE)].rearrange("p (j e) -> p j e", e=NE),
                                  ex[:], sums[:, 1, :].rearrange("p (j a) -> p j a", a=1).broadcast_to([P, ST, NE]),
                                  ALU.mult).then_inc(r_chain, 1)

            def product(n, u):
                dve.wait_ge(silued, n + 1)
                dve.wait_ge(hl_ok, n + 1)
                dve.tensor_tensor(hf[u][:], pGU[u][:, 1, :], sg[u][:], ALU.mult).then_inc(h_ok, 1)

            def add(s, c):
                dve.wait_ge(dn_ps, s * CH + c + 3)
                dve.wait_ge(r_chain, (s + 1) * R)
                dve.wait_ge(added, s * (CH - 1) + (c if c < NE else NE) + 1)
                for j in range(ST):
                    xs = X[:, bass.ds((s * ST + j) * D, D)]
                    if c < NE:
                        last = dve.scalar_tensor_tensor(
                            xs, pD[:, j, :], coef[:, bass.ds((s % 2) * (ST * NE) + (j * NE + c), 1)], xs,
                            ALU.mult, ALU.add)
                    else:
                        last = dve.tensor_tensor(xs, pD[:, j, :], xs, ALU.add)
                last.then_inc(added, 1)

            def stats(s):
                hold(dve, added, (s + 1) * (CH - 1) + 1, spare[:])
                for j in range(ST):
                    last = dve.bn_stats(st[:, j, :], X[:, bass.ds((s * ST + j) * D, D)])
                last.then_inc(stated, 1)

            def moments(s):
                hold(dve, stated, 2 * s + 1, spare[:])
                for j in range(ST):
                    last = dve.bn_aggr(av[:, j, :], st[:, j, :])
                last.then_inc(stated, 1)
                dve.wait_ge(stated, 2 * s + 2)
                dve.tensor_copy(MV[:, bass.ds(s * (2 * ST), 2 * ST)], av[:].rearrange("p j a -> p (j a)"))

            def group(s, first):
                for c in range(CH):
                    if c in TURNS:
                        x_low(s + 1, TURNS.index(c))
                    if c + 1 in TURNS:
                        norm(s + 1, TURNS.index(c + 1))
                    if c == ROUTE + 3:
                        route_c(s + 1)
                    product(s * CH + c + 1, (c + 1) % 2)
                    if c != CH - 2:
                        add(s, c)
                    if c == ROUTE - 1 and not first:
                        stats(s - 1)
                    if c == ROUTE and not first:
                        moments(s - 1)
                    if c == ROUTE + 1:
                        route_a(s + 1)
                    if c == ROUTE + 2:
                        route_b(s + 1)

            norm(0, 0)
            norm(0, 1)
            for j in range(ST):
                x_low(0, j)
                if j + 2 < ST:
                    norm(0, j + 2)
                weights_low(j)
            route_a(0)
            product(0, 0)
            route_b(0)
            route_c(0)
            group(0, True)
            with dve.Fori(1, NG - 1) as s:
                group(s, False)
            for c in range(CH):
                if c < CH - 1:
                    product((NG - 1) * CH + c + 1, (c + 1) % 2)
                if c != CH - 2:
                    add(NG - 1, c)
                else:
                    stats(NG - 2)
                    moments(NG - 2)
            stats(NG - 1)
            moments(NG - 1)


def mlp_phase(nc, dram, sb):
    with ExitStack() as ctx:
        sem = lambda n: ctx.enter_context(nc.semaphore(n + "_m"))
        sbt = lambda n, s, d=F32: ctx.enter_context(nc.sbuf_tensor(n + "_m", s, d))
        pst = lambda n, s, d=F32: ctx.enter_context(nc.psum_tensor(n + "_m", s, d))
        (x_normed, x_affine, biased, a_step, qa_ok, qat_ps, qat_sb, up_ps, up_ok, gelu_ok, e_step, half_ok,
         rooted, normed, gained, shifted, c_step, qc_ok, qct_ps, qct_sb, down_ps, y_ok) = (sem(n) for n in (
             "x_normed", "x_affine", "biased", "a_step", "qa_ok", "qat_ps", "qat_sb", "up_ps", "up_ok",
             "gelu_ok", "e_step", "half_ok", "rooted", "normed", "gained", "shifted", "c_step", "qc_ok",
             "qct_ps", "qct_sb", "down_ps", "y_ok"))
        stored = sem("stored")
        r, s_r, s_sd = sbt("r", [P, 3, T]), sem("rstd_step"), sem("sd")
        ha = [sbt(f"ha{i}", [P, D]) for i in range(2)]
        sa = [sbt(f"sa{i}", [P, 8]) for i in range(2)]
        qa = [sbt(f"qa{i}", [P, D], BF16) for i in range(2)]
        qat = [sbt(f"qat{i}", [P, G, P], BF16) for i in range(2)]
        hb = [sbt(f"hb{i}", [P, HID]) for i in range(2)]
        ge = [sbt(f"ge{i}", [P, HID]) for i in range(2)]
        hn = [sbt(f"hn{i}", [P, HID]) for i in range(2)]
        st = [sbt(f"st{i}", [P, 2, 6]) for i in range(2)]
        se = [sbt(f"se{i}", [P, 8]) for i in range(2)]
        sc = [sbt(f"sc{i}", [P, 8]) for i in range(2)]
        half = sbt("half", [P, 1])
        spare = sbt("spare", [P, 1])
        qc = [sbt(f"qc{i}", [P, HID], BF16) for i in range(2)]
        qct = [sbt(f"qct{i}", [P, KH, P], BF16) for i in range(2)]
        pU = [pst(f"pU{i}", [P, HID]) for i in range(2)]
        pA = pst("pA", [P, G * P], BF16)
        pC = pst("pC", [P, HID], BF16)
        pY = pst("pY", [P, 512])
        block = ctx.enter_context(nc.Block())
        X = sb["x"][:].rearrange("p t d -> p (t d)")
        out = dram["out"].rearrange("b s d -> (b s) d")
        A, E, C = 6, 4, 6
        LEAD, LAG = 6, 1

        @block.sync
        def _(sp):
            with sp.Fori(0, T) as t:
                sp.wait_ge(y_ok, t + 2)
                sp.dma_start(out[bass.ds(t * P, P), :], X[:, piece(t, D)]).then_inc(stored, 16)
            sp.wait_ge(stored, 16 * T)

        @block.gpsimd
        def _(pool):
            pool.wait_ge(sb["mlp_in"], 16 * len(MLP_ROWS))
            pool.memset(half[:], -0.5).then_inc(half_ok, 1)
            pool.wait_ge(half_ok, 1)

            def x_gain(t, u):
                pool.wait_ge(x_normed, t + 1)
                pool.tensor_tensor(ha[u][:], ha[u][:], sb["g1"][:], ALU.mult).then_inc(x_affine, 1)

            def x_offset(t, u):
                pool.wait_ge(x_affine, 2 * t + 1)
                pool.tensor_tensor(ha[u][:], ha[u][:], sb["c1"][:], ALU.add).then_inc(x_affine, 1)

            def gain(t, u):
                pool.wait_ge(normed, t + 3)
                pool.tensor_tensor(hn[u][:], hn[u][:], sb["g2"][:], ALU.mult).then_inc(gained, 1)

            def root(t, u):
                pool.wait_ge(e_step, t * E + 3)
                pool.tensor_tensor(se[u][:, 3:4], se[u][:, 2:3], half[:], ALU.pow).then_inc(rooted, 1)

            def offset(t, u):
                pool.wait_ge(gained, t + 1)
                pool.tensor_tensor(hn[u][:], hn[u][:], sb["c2"][:], ALU.add).then_inc(shifted, 1)

            def step(t, u, has):
                if has(5):
                    x_gain(t + 5, 1 - u)
                    x_offset(t + 5, 1 - u)
                if has(2):
                    root(t + 2, u)
                if has(1):
                    gain(t + 1, 1 - u)
                    offset(t + 1, 1 - u)

            run_steps(pool, step, LEAD, LAG)

        @block.tensor
        def _(pe):
            def turn_x(t, u):
                pe.wait_ge(qa_ok, t + 3)
                pe.wait_ge(qat_sb, t + 1)
                for k in range(G):
                    mm = pe.transpose(pA[:, k * P:(k + 1) * P], qa[u][:, k * P:(k + 1) * P], sb["identb"][:])
                mm.then_inc(qat_ps, 1)

            def up(t, u):
                pe.wait_ge(qat_sb, t + 2)
                pe.wait_ge(up_ok, t + 1)
                for n in range(2):
                    for k in range(G):
                        mm = pe.matmul(pU[u][:, n * 512:(n + 1) * 512], qat[u][:, k, :],
                                       sb["q1"][:, k, n * 512:(n + 1) * 512], start=(k == 0), stop=(k == G - 1))
                mm.then_inc(up_ps, 1)

            def turn_h(t, u):
                pe.wait_ge(qc_ok, t + 3)
                pe.wait_ge(qct_sb, t + 1)
                for k in range(KH):
                    mm = pe.transpose(pC[:, k * P:(k + 1) * P], qc[u][:, k * P:(k + 1) * P], sb["identb"][:])
                mm.then_inc(qct_ps, 1)

            def down(t, u):
                pe.wait_ge(qct_sb, t + 2)
                pe.wait_ge(y_ok, t + 1)
                for k in range(KH):
                    mm = pe.matmul(pY[:, 0:D], qct[u][:, k, :], sb["q2"][:, k, :], start=(k == 0), stop=(k == KH - 1))
                mm.then_inc(down_ps, 1)

            def step(t, u, has):
                if has(4):
                    turn_x(t + 4, u)
                if has(4):
                    up(t + 4, u)
                if has(-1):
                    down(t - 1, 1 - u)
                if has(0):
                    turn_h(t, u)

            run_steps(pe, step, LEAD, LAG)

        @block.scalar
        def _(act):
            act.sem_inc(qa_ok, 2)
            act.sem_inc(qc_ok, 2)
            act.sem_inc(normed, 2)
            act.sem_inc(qat_sb, 1)
            act.sem_inc(qct_sb, 1)

            norm_root(act, r, s_r, s_sd)
            act.wait_ge(s_r, NORM_STEPS)

            def x_norm(t, u):
                act.wait_ge(qa_ok, t + 1)
                act.activation(ha[u][:], X[:, piece(t, D)], ACT.Identity, scale=sb["rs"][:, bass.ds(t, 1)],
                               bias=sb["nm"][:, bass.ds(t, 1)]).then_inc(x_normed, 1)

            def x_integers(t, u):
                act.wait_ge(a_step, t * A + A)
                act.wait_ge(qat_ps, t + 1)
                act.activation(qa[u][:], ha[u][:], ACT.Copy, bias=-MAGIC).then_inc(qa_ok, 1)

            def x_turned(t, u):
                act.wait_ge(qat_ps, t + 3)
                act.wait_ge(up_ps, t + 1)
                act.activation(qat[u][:].rearrange("p k n -> p (k n)"), pA[:], ACT.Copy).then_inc(qat_sb, 1)

            def gelu(t, u):
                act.wait_ge(up_ok, t + 3)
                act.wait_ge(normed, t + 1)
                act.activation(ge[u][:], hb[u][:], ACT.Gelu).then_inc(gelu_ok, 1)

            def h_norm(t, u):
                act.wait_ge(e_step, t * E + E)
                act.wait_ge(qc_ok, t + 1)
                act.activation(hn[u][:], ge[u][:], ACT.Identity, scale=se[u][:, 3:4],
                               bias=se[u][:, 4:5]).then_inc(normed, 1)

            def h_integers(t, u):
                act.wait_ge(c_step, t * C + C)
                act.activation(qc[u][:], hn[u][:], ACT.Copy, bias=-MAGIC).then_inc(qc_ok, 1)

            def h_turned(t, u):
                act.wait_ge(qct_ps, t + 1)
                act.activation(qct[u][:].rearrange("p k n -> p (k n)"), pC[:], ACT.Copy).then_inc(qct_sb, 1)

            def step(t, u, has):
                if has(-1):
                    h_turned(t - 1, 1 - u)
                if has(4):
                    x_integers(t + 4, u)
                if has(6):
                    x_norm(t + 6, u)
                if has(4):
                    x_turned(t + 4, u)
                if has(0):
                    h_integers(t, u)
                if has(2):
                    h_norm(t + 2, u)
                if has(4):
                    gelu(t + 4, u)

            run_steps(act, step, LEAD, LAG)

        @block.vector
        def _(dve):
            dve.sem_inc(up_ok, 2)
            dve.sem_inc(y_ok, 1)
            dve.sem_inc(qat_ps, 2)
            dve.sem_inc(up_ps, 2)
            norm_variance(dve, sb, r, s_r)
            norm_factors(dve, sb, r, s_r, s_sd)

            def largest(sides):
                for h, s, k, sem_, n in sides:
                    dve.tensor_reduce(s[:, 0:1], h, AX.X, ALU.max, apply_absolute_value=True).then_inc(sem_, 1)

            def scales(sides):
                for h, s, k, sem_, n in sides:
                    dve.wait_ge(sem_, n + 1)
                    dve.tensor_scalar(s[:, 1:2], s[:, 0:1], 1e-5, None, ALU.max).then_inc(sem_, 1)
                for h, s, k, sem_, n in sides:
                    dve.wait_ge(sem_, n + 2)
                    dve.reciprocal(s[:, 2:3], s[:, 1:2]).then_inc(sem_, 1)
                for h, s, k, sem_, n in sides:
                    dve.wait_ge(sem_, n + 3)
                    dve.tensor_scalar(s[:, 3:4], s[:, 2:3], 127.0, None, ALU.mult).then_inc(sem_, 1)
                for h, s, k, sem_, n in sides:
                    dve.tensor_scalar(s[:, 4:5], s[:, 1:2], 1.0 / 127.0, sb["wsi"][:, k:k + 1],
                                      ALU.mult, ALU.mult).then_inc(sem_, 1)

            def round_up(side):
                h, s, k, sem_, n = side
                dve.wait_ge(sem_, n + 5)
                dve.tensor_scalar(h, h, s[:, 3:4], MAGIC, ALU.mult, ALU.add).then_inc(sem_, 1)

            dve.wait_ge(sb["mlp_in"], 16 * len(MLP_ROWS))

            def bias(t):
                dve.wait_ge(x_normed, t + 1)
                dve.tensor_tensor(X[:, piece(t, D)], X[:, piece(t, D)], sb["b2"][:], ALU.add).then_inc(biased, 1)

            def hidden(t, u):
                dve.wait_ge(up_ps, t + 3)
                dve.scalar_tensor_tensor(hb[u][:], pU[u][:], sa[u][:, 4:5], sb["b1"][:],
                                         ALU.mult, ALU.add).then_inc(up_ok, 1)

            def stats(t, u):
                dve.wait_ge(gelu_ok, t + 1)
                for n in range(2):
                    last = dve.bn_stats(st[u][:, n, :], ge[u][:, n * 512:(n + 1) * 512])
                last.then_inc(e_step, 1)
                hold(dve, e_step, t * E + 1, spare[:])
                dve.bn_aggr(se[u][:, 0:2], st[u][:].rearrange("p a b -> p (a b)")).then_inc(e_step, 1)
                dve.wait_ge(e_step, t * E + 2)
                dve.tensor_scalar(se[u][:, 2:3], se[u][:, 1:2], EPS, None, ALU.add).then_inc(e_step, 1)

            def factor(t, u):
                dve.wait_ge(rooted, t + 1)
                dve.tensor_scalar(se[u][:, 4:5], se[u][:, 0:1], se[u][:, 3:4], -1.0, ALU.mult, ALU.mult).then_inc(e_step, 1)

            def result(t, u):
                dve.wait_ge(down_ps, t + 1)
                dve.wait_ge(biased, t + 1)
                dve.scalar_tensor_tensor(X[:, piece(t, D)], pY[:, 0:D], sc[u][:, 4:5], X[:, piece(t, D)],
                                         ALU.mult, ALU.add).then_inc(y_ok, 1)

            def step(t, u, has):
                sides = []
                if has(0):
                    dve.wait_ge(shifted, t + 1)
                    sides.append((hn[u][:], sc[u], 1, c_step, t * C))
                if has(5):
                    dve.wait_ge(x_affine, 2 * (t + 5) + 2)
                    sides.append((ha[1 - u][:], sa[1 - u], 0, a_step, (t + 5) * A))
                largest(sides)
                if has(5):
                    bias(t + 5)
                scales(sides)
                if has(2):
                    factor(t + 2, u)
                if has(0):
                    round_up(sides[0])
                if has(3):
                    stats(t + 3, 1 - u)
                if has(4):
                    hidden(t + 4, u)
                if has(5):
                    round_up(sides[-1])
                if has(-1):
                    result(t - 1, 1 - u)

            run_steps(dve, step, LEAD, LAG)


def build(nc, dram):
    with ExitStack() as ctx:
        sb = {}

        def keep(name, shape, dt=F32):
            sb[name] = ctx.enter_context(nc.sbuf_tensor(name, shape, dt))

        keep("x", [P, T, D])
        keep("mv", [P, T, 2])
        keep("rs", [P, T])
        keep("nm", [P, T])
        keep("ident", [P, P])
        keep("ones", [P, P])
        keep("hmask", [P, HG])
        keep("kmask", [P, CK, HG])
        keep("lower", [P, NE, NE])
        keep("ctx", [P, G, B * SK])
        keep("m1", [P, T, SK], U8)
        keep("wsi", [P, 2])
        for name in ("moe_in", "mlp_in", "w_in"):
            sb[name] = ctx.enter_context(nc.semaphore(name))
        sb["x_in"] = [ctx.enter_context(nc.semaphore(f"x_in{b}")) for b in range(B)]
        sb["att_in"] = [ctx.enter_context(nc.semaphore(f"att_in{n}")) for n in range(2)]
        for name in ("aw", "bqkv", "bo"):
            sb[name] = [None, None]

        def attention_weights(stack, layer):
            for name, shape in (("aw", [P, G, 4 * D]), ("bqkv", [P, 3, G]), ("bo", [P, D])):
                sb[name][layer] = stack.enter_context(nc.sbuf_tensor(f"{name}{layer}", shape, F32))

        def attention(layer):
            with ExitStack() as att:
                sb["tag"] = f"_a{layer}"
                for part in ("Kh", "Kl"):
                    sb[part] = att.enter_context(nc.sbuf_tensor(f"{part}{layer}", [P, B * G, HG * SK], F32R))
                sb["V"] = att.enter_context(nc.sbuf_tensor(f"V{layer}", [P, B * G, CK * VW], F32))
                sb["mask"] = att.enter_context(nc.sbuf_tensor(f"mask{layer}", [P, T if layer else TB, SK], F32))
                if layer == 0:
                    load_phase(nc, dram, sb)
                with ExitStack() as raw:
                    if layer == 1:
                        sb["w1"] = raw.enter_context(nc.sbuf_tensor("w1", [P, G, HID], F32))
                        sb["w2"] = raw.enter_context(nc.sbuf_tensor("w2", [P, KH, D], F32))
                    norm_and_keys_phase(nc, dram, sb, layer)
                attention_phase(nc, sb, layer)

        attention_weights(ctx, 1)
        moe = ExitStack()
        for name, shape in (("gu", [P, G, CH * 2 * P]), ("dn", [P, CH, D]), ("rt", [P, G, NE])):
            sb[name] = moe.enter_context(nc.sbuf_tensor(name, shape, F32))
        with ExitStack() as first:
            attention_weights(first, 0)
            sb["m0"] = first.enter_context(nc.sbuf_tensor("m0", [P, TB, SK], F32))
            attention(0)
        sb["tag"] = "_f0"
        moe_phase(nc, sb)
        moe.close()
        for name, w in zip(MLP_ROWS, (D, D, HID, HID, HID, D)):
            keep(name, [P, w])
        keep("identb", [P, P], BF16)
        keep("q1", [P, G, HID], BF16)
        keep("q2", [P, KH, D], BF16)
        attention(1)
        mlp_phase(nc, dram, sb)


def kernel(**inputs):
    import concourse.bacc as bacc
    from concourse.bass_utils import run_bass_kernel_spmd

    a = {k: np.asarray(v) for k, v in inputs.items()}
    keep = {
        "x": a["x"],
        "ctx": a["ctx_1024"].transpose(2, 0, 1).reshape(D, B * SK),
        "m0": a["mask_1x1xSxS2_fk1"].reshape(SQ, SK),
        "m1": a["mask_Bx1xSxS2_bk1"].reshape(B * SQ, SK),
        "aw0": np.concatenate([a[f"L0_xattn_w{n}_w"] for n in "qkvo"], axis=1),
        "aw1": np.concatenate([a[f"L1_xattn_W{n}"].T for n in "qkvo"], axis=1),
        "bqkv0": np.concatenate([a[f"L0_xattn_w{n}_b"] for n in "qkv"]).reshape(3 * G, P).T,
        "bqkv1": np.concatenate([a[f"L1_xattn_b{n}"] for n in "qkv"]).reshape(3 * G, P).T,
        "bo0": a["L0_xattn_wo_b"].reshape(1, D), "bo1": a["L1_xattn_bo"].reshape(1, D),
        "rt": a["L0_ffn_router"],
        "gu": np.stack([
            np.concatenate([a["L0_ffn_experts_gate"].transpose(1, 0, 2), a["L0_ffn_shared_gate"].reshape(D, DS // P, P)], axis=1),
            np.concatenate([a["L0_ffn_experts_up"].transpose(1, 0, 2), a["L0_ffn_shared_up"].reshape(D, DS // P, P)], axis=1),
        ], axis=2).reshape(D, CH * 2 * P),
        "dn": np.concatenate([a["L0_ffn_experts_down"].reshape(NE * DE, D), a["L0_ffn_shared_down"]], axis=0),
        "w1": a["L1_ffn_w1"].T, "w2": a["L1_ffn_w2"].T,
        "g1": a["L1_ffn_ln1_g"].reshape(1, D), "c1": a["L1_ffn_ln1_b"].reshape(1, D),
        "b1": a["L1_ffn_b1"].reshape(1, HID), "g2": a["L1_ffn_ln2_g"].reshape(1, HID),
        "c2": a["L1_ffn_ln2_b"].reshape(1, HID), "b2": a["L1_ffn_b2"].reshape(1, D),
    }
    nc = bacc.Bacc("TRN2", target_bir_lowering=False, num_devices=1)
    arrays, dram = {}, {}
    for name, v in keep.items():
        arrays[name + "_in"] = np.ascontiguousarray(v)
        dram[name] = nc.dram_tensor(name + "_in", v.shape, mybir.dt.from_np(v.dtype), kind="ExternalInput").ap()
    dram["out"] = nc.dram_tensor("out_x", (B, SQ, D), F32, kind="ExternalOutput").ap()
    for name in ("aw", "bqkv", "bo"):
        dram[name] = [dram[name + "0"], dram[name + "1"]]
    build(nc, dram)
    return run_bass_kernel_spmd(nc, [arrays], core_ids=[0]).results[0]["out_x"]
```
